# Optimizing a Trainium2 kernel written in Bass

```python
import numpy as np
import jax
import jax.numpy as jnp

def _softmax(x, axis=-1):
    return jax.nn.softmax(x, axis=axis)

def _gelu(x):
    return jax.nn.gelu(x, approximate=True)

def _silu(x):
    return jax.nn.silu(x)

def _sigmoid(x):
    return jax.nn.sigmoid(x)

def _layernorm(x, axis=-1, eps=1e-05):
    m = jnp.mean(x, axis=axis, keepdims=True)
    v = jnp.var(x, axis=axis, keepdims=True)
    return (x - m) / jnp.sqrt(v + eps)

def _scatter_add(tgt, idx, src, axis=0):
    return tgt.at[idx].add(src)

def _segment_sum(src, seg, n):
    return jax.ops.segment_sum(src, seg, n)
kernel_name = 'mk_macaron_d1_jaxref_r8_8633ab'

def setup_inputs(seed: int=0):
    np.random.seed(seed)
    _w = jnp.asarray

    def _L0_attn_setup():
        import jax, jax.numpy as jnp
        import numpy as np
        DIM = 128
        N_HEADS = 16
        HEAD_DIM = DIM // N_HEADS
        HIDDEN = 352
        WINDOW_PER_SIDE = 128
        EPS = 1e-05
        THETA = 10000.0

        def rope_cos_sin(seqlen, head_dim):
            freqs = 1.0 / THETA ** (jnp.arange(0, head_dim, 2, dtype=jnp.float32) / head_dim)
            t = jnp.arange(seqlen, dtype=jnp.float32)
            ang = jnp.outer(t, freqs)
            return (jnp.cos(ang), jnp.sin(ang))

        def apply_rope(x, cos, sin):
            xr = x[..., 0::2]
            xi = x[..., 1::2]
            c = cos[None, :, None, :]
            s = sin[None, :, None, :]
            or_ = xr * c - xi * s
            oi_ = xr * s + xi * c
            return jnp.stack([or_, oi_], axis=-1).reshape(x.shape)

        def layernorm(x, g, b):
            mu = jnp.mean(x, axis=-1, keepdims=True)
            var = jnp.mean(jnp.square(x - mu), axis=-1, keepdims=True)
            return (x - mu) * jax.lax.rsqrt(var + EPS) * g + b

        def attention(x, wq, wk, wv, wo):
            b, s, _ = x.shape
            scale = HEAD_DIM ** (-0.5)
            q = (x @ wq).reshape(b, s, N_HEADS, HEAD_DIM)
            k = (x @ wk).reshape(b, s, N_HEADS, HEAD_DIM)
            v = (x @ wv).reshape(b, s, N_HEADS, HEAD_DIM)
            cos, sin = rope_cos_sin(s, HEAD_DIM)
            q = apply_rope(q, cos, sin)
            k = apply_rope(k, cos, sin)
            i = jnp.arange(s)[:, None]
            j = jnp.arange(s)[None, :]
            mask = (j <= i) & (i - j <= WINDOW_PER_SIDE)
            scores = jnp.einsum('bqhd,bkhd->bhqk', q, k) * scale
            scores = jnp.where(mask[None, None], scores, jnp.finfo(scores.dtype).min)
            probs = jax.nn.softmax(scores, axis=-1)
            out = jnp.einsum('bhqk,bkhd->bqhd', probs, v).reshape(b, s, -1)
            return out @ wo

        def ffn(x, w1, w2, w3):
            return jax.nn.silu(x @ w1) * (x @ w3) @ w2
        key = jax.random.key(seed)
        ks = jax.random.split(key, 9)
        sd = 0.02
        x = jax.random.normal(ks[0], (4, 256, DIM), dtype=jnp.float32)
        wq = jax.random.normal(ks[1], (DIM, DIM), dtype=jnp.float32) * sd
        wk = jax.random.normal(ks[2], (DIM, DIM), dtype=jnp.float32) * sd
        wv = jax.random.normal(ks[3], (DIM, DIM), dtype=jnp.float32) * sd
        wo = jax.random.normal(ks[4], (DIM, DIM), dtype=jnp.float32) * sd
        w1 = jax.random.normal(ks[5], (DIM, HIDDEN), dtype=jnp.float32) * sd
        w2 = jax.random.normal(ks[6], (HIDDEN, DIM), dtype=jnp.float32) * sd
        w3 = jax.random.normal(ks[7], (DIM, HIDDEN), dtype=jnp.float32) * sd
        ln1_g = jnp.ones((DIM,), jnp.float32)
        ln1_b = jnp.zeros((DIM,), jnp.float32)
        ln2_g = jnp.ones((DIM,), jnp.float32)
        ln2_b = jnp.zeros((DIM,), jnp.float32)
        return dict(x=x, wq=wq, wk=wk, wv=wv, wo=wo, w1=w1, w2=w2, w3=w3, ln1_g=ln1_g, ln1_b=ln1_b, ln2_g=ln2_g, ln2_b=ln2_b)
    _L0_attn_in = _L0_attn_setup()

    def _L0_ffn_setup():
        import jax, jax.numpy as jnp
        import numpy as np
        NUM_EXPERTS = 8
        TOP_K = 2
        NUM_GRIDS = 8
        INV_DENOM = 0.5
        GRID = np.linspace(-1.2, 0.2, NUM_GRIDS).astype(np.float32)
        LN_EPS = 1e-05

        def _layernorm(x, g, b):
            mu = x.mean(-1, keepdims=True)
            var = x.var(-1, keepdims=True)
            return (x - mu) * jax.lax.rsqrt(var + LN_EPS) * g + b

        def _rswaf(x, grid):
            t = jnp.tanh((x[..., None] - grid) * INV_DENOM)
            return 1.0 - t * t
        key = jax.random.key(seed)
        ks = jax.random.split(key, 8)
        B, S, H, F = (1, 256, 128, 512)
        F2 = F // 2
        E2 = NUM_EXPERTS // 2
        G = NUM_GRIDS
        s = 0.02
        return {'hidden_states': jax.random.normal(ks[0], (B, S, H), jnp.float32), 'gate_W': jax.random.normal(ks[1], (H, NUM_EXPERTS), jnp.float32) * s, 'mlp_W1': jax.random.normal(ks[2], (E2, H, F), jnp.float32) * s, 'mlp_b1': jnp.zeros((E2, F), jnp.float32), 'mlp_W2': jax.random.normal(ks[3], (E2, F, H), jnp.float32) * s, 'mlp_b2': jnp.zeros((E2, H), jnp.float32), 'kan_ln_g0': jnp.ones((E2, H), jnp.float32), 'kan_ln_b0': jnp.zeros((E2, H), jnp.float32), 'kan_sl_W0': jax.random.normal(ks[4], (E2, H * G, F2), jnp.float32) * s, 'kan_sl_b0': jnp.zeros((E2, F2), jnp.float32), 'kan_ln_g1': jnp.ones((E2, F2), jnp.float32), 'kan_ln_b1': jnp.zeros((E2, F2), jnp.float32), 'kan_sl_W1': jax.random.normal(ks[5], (E2, F2 * G, H), jnp.float32) * s, 'kan_sl_b1': jnp.zeros((E2, H), jnp.float32)}
    _L0_ffn_in = _L0_ffn_setup()
    _d = {'L0_attn_x': _L0_attn_in['x'], 'L0_attn_wq': _L0_attn_in['wq'], 'L0_attn_wk': _L0_attn_in['wk'], 'L0_attn_wv': _L0_attn_in['wv'], 'L0_attn_wo': _L0_attn_in['wo'], 'L0_attn_w1': _L0_attn_in['w1'], 'L0_attn_w2': _L0_attn_in['w2'], 'L0_attn_w3': _L0_attn_in['w3'], 'L0_attn_ln1_g': _L0_attn_in['ln1_g'], 'L0_attn_ln1_b': _L0_attn_in['ln1_b'], 'L0_attn_ln2_g': _L0_attn_in['ln2_g'], 'L0_attn_ln2_b': _L0_attn_in['ln2_b'], 'L0_ffn_gate_W': _L0_ffn_in['gate_W'], 'L0_ffn_mlp_W1': _L0_ffn_in['mlp_W1'], 'L0_ffn_mlp_b1': _L0_ffn_in['mlp_b1'], 'L0_ffn_mlp_W2': _L0_ffn_in['mlp_W2'], 'L0_ffn_mlp_b2': _L0_ffn_in['mlp_b2'], 'L0_ffn_kan_ln_g0': _L0_ffn_in['kan_ln_g0'], 'L0_ffn_kan_ln_b0': _L0_ffn_in['kan_ln_b0'], 'L0_ffn_kan_sl_W0': _L0_ffn_in['kan_sl_W0'], 'L0_ffn_kan_sl_b0': _L0_ffn_in['kan_sl_b0'], 'L0_ffn_kan_ln_g1': _L0_ffn_in['kan_ln_g1'], 'L0_ffn_kan_ln_b1': _L0_ffn_in['kan_ln_b1'], 'L0_ffn_kan_sl_W1': _L0_ffn_in['kan_sl_W1'], 'L0_ffn_kan_sl_b1': _L0_ffn_in['kan_sl_b1']}
    _x0 = _d['L0_attn_x']
    _d['L0_attn_x'] = jax.random.normal(jax.random.fold_in(jax.random.key(seed), 1), (1, 2048, 128), dtype=_x0.dtype)
    del _x0
    return _d

def reference(L0_attn_x, L0_attn_wq, L0_attn_wk, L0_attn_wv, L0_attn_wo, L0_attn_w1, L0_attn_w2, L0_attn_w3, L0_attn_ln1_g, L0_attn_ln1_b, L0_attn_ln2_g, L0_attn_ln2_b, L0_ffn_gate_W, L0_ffn_mlp_W1, L0_ffn_mlp_b1, L0_ffn_mlp_W2, L0_ffn_mlp_b2, L0_ffn_kan_ln_g0, L0_ffn_kan_ln_b0, L0_ffn_kan_sl_W0, L0_ffn_kan_sl_b0, L0_ffn_kan_ln_g1, L0_ffn_kan_ln_b1, L0_ffn_kan_sl_W1, L0_ffn_kan_sl_b1):

    def _L0_attn_ref(x, wq, wk, wv, wo, w1, w2, w3, ln1_g, ln1_b, ln2_g, ln2_b):
        import jax, jax.numpy as jnp
        import numpy as np
        DIM = 128
        N_HEADS = 16
        HEAD_DIM = DIM // N_HEADS
        HIDDEN = 352
        WINDOW_PER_SIDE = 128
        EPS = 1e-05
        THETA = 10000.0

        def rope_cos_sin(seqlen, head_dim):
            freqs = 1.0 / THETA ** (jnp.arange(0, head_dim, 2, dtype=jnp.float32) / head_dim)
            t = jnp.arange(seqlen, dtype=jnp.float32)
            ang = jnp.outer(t, freqs)
            return (jnp.cos(ang), jnp.sin(ang))

        def apply_rope(x, cos, sin):
            xr = x[..., 0::2]
            xi = x[..., 1::2]
            c = cos[None, :, None, :]
            s = sin[None, :, None, :]
            or_ = xr * c - xi * s
            oi_ = xr * s + xi * c
            return jnp.stack([or_, oi_], axis=-1).reshape(x.shape)

        def layernorm(x, g, b):
            mu = jnp.mean(x, axis=-1, keepdims=True)
            var = jnp.mean(jnp.square(x - mu), axis=-1, keepdims=True)
            return (x - mu) * jax.lax.rsqrt(var + EPS) * g + b

        def attention(x, wq, wk, wv, wo):
            b, s, _ = x.shape
            scale = HEAD_DIM ** (-0.5)
            q = (x @ wq).reshape(b, s, N_HEADS, HEAD_DIM)
            k = (x @ wk).reshape(b, s, N_HEADS, HEAD_DIM)
            v = (x @ wv).reshape(b, s, N_HEADS, HEAD_DIM)
            cos, sin = rope_cos_sin(s, HEAD_DIM)
            q = apply_rope(q, cos, sin)
            k = apply_rope(k, cos, sin)
            i = jnp.arange(s)[:, None]
            j = jnp.arange(s)[None, :]
            mask = (j <= i) & (i - j <= WINDOW_PER_SIDE)
            scores = jnp.einsum('bqhd,bkhd->bhqk', q, k) * scale
            scores = jnp.where(mask[None, None], scores, jnp.finfo(scores.dtype).min)
            probs = jax.nn.softmax(scores, axis=-1)
            out = jnp.einsum('bhqk,bkhd->bqhd', probs, v).reshape(b, s, -1)
            return out @ wo

        def ffn(x, w1, w2, w3):
            return jax.nn.silu(x @ w1) * (x @ w3) @ w2
        h = x + attention(layernorm(x, ln1_g, ln1_b), wq, wk, wv, wo)
        out = h + ffn(layernorm(h, ln2_g, ln2_b), w1, w2, w3)
        return out

    def _L0_ffn_ref(hidden_states, gate_W, mlp_W1, mlp_b1, mlp_W2, mlp_b2, kan_ln_g0, kan_ln_b0, kan_sl_W0, kan_sl_b0, kan_ln_g1, kan_ln_b1, kan_sl_W1, kan_sl_b1):
        import jax, jax.numpy as jnp
        import numpy as np
        NUM_EXPERTS = 8
        TOP_K = 2
        NUM_GRIDS = 8
        INV_DENOM = 0.5
        GRID = np.linspace(-1.2, 0.2, NUM_GRIDS).astype(np.float32)
        LN_EPS = 1e-05

        def _layernorm(x, g, b):
            mu = x.mean(-1, keepdims=True)
            var = x.var(-1, keepdims=True)
            return (x - mu) * jax.lax.rsqrt(var + LN_EPS) * g + b

        def _rswaf(x, grid):
            t = jnp.tanh((x[..., None] - grid) * INV_DENOM)
            return 1.0 - t * t
        B, S, H = hidden_states.shape
        E2, _, F2 = (kan_sl_W0.shape[0], kan_sl_W0.shape[1], kan_sl_W0.shape[2])
        G = NUM_GRIDS
        x = hidden_states.reshape(-1, H)
        T = x.shape[0]
        logits = x @ gate_W
        probs = jax.nn.softmax(logits.astype(jnp.float32), axis=-1)
        rw, sel = jax.lax.top_k(probs, TOP_K)
        rw = rw / rw.sum(axis=-1, keepdims=True)
        w_full = jnp.sum(jax.nn.one_hot(sel, NUM_EXPERTS, dtype=rw.dtype) * rw[..., None], axis=1)
        w_full = w_full.astype(x.dtype)
        h = jnp.einsum('th,ehf->etf', x, mlp_W1) + mlp_b1[:, None, :]
        h = jax.nn.gelu(h, approximate=False)
        mlp_out = jnp.einsum('etf,efh->eth', h, mlp_W2) + mlp_b2[:, None, :]
        grid = jnp.asarray(GRID)
        h0 = _layernorm(x[None], kan_ln_g0[:, None, :], kan_ln_b0[:, None, :])
        basis0 = _rswaf(h0, grid).reshape(E2, T, H * G)
        z = jnp.einsum('eti,eio->eto', basis0, kan_sl_W0) + kan_sl_b0[:, None, :]
        h1 = _layernorm(z, kan_ln_g1[:, None, :], kan_ln_b1[:, None, :])
        basis1 = _rswaf(h1, grid).reshape(E2, T, F2 * G)
        kan_out = jnp.einsum('eti,eio->eto', basis1, kan_sl_W1) + kan_sl_b1[:, None, :]
        expert_out = jnp.concatenate([mlp_out, kan_out], axis=0)
        out = jnp.einsum('eth,te->th', expert_out, w_full)
        return out.reshape(B, S, H)
    x = L0_attn_x
    x = x + 0.5 * _L0_ffn_ref(_layernorm(x, axis=-1), L0_ffn_gate_W, L0_ffn_mlp_W1, L0_ffn_mlp_b1, L0_ffn_mlp_W2, L0_ffn_mlp_b2, L0_ffn_kan_ln_g0, L0_ffn_kan_ln_b0, L0_ffn_kan_sl_W0, L0_ffn_kan_sl_b0, L0_ffn_kan_ln_g1, L0_ffn_kan_ln_b1, L0_ffn_kan_sl_W1, L0_ffn_kan_sl_b1)
    x = x + _L0_attn_ref(_layernorm(x, axis=-1), L0_attn_wq, L0_attn_wk, L0_attn_wv, L0_attn_wo, L0_attn_w1, L0_attn_w2, L0_attn_w3, L0_attn_ln1_g, L0_attn_ln1_b, L0_attn_ln2_g, L0_attn_ln2_b)
    x = x + 0.5 * _L0_ffn_ref(_layernorm(x, axis=-1), L0_ffn_gate_W, L0_ffn_mlp_W1, L0_ffn_mlp_b1, L0_ffn_mlp_W2, L0_ffn_mlp_b2, L0_ffn_kan_ln_g0, L0_ffn_kan_ln_b0, L0_ffn_kan_sl_W0, L0_ffn_kan_sl_b0, L0_ffn_kan_ln_g1, L0_ffn_kan_ln_b1, L0_ffn_kan_sl_W1, L0_ffn_kan_sl_b1)
    return x

_drawn_inputs = setup_inputs


def setup_inputs(seed=0):
    import zlib

    import numpy as np

    out = dict(_drawn_inputs(seed))
    spreads = {'L0_attn_ln1_g': (1.0, 0.6),
     'L0_attn_ln1_b': (0.0, 0.8),
     'L0_attn_ln2_g': (1.0, 0.6),
     'L0_attn_ln2_b': (0.0, 0.8),
     'L0_ffn_mlp_b1': (0.0, 0.683),
     'L0_ffn_mlp_b2': (0.0, 0.1),
     'L0_ffn_kan_ln_g0': (1.0, 0.6),
     'L0_ffn_kan_ln_b0': (0.0, 0.8),
     'L0_ffn_kan_sl_b0': (0.0, 0.366),
     'L0_ffn_kan_ln_g1': (1.0, 0.6),
     'L0_ffn_kan_ln_b1': (0.0, 0.619),
     'L0_ffn_kan_sl_b1': (0.0, 0.1)}
    factors = {'L0_attn_wq': 8.0,
     'L0_attn_wk': 8.0,
     'L0_attn_wv': 7.335,
     'L0_attn_wo': 7.517,
     'L0_attn_w1': 6.639,
     'L0_attn_w2': 6.654,
     'L0_attn_w3': 6.015}
    for name, (base, spread) in spreads.items():
        noise = np.random.default_rng([zlib.crc32(name.encode()), seed]).standard_normal(out[name].shape)
        drawn = base * np.exp(spread * noise) if base else spread * noise
        out[name] = jnp.asarray(drawn.astype(out[name].dtype))
    for name, factor in factors.items():
        out[name] = (out[name] * factor).astype(out[name].dtype)
    return out
```

```python
from contextlib import ExitStack

import numpy as np

import concourse.bass as bass
from concourse import mybir

ALU = mybir.AluOpType
ACT = mybir.ActivationFunctionType
AX = mybir.AxisListType
F32 = mybir.dt.float32
BF16 = mybir.dt.bfloat16
F16 = mybir.dt.float16
I32 = mybir.dt.int32
U32 = mybir.dt.uint32

P = 128
T = 2048
NT = T // P
C = 128
NE = 8
E2 = NE // 2
TOPK = 2
F = 512
FC = F // P
F2 = F // 2
F2C = F2 // P
G = 8
GRID = np.linspace(-1.2, 0.2, G).astype(np.float32)
EPS = 1e-5
MAXB = TOPK * T // P + NE - 1
XB = MAXB + 3
YB = MAXB + 5
BOUND = "both loops together have at most MAXB blocks"
NS = MAXB + 5


class Names:
    pass


def bc(ap, axis, n):
    a = ap.unsqueeze(axis)
    shape = list(a.shape)
    shape[axis] = n
    return a.to_broadcast(shape)


def constants(nc, k):
    sb, sem = k.sb, k.sem
    k.ident = sb("ident", [P, P])
    k.ones = sb("ones", [P, P])
    k.later = sb("later", [P, P])
    k.earlier = sb("earlier", [P, NE, NE])
    k.minus_half = sb("minus_half", [P, NT])
    k.slot_no = sb("slot_no", [P, NS])
    k.scan_ones = sb("scan_ones", [P, NT])
    k.const_made = sem("const_made")
    k.const_set = sem("const_set")
    k.N_CONST = 8




def make_constants(pool, k):
    pool.memset(k.ident[:], 0.0).then_inc(k.const_set, 1)
    pool.memset(k.ones[:], 1.0).then_inc(k.const_made, 1)
    pool.memset(k.later[:], 1.0).then_inc(k.const_set, 1)
    pool.memset(k.earlier[:], 1.0).then_inc(k.const_set, 1)
    pool.memset(k.minus_half[:], -0.5).then_inc(k.const_made, 1)
    pool.memset(k.scan_ones[:], 1.0).then_inc(k.const_made, 1)
    pool.memset(k.zeros[:], 0.0).then_inc(k.const_made, 1)
    pool.iota(k.slot_no[:], pattern=[[1, NS]], base=-1, channel_multiplier=0,
              allow_small_or_imprecise_dtypes=True).then_inc(k.const_made, 1)
    pool.wait_ge(k.const_set, 3)
    pool.affine_select(out=k.ident[:], in_=k.ident[:], compare_op=ALU.not_equal, fill=1.0, base=0,
                       pattern=[[-1, P]], channel_multiplier=1).then_inc(k.const_made, 1)
    pool.affine_select(out=k.later[:], in_=k.later[:], compare_op=ALU.is_gt, fill=0.0, base=0,
                       pattern=[[1, P]], channel_multiplier=-1).then_inc(k.const_made, 1)
    pool.affine_select(out=k.earlier[:], in_=k.earlier[:], compare_op=ALU.is_gt, fill=0.0, base=0,
                       pattern=[[1, NE], [-1, NE]], channel_multiplier=0).then_inc(k.const_made, 1)


def moe_tensors(nc, k):
    sb = k.sb
    k.gate_w = sb("gate_w", [P, NE])
    k.kan_b0 = sb("kan_b0", [P, E2, F2])
    k.kan_b1 = sb("kan_b1", [P, E2, C])
    k.kan_ln = sb("kan_ln", [P, 2 * (1 + F2C), E2])
    k.kan_g0, k.kan_c0 = k.kan_ln[:, 0], k.kan_ln[:, 1]
    k.kan_g1, k.kan_c1 = k.kan_ln[:, 2:2 + F2C], k.kan_ln[:, 2 + F2C:]
    k.weight = sb("weight", [P, TOPK, NT])
    k.idx_y = sb("idx_y", [P, TOPK, NT], I32)
    k.n_blocks = sb("n_blocks", [P, 2], I32)
    k.expert_of = sb("expert_of", [P, 2, NS], I32)
    k.zeroed = k.sem("zeroed")
    k.x_loaded = k.sem("x_loaded")
    k.small_loaded = k.sem("small_loaded")
    k.mlp_loaded = [k.sem(f"mlp_loaded_{n}") for n in range(2)]
    k.kan_loaded = [k.sem(f"kan_loaded_{n}") for n in range(2)]
    k.stored_out = k.sem("stored_out")


def moe_weights(nc, k, ctx, n):
    sb = lambda name, shape: ctx.enter_context(nc.sbuf_tensor(f"{name}_{n}", shape, F32))
    k.kan_w0 = sb("kan_w0", [P, E2, G, F2])
    k.kan_w1 = sb("kan_w1", [P, E2, F2C, G, C])
    k.mlp_w1 = sb("mlp_w1", [P, E2, F])
    k.mlp_w2 = sb("mlp_w2", [P, E2, FC, C])
    k.mlp_b1 = sb("mlp_b1", [P, E2, F])
    k.mlp_b2 = sb("mlp_b2", [P, E2, C])
    if n == 0:
        k.zeros = sb("zeros", [P, YB * C // 4])


def load_shared(q, k, a):
    q.dma_start(k.gate_w[:], a.gate_W).then_inc(k.small_loaded, 16)
    q.dma_start(k.kan_ln[:], a.kan_ln).then_inc(k.small_loaded, 16)
    q.dma_start(k.kan_b0[:], a.kan_sl_b0.partition_broadcast(P)).then_inc(k.small_loaded, 16)
    q.dma_start(k.kan_b1[:], a.kan_sl_b1.partition_broadcast(P)).then_inc(k.small_loaded, 16)


N_SHARED = 4


def load_experts(q, k, a, n):
    q.dma_start(k.mlp_w1[:], a.mlp_W1.rearrange("e p f -> p e f")).then_inc(k.mlp_loaded[n], 16)
    for e in range(E2):
        q.dma_start(k.mlp_w2[:, e], a.mlp_W2[e].rearrange("(c p) h -> p c h", p=P)).then_inc(k.mlp_loaded[n], 16)
    q.dma_start(k.mlp_b1[:], a.mlp_b1.partition_broadcast(P)).then_inc(k.mlp_loaded[n], 16)
    q.dma_start(k.mlp_b2[:], a.mlp_b2.partition_broadcast(P)).then_inc(k.mlp_loaded[n], 16)
    for e in range(E2):
        q.dma_start(k.kan_w0[:, e], a.kan_sl_W0[e].rearrange("(p g) o -> p g o", g=G)
                    ).then_inc(k.kan_loaded[n], 16)
        q.dma_start(k.kan_w1[:, e], a.kan_sl_W1[e].rearrange("(c p g) o -> p c g o", p=P, g=G)
                    ).then_inc(k.kan_loaded[n], 16)


N_MLP = E2 + 3


def route(nc, k, a, n):
    with ExitStack() as ctx:
        sb = lambda name, shape, dt=F32: ctx.enter_context(nc.sbuf_tensor(f"{name}_{n}", shape, dt))
        ps = lambda name, shape: ctx.enter_context(nc.psum_tensor(f"{name}_{n}", shape, F32))
        sem = lambda name: k.phase_sem(f"{name}_{n}")
        xn = sb("xn", [P, NT, C])
        xnT = sb("xnT", [P, NT * P])
        rows = sb("rows", [P, NT, TOPK, C])
        st = sb("st", [P, NT, 6])
        mv = sb("mv", [P, NT, 2])
        st2 = sb("st2", [P, NT, 6])
        mv2 = sb("mv2", [P, NT, 2])
        var_eps = sb("var_eps", [P, NT])
        var_eps2 = sb("var_eps2", [P, NT])
        rstd = sb("rstd", [P, NT])
        rstd2 = sb("rstd2", [P, NT])
        shift2 = sb("shift2", [P, NT])
        logit = sb("logit", [P, NT, NE])
        top = sb("top", [P, NT])
        below = sb("below", [P, NT, NE])
        prob = sb("prob", [P, NT, NE])
        above = sb("above", [P, NT, NE, NE])
        equal = sb("equal", [P, NT, NE, NE])
        place = sb("place", [P, NT, NE])
        chosen = sb("chosen", [P, NT, NE])
        pick = sb("pick", [P, TOPK, NT, NE])
        weighed = sb("weighed", [P, NT, NE])
        den = sb("den", [P, NT])
        tile_sum = sb("tile_sum", [P, NT, NE])
        up_to = sb("up_to", [P, NT, NE])
        blocks_i = sb("blocks_i", [P, NE], I32)
        blocks = sb("blocks", [P, NE])
        blocks_up_to = sb("blocks_up_to", [P, NE])
        base = sb("base", [P, NE])
        pos = sb("pos", [P, NT, NE])
        tmp = sb("tmp", [P, TOPK, NT, NE])
        at = sb("at", [P, TOPK, NT])
        is_kan = sb("is_kan", [P, TOPK, NT])
        not_kan = sb("not_kan", [P, TOPK, NT])
        row_scale = sb("row_scale", [P, TOPK, NT])
        row_shift = sb("row_shift", [P, TOPK, NT])
        idx_x = sb("idx_x", [P, TOPK, NT], I32)
        tab = sb("tab", [P, 2, NS])
        xT_ps = [ps(f"xT_ps{i}", [P, 4 * P]) for i in range(2)]
        logit_ps = ps("logit_ps", [P, NT, NE])
        cum_ps = ps("cum_ps", [P, NT, NE])
        sum_ps = ps("sum_ps", [P, NT, NE])

        var_ready, rstd_ready, xn_ready = sem("var_ready"), sem("rstd_ready"), sem("xn_ready")
        xT_ready, xT_copied = sem("xT_ready"), sem("xT_copied")
        logits_ready, below_ready, prob_ready = sem("logits_ready"), sem("below_ready"), sem("prob_ready")
        chosen_ready, counts_ready = sem("chosen_ready"), sem("counts_ready")
        idx_ready, rows_ready, scattered = sem("idx_ready"), sem("rows_ready"), sem("scattered")
        summed, sum_added = sem("summed"), sem("sum_added")
        step = sem("step")

        with nc.Block() as block:
            @block.vector
            def _(dve):
                done = [0]

                def link(ins):
                    done[0] += 1
                    ins.then_inc(step, 1)
                    dve.wait_ge(step, done[0])

                if n == 0:
                    dve.wait_ge(k.x_loaded, 16)
                for t in range(NT):
                    last = nc.vector.bn_stats(st[:, t], k.xs[:, t])
                link(last)
                for t in range(NT):
                    last = nc.vector.bn_aggr(mv[:, t], st[:, t])
                link(last)
                nc.vector.tensor_scalar(var_eps[:], mv[:, :, 1], EPS, None, ALU.add).then_inc(var_ready, 1)
                dve.wait_ge(rstd_ready, 1)
                for t in range(NT):
                    last = nc.vector.tensor_scalar(xn[:, t], k.xs[:, t], mv[:, t, 0:1], rstd[:, t:t + 1],
                                                   ALU.subtract, ALU.mult)
                    last.then_inc(xn_ready, 1)
                dve.wait_ge(xn_ready, NT)
                for t in range(NT):
                    last = nc.vector.bn_stats(st2[:, t], xn[:, t])
                link(last)
                for t in range(NT):
                    last = nc.vector.bn_aggr(mv2[:, t], st2[:, t])
                link(last)
                nc.vector.tensor_scalar(var_eps2[:], mv2[:, :, 1], EPS, None, ALU.add).then_inc(var_ready, 1)
                dve.wait_ge(logits_ready, 1)
                link(nc.vector.tensor_copy(logit[:], logit_ps[:]))
                link(nc.vector.tensor_reduce(top[:], logit[:], AX.X, ALU.max))
                nc.vector.tensor_tensor(below[:], logit[:], bc(top[:], 2, NE),
                                        ALU.subtract).then_inc(below_ready, 1)
                nc.vector.tensor_tensor(above[:], bc(logit[:], 2, NE), bc(logit[:], 3, NE), ALU.is_gt)
                link(nc.vector.tensor_tensor(equal[:], bc(logit[:], 2, NE), bc(logit[:], 3, NE),
                                             ALU.is_equal))
                dve.wait_ge(k.const_made, k.N_CONST)
                link(nc.vector.tensor_tensor(equal[:], equal[:], bc(k.earlier[:], 1, NT), ALU.mult))
                link(nc.vector.tensor_tensor(above[:], above[:], equal[:], ALU.add))
                link(nc.vector.tensor_reduce(place[:], above[:], AX.X, ALU.add))
                nc.vector.tensor_scalar(chosen[:], place[:], float(TOPK), None,
                                        ALU.is_lt).then_inc(chosen_ready, 1)
                nc.vector.tensor_scalar(pick[:, 0], place[:], 0.0, None, ALU.is_equal)
                nc.vector.tensor_scalar(pick[:, 1], place[:], 1.0, None, ALU.is_equal)
                dve.wait_ge(prob_ready, 1)
                dve.wait_ge(chosen_ready, 1)
                link(nc.vector.tensor_tensor(weighed[:], prob[:], chosen[:], ALU.mult))
                link(nc.vector.tensor_reduce(den[:], weighed[:], AX.X, ALU.add))
                link(nc.vector.reciprocal(den[:], den[:]))
                link(nc.vector.tensor_scalar(den[:], den[:], 0.5, None, ALU.mult))
                link(nc.vector.tensor_tensor(tmp[:], pick[:], bc(prob[:], 1, TOPK), ALU.mult))
                link(nc.vector.tensor_reduce(k.weight[:], tmp[:], AX.X, ALU.add))
                link(nc.vector.tensor_tensor(k.weight[:], k.weight[:], bc(den[:], 1, TOPK), ALU.mult))
                dve.wait_ge(counts_ready, 1)
                link(nc.vector.tensor_copy(tile_sum[:], sum_ps[:]))
                for e in range(NE):
                    last = nc.vector.tensor_tensor_scan(up_to[:, :, e], k.scan_ones[:], tile_sum[:, :, e],
                                                        0.0, ALU.mult, ALU.add)
                link(last)
                link(nc.vector.tensor_scalar(blocks_i[:], up_to[:, NT - 1], float(P - 1), None, ALU.add))
                link(nc.vector.tensor_scalar(blocks_i[:], blocks_i[:], P.bit_length() - 1, None,
                                             ALU.logical_shift_right))
                link(nc.vector.tensor_copy(blocks[:], blocks_i[:]))
                for h in range(2):
                    last = nc.vector.tensor_tensor_scan(blocks_up_to[:, h * E2:(h + 1) * E2],
                                                        k.scan_ones[:, 0:E2], blocks[:, h * E2:(h + 1) * E2],
                                                        0.0, ALU.mult, ALU.add)
                link(last)
                nc.vector.tensor_copy(k.n_blocks[:, 0:1], blocks_up_to[:, E2 - 1:E2])
                nc.vector.tensor_copy(k.n_blocks[:, 1:2], blocks_up_to[:, NE - 1:NE])
                for h in range(2):
                    link(nc.vector.tensor_scalar(tab[:, h], k.slot_no[:], blocks_up_to[:, h * E2:h * E2 + 1],
                                                 None, ALU.is_ge))
                    for e in range(1, E2 - 1):
                        link(nc.vector.scalar_tensor_tensor(
                            tab[:, h], k.slot_no[:], blocks_up_to[:, h * E2 + e:h * E2 + e + 1],
                            tab[:, h], ALU.is_ge, ALU.add))
                nc.vector.tensor_copy(k.expert_of[:], tab[:])
                link(nc.vector.tensor_tensor(base[:], blocks_up_to[:], blocks[:], ALU.subtract))
                link(nc.vector.tensor_scalar(base[:, E2:NE], base[:, E2:NE], blocks_up_to[:, E2 - 1:E2],
                                             None, ALU.add))
                link(nc.vector.tensor_scalar(base[:], base[:], float(P), None, ALU.mult))
                link(nc.vector.tensor_tensor(up_to[:], up_to[:], tile_sum[:], ALU.subtract))
                link(nc.vector.tensor_tensor(pos[:], cum_ps[:], up_to[:], ALU.add))
                link(nc.vector.tensor_tensor(pos[:], pos[:], bc(base[:], 1, NT), ALU.add))
                link(nc.vector.tensor_tensor(tmp[:], pick[:], bc(pos[:], 1, TOPK), ALU.mult))
                nc.vector.tensor_reduce(at[:], tmp[:], AX.X, ALU.add)
                link(nc.vector.tensor_reduce(is_kan[:], pick[:, :, :, E2:NE], AX.X, ALU.add))
                nc.vector.tensor_copy(idx_x[:], at[:]).then_inc(idx_ready, 1)
                link(nc.vector.tensor_scalar(at[:], at[:], float(P), None, ALU.add))
                nc.vector.scalar_tensor_tensor(k.idx_y[:], is_kan[:], float(P), at[:], ALU.mult, ALU.add)
                link(nc.vector.tensor_scalar(not_kan[:], is_kan[:], -1.0, 1.0, ALU.mult, ALU.add))
                dve.wait_ge(rstd_ready, 2)
                link(nc.vector.scalar_tensor_tensor(shift2[:], mv2[:, :, 0], -1.0, rstd2[:],
                                                    ALU.mult, ALU.mult))
                nc.vector.tensor_tensor(row_shift[:], is_kan[:], bc(shift2[:], 1, TOPK), ALU.mult)
                link(nc.vector.tensor_tensor(row_scale[:], is_kan[:], bc(rstd2[:], 1, TOPK), ALU.mult))
                link(nc.vector.tensor_tensor(row_scale[:], row_scale[:], not_kan[:], ALU.add))
                for t in range(NT):
                    for j in range(TOPK):
                        nc.vector.tensor_scalar(rows[:, t, j], xn[:, t], row_scale[:, j, t:t + 1],
                                                row_shift[:, j, t:t + 1], ALU.mult,
                                                ALU.add).then_inc(rows_ready, 1)
                if n == 0:
                    for e in range(E2):
                        dve.wait_ge(summed, e + 1)
                        sums = xT_ps[e % 2]
                        nc.vector.tensor_tensor(k.kan_b0[:, e], k.kan_b0[:, e], sums[:, 0:F2],
                                                ALU.add).then_inc(sum_added, 1)
                        nc.vector.tensor_tensor(k.kan_b1[:, e], k.kan_b1[:, e], sums[:, F2:F2 + C],
                                                ALU.add).then_inc(sum_added, 1)

            @block.sync
            def _(sp):
                if n == 0:
                    sp.dma_start(k.xs[:], a.x[0].rearrange("(t p) c -> p t c", p=P)).then_inc(k.x_loaded, 16)
                    load_shared(sp, k, a)
                load_experts(sp, k, a, n)

            @block.gpsimd
            def _(pool):
                if n == 0:
                    make_constants(pool, k)
                    pool.wait_ge(k.const_made, k.N_CONST)
                pool.wait_ge(var_ready, 1)
                nc.gpsimd.tensor_tensor(rstd[:], var_eps[:], k.minus_half[:], ALU.pow).then_inc(rstd_ready, 1)
                pool.wait_ge(var_ready, 2)
                nc.gpsimd.tensor_tensor(rstd2[:], var_eps2[:], k.minus_half[:], ALU.pow).then_inc(rstd_ready, 1)
                if n == 0:
                    pool.wait_ge(k.zeroed, 32)
                pool.wait_ge(idx_ready, 1)
                for t in range(NT):
                    for j in range(TOPK):
                        pool.wait_ge(rows_ready, TOPK * t + j + 1)
                        pool.indirect_dma_start(
                            k.x_sorted, bass.IndirectOffsetOnAxis(ap=idx_x[:, j, t:t + 1].bitcast(U32), axis=0),
                            rows[:, t, j], None).then_inc(scattered, 16)
                pool.wait_ge(scattered, 16 * NT * TOPK)

            @block.tensor
            def _(pe):
                pe.wait_ge(k.const_made, k.N_CONST)
                for g in range(NT // 4):
                    if g >= 2:
                        pe.wait_ge(xT_copied, g - 1)
                    for t in range(4 * g, 4 * g + 4):
                        pe.wait_ge(xn_ready, t + 1)
                        last = nc.tensor.transpose(xT_ps[g % 2][:, (t % 4) * P:(t % 4 + 1) * P], xn[:, t],
                                                   k.ident[:])
                    last.then_inc(xT_ready, 1)
                if n == 0:
                    pe.wait_ge(k.small_loaded, 16 * N_SHARED)
                for t in range(NT):
                    pe.wait_ge(xT_copied, t // 4 + 1)
                    last = nc.tensor.matmul(logit_ps[:, t], xnT[:, t * P:(t + 1) * P], k.gate_w[:],
                                            start=True, stop=True)
                last.then_inc(logits_ready, 1)
                pe.wait_ge(chosen_ready, 1)
                nc.tensor.matmul(sum_ps[:], k.ones[:], chosen[:], start=True, stop=True)
                nc.tensor.matmul(cum_ps[:], k.later[:], chosen[:], start=True,
                                 stop=True).then_inc(counts_ready, 1)
                if n == 0:
                    pe.wait_ge(k.kan_loaded[0], 16 * 2 * E2)
                    for e in range(E2):
                        if e >= 2:
                            pe.wait_ge(sum_added, 2 * (e - 1))
                        sums = xT_ps[e % 2]
                        for g in range(G):
                            nc.tensor.matmul(sums[:, 0:F2], k.ones[:], k.kan_w0[:, e, g], start=(g == 0),
                                             stop=(g == G - 1))
                        for c in range(F2C):
                            for g in range(G):
                                last = nc.tensor.matmul(sums[:, F2:F2 + C], k.ones[:], k.kan_w1[:, e, c, g],
                                                        start=(c == 0 and g == 0), stop=(c == F2C - 1 and g == G - 1))
                        last.then_inc(summed, 1)

            @block.scalar
            def _(act):
                if n == 0:
                    act.wait_ge(k.const_made, k.N_CONST)
                    for buf, nb in ((k.x_sorted, XB), (k.y_sorted, YB)):
                        w = nb * C // 4
                        act.dma_start(buf.rearrange("(p b) c -> p (b c)", p=P).rearrange("p (r w) -> p r w", r=4),
                                      bc(k.zeros[:, 0:w], 1, 4)).then_inc(k.zeroed, 16)
                for g in range(NT // 4):
                    act.wait_ge(xT_ready, g + 1)
                    nc.scalar.copy(xnT[:, g * 4 * P:(g + 1) * 4 * P], xT_ps[g % 2][:]).then_inc(xT_copied, 1)
                act.wait_ge(below_ready, 1)
                nc.scalar.activation(prob[:], below[:], ACT.Exp).then_inc(prob_ready, 1)


def mlp_blocks(nc, k, a, n):
    with ExitStack() as ctx:
        sb = lambda name, shape, dt=F32: ctx.enter_context(nc.sbuf_tensor(f"{name}_{n}", shape, dt))
        ps = lambda name, shape: ctx.enter_context(nc.psum_tensor(f"{name}_{n}", shape, F32))
        sem = lambda name: k.phase_sem(f"{name}_{n}")
        x_in = sb("m_x_in", [P, C])
        xT = sb("m_xT", [P, P])
        z = sb("m_z", [P, F])
        hT = sb("m_hT", [P, FC, P])
        y = sb("m_y", [P, C])
        xT_ps = ps("m_xT_ps", [P, P])
        z_ps = ps("m_z_ps", [P, F])
        zT_ps = ps("m_zT_ps", [P, FC, P])
        y_ps = ps("m_y_ps", [P, C])
        loaded, turned, xT_ready = sem("m_loaded"), sem("m_turned"), sem("m_xT_ready")
        z_done, z_ready, zT_done = sem("m_z_done"), sem("m_z_ready"), sem("m_zT_done")
        hT_ready, y_done, y_ready, stored = sem("m_hT_ready"), sem("m_y_done"), sem("m_y_ready"), sem("m_stored")
        cleared, all_moved = sem("m_cleared"), sem("m_all_moved")
        storing, y_free = sem("m_storing"), sem("m_y_free")

        def rounds(eng):
            return eng.value_load(k.n_blocks[0:1, 0:1], min_val=0, max_val=MAXB) + 1

        def expert(eng, entry):
            return eng.value_load(k.expert_of[0:1, 0, bass.ds(entry, 1)], min_val=0, max_val=E2 - 1)

        xs_blocks = k.x_sorted.rearrange("(b p) c -> b p c", p=P)
        ys_blocks = k.y_sorted.rearrange("(b p) c -> b p c", p=P)

        with nc.Block() as block:
            @block.sync
            def _(sp):
                end = rounds(sp)
                sp.dma_start(x_in[:], xs_blocks[0]).then_inc(loaded, 16)
                with sp.Fori(0, end) as i:
                    sp.wait_ge(turned, i + 1)
                    sp.dma_start(x_in[:], xs_blocks[bass.ds(i + 1, 1)]).then_inc(loaded, 16)
                sp.wait_ge(loaded, end * 16 + 16)
                sp.sem_inc(all_moved, 1)

            @block.tensor
            def _(pe):
                end = rounds(pe)

                def turn(blocks_loaded):
                    pe.wait_ge(loaded, blocks_loaded * 16)
                    nc.tensor.transpose(xT_ps[:], x_in[:], k.ident[:]).then_inc(turned, 1)

                turn(1)
                pe.wait_ge(k.mlp_loaded[n], 16 * N_MLP)
                pe.sem_inc(y_ready, 1)
                with pe.Fori(0, end) as i:
                    e = expert(pe, i + 1)
                    e_last = expert(pe, i)
                    pe.wait_ge(xT_ready, i + 1)
                    nc.tensor.matmul(z_ps[:], xT[:], k.mlp_w1[:, bass.ds(e, 1)], start=True,
                                     stop=True).then_inc(z_done, 1)
                    turn(i + 2)
                    pe.wait_ge(hT_ready, i + 1)
                    pe.wait_ge(y_ready, i + 1)
                    for c in range(FC):
                        last = nc.tensor.matmul(y_ps[:], hT[:, c], k.mlp_w2[:, bass.ds(e_last, 1), c],
                                                start=(c == 0), stop=(c == FC - 1))
                    last.then_inc(y_done, 1)
                    pe.wait_ge(z_ready, i + 1)
                    for c in range(FC):
                        last = nc.tensor.transpose(zT_ps[:, c], z[:, c * P:(c + 1) * P], k.ident[:])
                    last.then_inc(zT_done, 1)

            @block.vector
            def _(dve):
                end = rounds(dve)
                nc.vector.memset(hT[:], 0.0).then_inc(cleared, 1)
                dve.wait_ge(turned, 1)
                nc.vector.tensor_copy(xT[:], xT_ps[:]).then_inc(xT_ready, 1)
                with dve.Fori(0, end) as i:
                    e = expert(dve, i + 1)
                    e_last = expert(dve, i)
                    dve.wait_ge(z_done, i + 1)
                    nc.vector.tensor_tensor(z[:], z_ps[:], k.mlp_b1[:, bass.ds(e, 1)],
                                            ALU.add).then_inc(z_ready, 1)
                    dve.wait_ge(turned, i + 2)
                    nc.vector.tensor_copy(xT[:], xT_ps[:]).then_inc(xT_ready, 1)
                    dve.wait_ge(y_done, i + 1)
                    dve.wait_ge(y_free, i + 1)
                    nc.vector.tensor_tensor(y[:], y_ps[:], k.mlp_b2[:, bass.ds(e_last, 1)],
                                            ALU.add).then_inc(y_ready, 1)

            @block.gpsimd
            def _(pool):
                end = rounds(pool)
                pool.sem_inc(y_free, 1)
                with pool.Fori(0, end) as i:
                    pool.wait_ge(y_ready, i + 2)
                    pool.sem_inc(storing, 1)
                    pool.dma_start(ys_blocks[bass.ds(i, 1)], y[:]).then_inc(stored, 16)
                    pool.wait_ge(stored, i * 16 + 16)
                    pool.sem_inc(y_free, 1)

            @block.scalar
            def _(act):
                end = rounds(act)
                act.wait_ge(cleared, 1)
                act.preload_act_table(ACT.Gelu)
                act.sem_inc(hT_ready, 1)
                with act.Fori(0, end) as i:
                    act.wait_ge(zT_done, i + 1)
                    nc.scalar.activation(hT[:], zT_ps[:], ACT.Gelu).then_inc(hT_ready, 1)


def kan_blocks(nc, k, a, n):
    with ExitStack() as ctx:
        sb = lambda name, shape, dt=F32: ctx.enter_context(nc.sbuf_tensor(f"{name}_{n}", shape, dt))
        ps = lambda name, shape: ctx.enter_context(nc.psum_tensor(f"{name}_{n}", shape, F32))
        sem = lambda name: k.phase_sem(f"{name}_{n}")
        x_in = sb("k_x_in", [P, C])
        h0T = sb("k_h0T", [P, P])
        tanh0 = sb("k_tanh0", [P, G, P])
        basis0 = sb("k_basis0", [P, G, P])
        z = sb("k_z", [P, F2])
        st = sb("k_st", [P, 6])
        mv = sb("k_mv", [P, 2])
        var_eps = sb("k_var_eps", [P, 1])
        rstd = sb("k_rstd", [P, 1])
        zn = sb("k_zn", [P, F2])
        h1T = sb("k_h1T", [P, F2C, P])
        tanh1 = sb("k_tanh1", [P, G, F2C, P])
        basis1 = sb("k_basis1", [P, G, F2C, P])
        y = sb("k_y", [P, C])
        xT_ps = ps("k_xT_ps", [P, P])
        z_ps = ps("k_z_ps", [P, F2])
        znT_ps = ps("k_znT_ps", [P, F2C, P])
        y_ps = ps("k_y_ps", [P, C])
        loaded, turned, h0_ready = sem("k_loaded"), sem("k_turned"), sem("k_h0_ready")
        tanh0_done, basis0_ready = sem("k_tanh0_done"), sem("k_basis0_ready")
        tanh1_done, basis1_ready = sem("k_tanh1_done"), sem("k_basis1_ready")
        z_done, z_ready, stats_done, var_ready = sem("k_z_done"), sem("k_z_ready"), sem("k_stats_done"), sem("k_var_ready")
        mean_ready, rstd_ready, zn_ready = sem("k_mean_ready"), sem("k_rstd_ready"), sem("k_zn_ready")
        znT_done, h1_ready = sem("k_znT_done"), sem("k_h1_ready")
        y_done, y_ready, stored = sem("k_y_done"), sem("k_y_ready"), sem("k_stored")
        all_moved, storing, y_free = sem("k_all_moved"), sem("k_storing"), sem("k_y_free")
        H0, H1 = 2, 4
        G0, G1 = G // H0, G // H1

        def rounds(eng):
            return eng.value_load(k.n_blocks[0:1, 1:2], min_val=0, max_val=MAXB) + 1

        def first(eng):
            return eng.value_load(k.n_blocks[0:1, 0:1], min_val=0, max_val=MAXB)

        def expert(eng, entry):
            return eng.value_load(k.expert_of[0:1, 1, bass.ds(entry, 1)], min_val=0, max_val=E2 - 1)

        xs_blocks = k.x_sorted.rearrange("(b p) c -> b p c", p=P)
        ys_blocks = k.y_sorted.rearrange("(b p) c -> b p c", p=P)

        with nc.Block() as block:
            @block.sync
            def _(sp):
                end = rounds(sp)
                start = first(sp)
                sp.dma_start(x_in[:], xs_blocks[bass.ds(start, 1)]).then_inc(loaded, 16)
                with sp.Fori(0, end) as i:
                    sp.wait_ge(turned, i + 1)
                    src = nc.s_assert_within(start + i + 1, 0, XB - 1, skip_runtime_bounds_check_because=BOUND)
                    sp.dma_start(x_in[:], xs_blocks[bass.ds(src, 1)]).then_inc(loaded, 16)
                sp.wait_ge(loaded, end * 16 + 16)
                sp.sem_inc(all_moved, 1)

            @block.tensor
            def _(pe):
                end = rounds(pe)

                def turn(blocks_loaded):
                    pe.wait_ge(loaded, blocks_loaded * 16)
                    nc.tensor.transpose(xT_ps[:], x_in[:], k.ident[:]).then_inc(turned, 1)

                turn(1)
                pe.wait_ge(k.kan_loaded[n], 16 * 2 * E2)
                pe.sem_inc(y_ready, 1)
                with pe.Fori(0, end) as i:
                    e = expert(pe, i + 1)
                    e_last = expert(pe, i)
                    pe.wait_ge(h0_ready, i + 1)
                    turn(i + 2)
                    for g in range(G):
                        if g % G0 == 0:
                            pe.wait_ge(basis0_ready, H0 * i + g // G0 + 1)
                        last = nc.tensor.matmul(z_ps[:], basis0[:, g], k.kan_w0[:, bass.ds(e, 1), g],
                                                start=(g == 0), stop=(g == G - 1))
                    last.then_inc(z_done, 1)
                    pe.wait_ge(y_ready, i + 1)
                    for g in range(G):
                        if g % G1 == 0:
                            pe.wait_ge(basis1_ready, H1 * i + g // G1 + 1)
                        for c in range(F2C):
                            last = nc.tensor.matmul(y_ps[:], basis1[:, g, c], k.kan_w1[:, bass.ds(e_last, 1), c, g],
                                                    start=(g == 0 and c == 0), stop=(g == G - 1 and c == F2C - 1))
                    last.then_inc(y_done, 1)
                    pe.wait_ge(zn_ready, i + 1)
                    for c in range(F2C):
                        last = nc.tensor.transpose(znT_ps[:, c], zn[:, c * P:(c + 1) * P], k.ident[:])
                    last.then_inc(znT_done, 1)

            @block.vector
            def _(dve):
                end = rounds(dve)

                def affine0(e, blocks_turned):
                    dve.wait_ge(turned, blocks_turned)
                    nc.vector.tensor_scalar(h0T[:], xT_ps[:], k.kan_g0[:, bass.ds(e, 1)],
                                            k.kan_c0[:, bass.ds(e, 1)], ALU.mult, ALU.add).then_inc(h0_ready, 1)

                def square0(before):
                    for h in range(H0):
                        dve.wait_ge(tanh0_done, before + h + 1)
                        part = slice(h * G0, (h + 1) * G0)
                        nc.vector.tensor_tensor(basis0[:, part], tanh0[:, part], tanh0[:, part],
                                                ALU.mult).then_inc(basis0_ready, 1)

                nc.vector.memset(h1T[:], 0.0).then_inc(h1_ready, 1)
                affine0(expert(dve, 1), 1)
                square0(0)
                with dve.Fori(0, end) as i:
                    e_next = expert(dve, i + 2)
                    e = expert(dve, i + 1)
                    e_last = expert(dve, i)
                    dve.wait_ge(tanh0_done, H0 * i + H0)
                    affine0(e_next, i + 2)
                    for h in range(H1):
                        dve.wait_ge(tanh1_done, H1 * i + h + 1)
                        part = slice(h * G1, (h + 1) * G1)
                        nc.vector.tensor_tensor(basis1[:, part], tanh1[:, part], tanh1[:, part],
                                                ALU.mult).then_inc(basis1_ready, 1)
                    dve.wait_ge(z_done, i + 1)
                    nc.vector.tensor_tensor(z[:], k.kan_b0[:, bass.ds(e, 1)], z_ps[:],
                                            ALU.subtract).then_inc(z_ready, 1)
                    dve.wait_ge(z_ready, i + 1)
                    nc.vector.bn_stats(st[:], z[:]).then_inc(stats_done, 1)
                    dve.wait_ge(h0_ready, 1)
                    dve.wait_ge(stats_done, i + 1)
                    nc.vector.bn_aggr(mv[:], st[:]).then_inc(mean_ready, 1)
                    dve.wait_ge(mean_ready, i + 1)
                    nc.vector.tensor_scalar(var_eps[:], mv[:, 1:2], EPS, None, ALU.add).then_inc(var_ready, 1)
                    square0(H0 * i + H0)
                    dve.wait_ge(rstd_ready, i + 1)
                    nc.vector.tensor_scalar(zn[:], z[:], mv[:, 0:1], rstd[:], ALU.subtract,
                                            ALU.mult).then_inc(zn_ready, 1)
                    dve.wait_ge(znT_done, i + 1)
                    dve.wait_ge(tanh1_done, H1 * i + H1)
                    for c in range(F2C):
                        last = nc.vector.tensor_scalar(h1T[:, c], znT_ps[:, c], k.kan_g1[:, c, bass.ds(e, 1)],
                                                       k.kan_c1[:, c, bass.ds(e, 1)], ALU.mult, ALU.add)
                    last.then_inc(h1_ready, 1)
                    dve.wait_ge(y_done, i + 1)
                    dve.wait_ge(y_free, i + 1)
                    nc.vector.tensor_tensor(y[:], k.kan_b1[:, bass.ds(e_last, 1)], y_ps[:],
                                            ALU.subtract).then_inc(y_ready, 1)

            @block.scalar
            def _(act):
                end = rounds(act)

                def tanh0_parts():
                    for g in range(G):
                        ins = nc.scalar.activation(tanh0[:, g], h0T[:], ACT.Tanh, bias=float(-0.5 * GRID[g]),
                                                   scale=0.5)
                        if g % G0 == G0 - 1:
                            ins.then_inc(tanh0_done, 1)

                act.wait_ge(h0_ready, 1)
                tanh0_parts()
                with act.Fori(0, end) as i:
                    act.wait_ge(h1_ready, i + 1)
                    for g in range(G):
                        ins = nc.scalar.activation(tanh1[:, g], h1T[:], ACT.Tanh, bias=float(-0.5 * GRID[g]),
                                                   scale=0.5)
                        if g % G1 == G1 - 1:
                            ins.then_inc(tanh1_done, 1)
                    act.wait_ge(h0_ready, i + 2)
                    act.wait_ge(basis0_ready, H0 * i + H0)
                    tanh0_parts()

            @block.gpsimd
            def _(pool):
                end = rounds(pool)
                start = first(pool)
                pool.sem_inc(y_free, 1)
                with pool.Fori(0, end) as i:
                    pool.wait_ge(var_ready, i + 1)
                    nc.gpsimd.tensor_tensor(rstd[:], var_eps[:], k.minus_half[:, 0:1],
                                            ALU.pow).then_inc(rstd_ready, 1)
                    pool.wait_ge(y_ready, i + 2)
                    dst = nc.s_assert_within(start + i + 1, 0, YB - 1, skip_runtime_bounds_check_because=BOUND)
                    pool.sem_inc(storing, 1)
                    pool.dma_start(ys_blocks[bass.ds(dst, 1)], y[:]).then_inc(stored, 16)
                    pool.wait_ge(stored, i * 16 + 16)
                    pool.sem_inc(y_free, 1)


def combine(nc, k, a, n, out):
    PART = 4
    with ExitStack() as ctx:
        got = ctx.enter_context(nc.sbuf_tensor(f"got_{n}", [P, NT, TOPK, C], F32))
        gathered = [k.phase_sem(f"gathered{g}_{n}") for g in range(NT // PART)]
        first_added, x_ready = (k.phase_sem(f"{x}_{n}") for x in ("first_added", "x_ready"))
        with nc.Block() as block:
            @block.gpsimd
            def _(pool):
                for t in range(NT):
                    for j in range(TOPK):
                        pool.indirect_dma_start(
                            got[:, t, j], None, k.y_sorted,
                            bass.IndirectOffsetOnAxis(ap=k.idx_y[:, j, t:t + 1].bitcast(U32), axis=0)
                        ).then_inc(gathered[t // PART], 16)

            @block.vector
            def _(dve):
                for g in range(NT // PART):
                    dve.wait_ge(gathered[g], 16 * PART * TOPK)
                    for j in range(TOPK):
                        for t in range(g * PART, (g + 1) * PART):
                            last = nc.vector.scalar_tensor_tensor(k.xs[:, t], got[:, t, j], k.weight[:, j, t:t + 1],
                                                                  k.xs[:, t], ALU.mult, ALU.add)
                        if j == 0:
                            last.then_inc(first_added, 1)
                            dve.wait_ge(first_added, g + 1)
                    last.then_inc(x_ready, 1)

            @block.sync
            def _(sp):
                if out is not None:
                    tiles = out[0].rearrange("(t p) c -> p t c", p=P)
                    for g in range(NT // PART):
                        sp.wait_ge(x_ready, g + 1)
                        part = slice(g * PART, (g + 1) * PART)
                        sp.dma_start(tiles[:, part], k.xs[:, part]).then_inc(k.stored_out, 16)
                    sp.wait_ge(k.stored_out, 16 * (NT // PART))


def moe(nc, k, a, n, out=None):
    with ExitStack() as ctx:
        moe_weights(nc, k, ctx, n)
        route(nc, k, a, n)
        mlp_blocks(nc, k, a, n)
        kan_blocks(nc, k, a, n)
        combine(nc, k, a, n, out)

NH = 16
HD = C // NH
PAIRS = NH // 2
WINDOW = 128
assert WINDOW == P
PARTS = 3
RUNS = [(0, 3), (3, 2), (5, 1)]
N_PROD = 6
M_ROW = N_PROD * HD
NEG = -1e30
VW = PARTS * HD + 2
HID = 352
HIDC = [(0, 128), (128, 128), (256, 96)]
QK_G = 4


def layernorm_stats(dve, link, x, st, mv, var_eps, ready):
    for t in range(NT):
        last = dve.bn_stats(st[:, t], x[:, t])
    link(last)
    for t in range(NT):
        last = dve.bn_aggr(mv[:, t], st[:, t])
    link(last)
    dve.tensor_scalar(var_eps[:], mv[:, :, 1], EPS, None, ALU.add).then_inc(ready, 1)


def project(nc, k, a, s):
    with ExitStack() as ctx:
        sb = lambda name, shape, dt=F32: ctx.enter_context(nc.sbuf_tensor(f"a_{name}", shape, dt))
        ps = lambda name, shape: ctx.enter_context(nc.psum_tensor(f"a_{name}", shape, F32))
        sem = lambda name: k.phase_sem(f"a_{name}")
        W4 = 4 * P
        NCH = NT // 4
        n1 = sb("n1", [P, NT, C])
        n1T = sb("n1T", [P, T])
        w = sb("w", [P, 5, C])
        cos = sb("cos", [P, T])
        sin = sb("sin", [P, T])
        st = sb("st", [P, NT, 6])
        mv = sb("mv", [P, NT, 2])
        mv2 = sb("mv2", [P, NT, 2])
        var_eps = sb("var_eps", [P, NT])
        rstd = sb("rstd", [P, 2, NT])
        part = sb("part", [P, 2, PARTS, W4], BF16)
        by_cos = sb("by_cos", [P, W4])
        by_sin = sb("by_sin", [P, W4])
        turned_ = sb("turned", [P, W4])
        rest = sb("rest", [P, W4])
        vrest = sb("vrest", [P, W4])
        vrest2 = sb("vrest2", [P, W4])
        nT_ps = ps("nT_ps", [P, W4])
        q_ps = [[ps(f"q_ps{x}{y}", [P, W4]) for y in range(2)] for x in range(2)]
        v_ps = ps("v_ps", [P, 4, C])
        loaded, w_swapped, var_ready, rstd_ready = sem("loaded"), sem("w_swapped"), sem("var_ready"), sem("rstd_ready")
        n1_ready, nT_done, nT_ready = sem("n1_ready"), sem("nT_done"), sem("nT_ready")
        qk_done, qk_used, v_done, v_used = sem("qk_done"), sem("qk_used"), sem("v_done"), sem("v_used")
        rot_ready, hi_ready, rest_ready, mid_ready = sem("rot_ready"), sem("hi_ready"), sem("rest_ready"), sem("mid_ready")
        parts_ready, parts_out, k_cleared, q_cleared = sem("parts_ready"), sem("parts_out"), sem("k_cleared"), sem("q_cleared")
        stacked = sem("stacked")
        v_hi, v_rest, v_mid, v_rest2, v_split = sem("v_hi"), sem("v_rest"), sem("v_mid"), sem("v_rest2"), sem("v_split")
        step = sem("step")
        parts_dram = nc.dram_tensor("qk_parts", [2, PARTS, C, T], BF16, kind="Internal").ap()
        NU = 2 * NCH

        with nc.Block() as block:
            @block.sync
            def _(sp):
                sp.dma_start(w[:, 0], a.wq).then_inc(loaded, 16)
                sp.dma_start(w[:, 1], a.wk).then_inc(loaded, 16)
                sp.dma_start(w[:, 2], a.wv).then_inc(loaded, 16)
                sp.dma_start(k.ln_vec[:], a.attn_ln).then_inc(loaded, 16)
                for tab, src in ((cos, a.cos), (sin, a.sin)):
                    for h in range(NH):
                        sp.dma_start(tab[h * HD:(h + 1) * HD], src).then_inc(loaded, 16)
                sp.dma_start(s.wo[:], a.wo).then_inc(s.tail_loaded, 16)
                sp.dma_start(s.w1[:], a.w1).then_inc(s.tail_loaded, 16)
                sp.dma_start(s.w3[:], a.w3).then_inc(s.tail_loaded, 16)
                for c, (at, size) in enumerate(HIDC):
                    sp.dma_start(s.w2[0:size, c], a.w2[at:at + size]).then_inc(s.tail_loaded, 16)
                sp.wait_ge(k_cleared, 4)
                sp.wait_ge(q_cleared, 1)
                for u in range(NU):
                    x, g = u % 2, u // 2
                    sp.wait_ge(parts_ready, u + 1)
                    cols = slice(g * W4, (g + 1) * W4)
                    sp.dma_start(parts_dram[x, :, :, cols].rearrange("r c t -> c r t"), part[:, x]).then_inc(parts_out, 16)
                    sp.wait_ge(parts_out, 16 * u + 16)
                    for odd in range(2):
                        for r, (c0, cn) in enumerate(RUNS):
                            for c in range(cn):
                                row = 64 * odd + (c0 + c) * HD
                                src = parts_dram[x, c if x == 0 else r, :, cols].rearrange(
                                    "(p two d) t -> two d p t", two=2, d=HD)[odd]
                                if x == 0:
                                    dst = s.q_stack[row:row + HD, :, cols]
                                else:
                                    dst = s.k_stack[row:row + HD, odd::2, cols]
                                sp.dma_start(dst, src).then_inc(stacked, 16)
                sp.wait_ge(stacked, 16 * NU * 2 * N_PROD)

            @block.gpsimd
            def _(pool):
                pool.memset(s.mask[:], 0.0).then_inc(s.mask_set, 1)
                pool.wait_ge(s.mask_set, 1)
                pool.affine_select(out=s.mask[:], in_=s.mask[:], compare_op=ALU.is_ge, fill=NEG, base=0,
                                   pattern=[[0, 2], [1, 2 * P]], channel_multiplier=-1).then_inc(s.mask_set, 1)
                pool.wait_ge(s.mask_set, 2)
                pool.affine_select(out=s.mask[:], in_=s.mask[:], compare_op=ALU.is_ge, fill=NEG, base=WINDOW,
                                   pattern=[[0, 2], [-1, 2 * P]], channel_multiplier=1).then_inc(s.mask_set, 1)
                pool.wait_ge(var_ready, 1)
                nc.gpsimd.tensor_tensor(rstd[:, 0], var_eps[:], k.minus_half[:], ALU.pow).then_inc(rstd_ready, 1)
                pool.wait_ge(var_ready, 2)
                nc.gpsimd.tensor_tensor(rstd[:, 1], var_eps[:], k.minus_half[:], ALU.pow).then_inc(rstd_ready, 1)
                ones2 = float(np.array([0x3F803F80], np.uint32).view(np.float32)[0])
                words = s.k_stack[:].bitcast(F32).rearrange("r (p two) t -> r two p t", two=2)
                pool.memset(s.q_stack[:].bitcast(F32), 0.0).then_inc(q_cleared, 1)
                pool.wait_ge(q_cleared, 1)
                for m, (r0, r1, odd, value) in enumerate(((32, 64, 0, ones2), (64, 128, 0, 0.0),
                                                          (96, 128, 1, ones2), (0, 64, 1, 0.0))):
                    pool.memset(words[r0:r1, odd], value).then_inc(k_cleared, 1)
                    pool.wait_ge(k_cleared, m + 1)

            @block.vector
            def _(dve):
                done = [0]

                def link(ins):
                    done[0] += 1
                    ins.then_inc(step, 1)
                    dve.wait_ge(step, done[0])

                nc.vector.tensor_copy(s.ident16[:], k.ident[:]).then_inc(s.ident16_ready, 1)
                nc.vector.memset(s.v_parts[:], 1.0)
                layernorm_stats(nc.vector, link, k.xs, st, mv, var_eps, var_ready)
                dve.wait_ge(rstd_ready, 1)
                for t in range(NT):
                    last = nc.vector.tensor_scalar(s.res[:, t], k.xs[:, t], mv[:, t, 0:1], rstd[:, 0, t:t + 1],
                                                   ALU.subtract, ALU.mult)
                link(last)
                layernorm_stats(nc.vector, link, s.res, st, mv2, var_eps, var_ready)
                dve.wait_ge(rstd_ready, 2)
                for t in range(NT):
                    nc.vector.tensor_scalar(n1[:, t], s.res[:, t], mv2[:, t, 0:1], rstd[:, 1, t:t + 1],
                                            ALU.subtract, ALU.mult).then_inc(n1_ready, 1)
                dve.wait_ge(loaded, 16 * (4 + 2 * NH))
                link(nc.vector.tensor_scalar(w[:, 0], w[:, 0], float(HD) ** -0.5, None, ALU.mult))
                pairs = w[:].rearrange("p m (c two) -> p m c two", two=2)
                nc.vector.tensor_copy(pairs[:, 3:5, :, 0], pairs[:, 0:2, :, 1])
                nc.vector.tensor_copy(pairs[:, 3:5, :, 1], pairs[:, 0:2, :, 0]).then_inc(w_swapped, 1)

                def values(g):
                    dst = s.v_parts[:, g * 4 + 1:(g + 1) * 4 + 1]
                    by_head = lambda x: x.rearrange("p (t h d) -> p t h d", t=4, h=NH)
                    dve.wait_ge(v_done, g + 1)
                    v = v_ps[:].rearrange("p t (h d) -> p t h d", h=NH)
                    link(nc.vector.tensor_copy(dst[:, :, :, 0:HD], v))
                    nc.vector.tensor_tensor(by_head(vrest[:]), v, dst[:, :, :, 0:HD], ALU.subtract).then_inc(v_used, 1)
                    dve.wait_ge(v_used, g + 1)
                    link(nc.vector.tensor_copy(dst[:, :, :, HD:2 * HD], by_head(vrest[:])))
                    link(nc.vector.tensor_tensor(dst[:, :, :, 2 * HD:3 * HD], by_head(vrest[:]),
                                                 dst[:, :, :, HD:2 * HD], ALU.subtract))

                for u in range(NU):
                    x, g = u % 2, u // 2
                    cols = slice(g * W4, (g + 1) * W4)
                    dve.wait_ge(qk_done, u + 1)
                    if u >= 1:
                        dve.wait_ge(hi_ready, u)
                    nc.vector.tensor_tensor(by_cos[:], q_ps[x][0][:], cos[:, cols], ALU.mult)
                    nc.vector.tensor_tensor(by_sin[:], q_ps[x][1][:], sin[:, cols], ALU.mult).then_inc(qk_used, 1)
                    dve.wait_ge(qk_used, u + 1)
                    nc.vector.tensor_tensor(turned_[:], by_cos[:], by_sin[:], ALU.add).then_inc(rot_ready, 1)
                    if x == 0:
                        values(g)
                    dve.wait_ge(hi_ready, u + 1)
                    nc.vector.tensor_tensor(rest[:], turned_[:], part[:, x, 0], ALU.subtract).then_inc(rest_ready, 1)
                    dve.wait_ge(mid_ready, u + 1)
                    nc.vector.tensor_tensor(part[:, x, 2], rest[:], part[:, x, 1],
                                            ALU.subtract).then_inc(parts_ready, 1)

            @block.scalar
            def _(act):
                def chunk_T(g):
                    act.wait_ge(nT_done, g + 1)
                    nc.scalar.activation(n1T[:, g * W4:(g + 1) * W4], nT_ps[:], ACT.Identity,
                                         bias=k.ln_vec[:, 1:2], scale=k.ln_vec[:, 0:1]).then_inc(nT_ready, 1)

                act.wait_ge(loaded, 16 * (4 + 2 * NH))
                chunk_T(0)
                for u in range(NU):
                    x, g = u % 2, u // 2
                    if x == 0 and g + 1 < NCH:
                        chunk_T(g + 1)
                    act.wait_ge(rot_ready, u + 1)
                    if u >= 2:
                        act.wait_ge(parts_out, 16 * (u - 1))
                    nc.scalar.copy(part[:, x, 0], turned_[:]).then_inc(hi_ready, 1)
                    act.wait_ge(rest_ready, u + 1)
                    nc.scalar.copy(part[:, x, 1], rest[:]).then_inc(mid_ready, 1)

            @block.tensor
            def _(pe):
                def chunk_T(g):
                    if g:
                        pe.wait_ge(nT_ready, g)
                    for t in range(4):
                        pe.wait_ge(n1_ready, 4 * g + t + 1)
                        last = nc.tensor.transpose(nT_ps[:, t * P:(t + 1) * P], n1[:, 4 * g + t], k.ident[:])
                    last.then_inc(nT_done, 1)

                chunk_T(0)
                pe.wait_ge(w_swapped, 1)
                for u in range(NU):
                    x, g = u % 2, u // 2
                    if x == 0:
                        if g + 1 < NCH:
                            chunk_T(g + 1)
                        pe.wait_ge(nT_ready, g + 1)
                        if g:
                            pe.wait_ge(v_used, g)
                        for t in range(4):
                            last = nc.tensor.matmul(v_ps[:, t], n1T[:, (4 * g + t) * P:(4 * g + t + 1) * P], w[:, 2],
                                                    start=True, stop=True)
                        last.then_inc(v_done, 1)
                    if u >= 2:
                        pe.wait_ge(qk_used, u - 1)
                    nc.tensor.matmul(q_ps[x][0][:], w[:, x], n1T[:, g * W4:(g + 1) * W4], start=True, stop=True)
                    nc.tensor.matmul(q_ps[x][1][:], w[:, 3 + x], n1T[:, g * W4:(g + 1) * W4], start=True,
                                     stop=True).then_inc(qk_done, 1)


def maxima(nc, k, a, s):
    with ExitStack() as ctx:
        sb = lambda name, shape, dt=F32: ctx.enter_context(nc.sbuf_tensor(f"x_{name}", shape, dt))
        sem = lambda name: k.phase_sem(f"x_{name}")
        minus_max = sb("minus_max", [P, NT, NH])
        mT = sb("mT", [NH, T])
        mrest = sb("mrest", [NH, T])
        mpart = sb("mpart", [NH, PARTS, T], BF16)
        NG = NH // QK_G
        scored, reduced = sem("scored"), sem("reduced")
        mT_done, mT_ready = sem("mT_done"), sem("mT_ready")
        hi, rest1, mid, low, out_done, in_done = (sem("hi"), sem("rest1"), sem("mid"), sem("low"), sem("out_done"),
                                                 sem("in_done"))
        m_dram = nc.dram_tensor("m_parts", [PARTS, NH, T], BF16, kind="Internal").ap()

        with ExitStack() as psctx:
            sc_ps = [psctx.enter_context(nc.psum_tensor(f"x_sc_ps{g}", [P, QK_G, 2 * P], F32)) for g in range(NG)]
            with nc.Block() as block:
                @block.tensor
                def _(pe):
                    pe.wait_ge(s.mask_set, 3)
                    pe.wait_ge(s.ident16_ready, 1)

                    def scores(i, first):
                        keys = P if first else 2 * P
                        for g in range(NG):
                            if not first:
                                pe.wait_ge(reduced, i * NG + g - NG + 1)
                            for b in range(QK_G // 2):
                                h = g * QK_G + 2 * b
                                bank = sc_ps[g][:, 2 * b:2 * b + 2, 2 * P - keys:]
                                nc.tensor.matmul(bank, s.ident16[:], s.mask[:, :, 2 * P - keys:],
                                                 start=True, stop=False)
                                for j in range(2):
                                    q = s.q_stack[:, h // 2, bass.ds(i * P, P)]
                                    kk = s.k_stack[:, h + j, bass.ds(i * P - (keys - P), keys)]
                                    last = nc.tensor.matmul(bank[:, j], q, kk, start=False, stop=(j == 1))
                            last.then_inc(scored, 1)

                    scores(0, True)
                    with pe.Fori(1, NT) as i:
                        scores(i, False)

                @block.vector
                def _(dve):
                    def reduce(i, first):
                        for g in range(NG):
                            dve.wait_ge(scored, i * NG + g + 1)
                            src = sc_ps[g][:, :, P:] if first else sc_ps[g][:]
                            dst = minus_max[:, bass.ds(i, 1), g * QK_G:(g + 1) * QK_G]
                            nc.vector.tensor_reduce(dst, src, AX.X, ALU.max, negate=True).then_inc(reduced, 1)

                    reduce(0, True)
                    with dve.Fori(1, NT) as i:
                        reduce(i, False)
        mT_ps = [ctx.enter_context(nc.psum_tensor(f"x_mT_ps{g}", [NH, 4 * P], F32)) for g in range(NT // 4)]
        with nc.Block() as block:
            @block.tensor
            def _(pe):
                for t in range(NT):
                    last = nc.tensor.transpose(mT_ps[t // 4][:, (t % 4) * P:(t % 4 + 1) * P], minus_max[:, t],
                                               k.ident[:])
                    if t % 4 == 3:
                        last.then_inc(mT_done, 1)

            @block.vector
            def _(dve):
                for g in range(NT // 4):
                    dve.wait_ge(mT_done, g + 1)
                    last = nc.vector.tensor_copy(mT[:, g * 4 * P:(g + 1) * 4 * P], mT_ps[g][:])
                last.then_inc(mT_ready, 1)
                dve.wait_ge(mT_ready, 1)
                nc.vector.tensor_copy(mpart[:, 0], mT[:]).then_inc(hi, 1)
                dve.wait_ge(hi, 1)
                nc.vector.tensor_tensor(mrest[:], mT[:], mpart[:, 0], ALU.subtract).then_inc(rest1, 1)
                dve.wait_ge(rest1, 1)
                nc.vector.tensor_copy(mpart[:, 1], mrest[:]).then_inc(mid, 1)
                dve.wait_ge(mid, 1)
                nc.vector.tensor_tensor(mpart[:, 2], mrest[:], mpart[:, 1], ALU.subtract).then_inc(low, 1)

            @block.sync
            def _(sp):
                sp.wait_ge(low, 1)
                sp.dma_start(m_dram.rearrange("r h t -> h r t"), mpart[:]).then_inc(out_done, 16)
                sp.wait_ge(out_done, 16)
                for odd in range(2):
                    row = 64 * odd + M_ROW
                    sp.dma_start(s.q_stack[row:row + PARTS, :, 0:T],
                                 m_dram.rearrange("r (p two) t -> two r p t", two=2)[odd]).then_inc(in_done, 16)
                sp.wait_ge(in_done, 32)


def attend(nc, k, a, s):
    with ExitStack() as ctx:
        sb = lambda name, shape, dt=F32: ctx.enter_context(nc.sbuf_tensor(f"p_{name}", shape, dt))
        ps = lambda name, shape: ctx.enter_context(nc.psum_tensor(f"p_{name}", shape, F32))
        sem = lambda name: k.phase_sem(f"p_{name}")
        NG = NH // QK_G
        assert NG == 4
        prob_bufs = [sb(f"prob{g}", [P, QK_G, 2 * P]) for g in range(3)]
        prob = [prob_bufs[0], prob_bufs[1], prob_bufs[2], prob_bufs[1]]
        hi = [sb(f"hi{u}", [P, NH, 2 * P], F16) for u in range(2)]
        low = [sb(f"low{u}", [P, NH, 2 * P], F16) for u in range(2)]
        total = sb("total", [P, NH, HD])
        inv = sb("inv", [P, NH])
        sc_ps = [ps(f"sc_ps{g}", [P, QK_G, 2 * P]) for g in range(2)]
        o_ps = [ps(f"o_ps{u}", [P, NH, VW]) for u in range(2)]
        scored, exp_done, out_done = sem("scored"), sem("exp_done"), sem("out_done")
        hi_act, hi_dve = sem("hi_act"), sem("hi_dve")
        low_pool, low_dve = sem("low_pool"), sem("low_dve")
        total_ready, inv_ready, att_ready = sem("total_ready"), sem("inv_ready"), sem("att_ready")
        cleared = sem("cleared")

        def head_slice(g):
            return slice(g * QK_G, (g + 1) * QK_G)

        def all_rounds(eng, one_round):
            for j in range(2):
                one_round(j, j, first=(j == 0), second=(j == 1))
            with eng.Fori(1, NT // 2) as jj:
                for u in range(2):
                    one_round(2 * jj + u, u, first=False, second=False)

        with nc.Block() as block:
            @block.tensor
            def _(pe):
                def values(j, u, g):
                    if g == 0:
                        pe.wait_ge(low_pool, j + 1)
                    else:
                        pe.wait_ge(low_dve, j * 3 + g)
                    for h in range(g * QK_G, (g + 1) * QK_G):
                        terms = [(x[w_][:, h, c * P:(c + 1) * P], tile)
                                 for w_, c, tile in ((1 - u, 1, j), (u, 0, j + 1)) for x in (hi, low)]
                        for m, (p_, tile) in enumerate(terms):
                            last = nc.tensor.matmul(o_ps[u][:, h], p_, s.v_parts[:, bass.ds(tile, 1), h],
                                                    start=(m == 0), stop=(m == 3))
                    last.then_inc(out_done, 1)

                def one_round(j, u, first, second):
                    for g in range(NG):
                        if g >= 2 or not first:
                            pe.wait_ge(exp_done, j * NG + g - 1)
                        for b in range(QK_G // 2):
                            h = g * QK_G + 2 * b
                            bank = sc_ps[g % 2][:, 2 * b:2 * b + 2]
                            nc.tensor.matmul(bank, s.ident16[:], s.mask[:], start=True, stop=False)
                            for x in range(2):
                                last = nc.tensor.matmul(
                                    bank[:, x], s.k_stack[:, h + x, bass.ds(j * P, P)],
                                    s.q_stack[:, h // 2, bass.ds(j * P, 2 * P)], start=False, stop=(x == 1))
                        last.then_inc(scored, 1)
                        if not first:
                            if g == 0 and not second:
                                pe.wait_ge(att_ready, j - 1)
                            values(j - 1, 1 - u, g)

                pe.wait_ge(cleared, 2)
                pe.sem_inc(att_ready, 1)
                all_rounds(pe, one_round)
                pe.wait_ge(att_ready, NT - 1)
                for g in range(NG):
                    values(NT - 1, 1, g)

            @block.scalar
            def _(act):
                def exp(j, g, first):
                    act.wait_ge(scored, j * NG + g + 1)
                    if g == 0 and not first:
                        act.wait_ge(low_pool, j)
                    if g == 1 and not first:
                        act.wait_ge(low_dve, j * 3)
                    if g == 3:
                        act.wait_ge(low_dve, j * 3 + 1)
                    nc.scalar.activation(prob[g][:], sc_ps[g % 2][:], ACT.Exp).then_inc(exp_done, 1)

                def round_off(j, u, g, first):
                    act.wait_ge(exp_done, j * NG + g + 1)
                    if not first:
                        act.wait_ge(out_done, j * NG + g - 3)
                    nc.scalar.copy(hi[u][:, head_slice(g)], prob[g][:]).then_inc(hi_act, 1)

                def one_round(j, u, first, second):
                    exp(j, 0, first)
                    exp(j, 1, first)
                    round_off(j, u, 0, first)
                    exp(j, 2, first)
                    round_off(j, u, 2, first)
                    exp(j, 3, first)

                act.preload_act_table(ACT.Exp)
                all_rounds(act, one_round)

            @block.gpsimd
            def _(pool):
                def one_round(j, u, first, second):
                    pool.wait_ge(hi_act, j * 2 + 1)
                    nc.gpsimd.tensor_tensor(low[u][:, head_slice(0)], prob[0][:], hi[u][:, head_slice(0)],
                                            ALU.subtract).then_inc(low_pool, 1)

                all_rounds(pool, one_round)

            @block.vector
            def _(dve):
                def round_off(j, u, g, first):
                    dve.wait_ge(exp_done, j * NG + g + 1)
                    if not first:
                        dve.wait_ge(out_done, j * NG + g - 3)
                    nc.vector.tensor_copy(hi[u][:, head_slice(g)], prob[g][:]).then_inc(hi_dve, 1)

                def remainder(j, u, g):
                    if g == 2:
                        dve.wait_ge(hi_act, j * 2 + 2)
                    else:
                        dve.wait_ge(hi_dve, j * 2 + (g + 1) // 2)
                    nc.vector.tensor_tensor(low[u][:, head_slice(g)], prob[g][:], hi[u][:, head_slice(g)],
                                            ALU.subtract).then_inc(low_dve, 1)

                def normalize(j, u):
                    dve.wait_ge(out_done, j * NG + NG)
                    sums = o_ps[u][:, :, 0:PARTS * HD].rearrange("p h (r d) -> p h d r", r=PARTS)
                    nc.vector.tensor_reduce(total[:], sums, AX.X, ALU.add).then_inc(total_ready, 1)
                    nc.vector.reciprocal(inv[:], o_ps[u][:, :, PARTS * HD]).then_inc(inv_ready, 1)
                    dve.wait_ge(total_ready, j + 1)
                    dve.wait_ge(inv_ready, j + 1)
                    nc.vector.tensor_tensor(
                        s.att[:, bass.ds(j, 1)].rearrange("p t (h d) -> p (t h) d", h=NH), total[:],
                        bc(inv[:], 2, HD), ALU.mult).then_inc(att_ready, 1)

                def one_round(j, u, first, second):
                    round_off(j, u, 1, first)
                    remainder(j, u, 1)
                    if not first and not second:
                        normalize(j - 2, u)
                    remainder(j, u, 2)
                    round_off(j, u, 3, first)
                    remainder(j, u, 3)

                nc.vector.memset(hi[1][:].bitcast(F32), 0.0).then_inc(cleared, 1)
                nc.vector.memset(low[1][:].bitcast(F32), 0.0).then_inc(cleared, 1)
                all_rounds(dve, one_round)
                normalize(NT - 2, 0)
                dve.wait_ge(att_ready, NT)
                normalize(NT - 1, 1)


def finish_attention(nc, k, a, s):
    with ExitStack() as ctx:
        sb = lambda name, shape, dt=F32: ctx.enter_context(nc.sbuf_tensor(f"f_{name}", shape, dt))
        ps = lambda name, shape: ctx.enter_context(nc.psum_tensor(f"f_{name}", shape, F32))
        sem = lambda name: k.phase_sem(f"f_{name}")
        W4 = 4 * P
        NCH = NT // 4
        attT = sb("attT", [P, W4])
        st = sb("st", [P, NT, 6])
        mv = sb("mv", [P, NT, 2])
        var_eps = sb("var_eps", [P, NT])
        rstd = sb("rstd", [P, NT])
        n2 = sb("n2", [P, 4, C])
        n2T = sb("n2T", [P, W4])
        gate = sb("gate", [P, 3, W4])
        hid = sb("hid", [P, 3, W4])
        T_ps = ps("T_ps", [P, W4])
        w_ps = ps("w_ps", [P, 4, C])
        u1_ps = [ps(f"u1_ps{x}", [P, W4]) for x in range(2)]
        u3_ps = [ps(f"u3_ps{x}", [P, W4]) for x in range(2)]
        aT_done, aT_ready, wo_done, h_ready = sem("aT_done"), sem("aT_ready"), sem("wo_done"), sem("h_ready")
        var_ready, rstd_ready, n2_ready = sem("var_ready"), sem("rstd_ready"), sem("n2_ready")
        nT_done, nT_ready, u_done, silu_done, hid_ready = (sem("nT_done"), sem("nT_ready"), sem("u_done"),
                                                         sem("silu_done"), sem("hid_ready"))
        y_done, x_ready = sem("y_done"), sem("x_ready")
        step = sem("step")

        with nc.Block() as block:
            @block.tensor
            def _(pe):
                pe.wait_ge(s.tail_loaded, 16 * 6)
                for g in range(NCH):
                    if g:
                        pe.wait_ge(aT_ready, g)
                    for t in range(4):
                        last = nc.tensor.transpose(T_ps[:, t * P:(t + 1) * P], s.att[:, 4 * g + t], k.ident[:])
                    last.then_inc(aT_done, 1)
                    pe.wait_ge(aT_ready, g + 1)
                    if g:
                        pe.wait_ge(h_ready, g)
                    for t in range(4):
                        last = nc.tensor.matmul(w_ps[:, t], attT[:, t * P:(t + 1) * P], s.wo[:], start=True, stop=True)
                    last.then_inc(wo_done, 1)
                pe.wait_ge(h_ready, NCH)
                for g in range(NCH):
                    pe.wait_ge(n2_ready, g + 1)
                    for t in range(4):
                        last = nc.tensor.transpose(T_ps[:, t * P:(t + 1) * P], n2[:, t], k.ident[:])
                    last.then_inc(nT_done, 1)
                    pe.wait_ge(nT_ready, g + 1)
                    for c, (at, size) in enumerate(HIDC):
                        v = 3 * g + c
                        if v >= 2:
                            pe.wait_ge(hid_ready, v - 1)
                        nc.tensor.matmul(u1_ps[v % 2][0:size], s.w1[:, at:at + size], n2T[:], start=True, stop=True)
                        nc.tensor.matmul(u3_ps[v % 2][0:size], s.w3[:, at:at + size], n2T[:], start=True,
                                         stop=True).then_inc(u_done, 1)
                    pe.wait_ge(hid_ready, 3 * g + 3)
                    if g:
                        pe.wait_ge(x_ready, g)
                    for t in range(4):
                        for c, (at, size) in enumerate(HIDC):
                            last = nc.tensor.matmul(w_ps[:, t], hid[0:size, c, t * P:(t + 1) * P], s.w2[0:size, c],
                                                    start=(c == 0), stop=(c == 2))
                    last.then_inc(y_done, 1)

            @block.scalar
            def _(act):
                for g in range(NCH):
                    act.wait_ge(aT_done, g + 1)
                    if g:
                        act.wait_ge(wo_done, g)
                    nc.scalar.copy(attT[:], T_ps[:]).then_inc(aT_ready, 1)
                for g in range(NCH):
                    act.wait_ge(nT_done, g + 1)
                    nc.scalar.activation(n2T[:], T_ps[:], ACT.Identity, bias=k.ln_vec[:, 3:4],
                                         scale=k.ln_vec[:, 2:3]).then_inc(nT_ready, 1)
                    for c, (at, size) in enumerate(HIDC):
                        act.wait_ge(u_done, 3 * g + c + 1)
                        if g:
                            act.wait_ge(hid_ready, 3 * g + c - 2)
                        nc.scalar.activation(gate[0:size, c], u1_ps[(3 * g + c) % 2][0:size],
                                             ACT.Silu).then_inc(silu_done, 1)

            @block.gpsimd
            def _(pool):
                pool.wait_ge(var_ready, 1)
                nc.gpsimd.tensor_tensor(rstd[:], var_eps[:], k.minus_half[:], ALU.pow).then_inc(rstd_ready, 1)

            @block.vector
            def _(dve):
                done = [0]

                def link(ins):
                    done[0] += 1
                    ins.then_inc(step, 1)
                    dve.wait_ge(step, done[0])

                for g in range(NCH):
                    dve.wait_ge(wo_done, g + 1)
                    part = slice(4 * g, 4 * g + 4)
                    last = nc.vector.tensor_tensor(s.res[:, part], s.res[:, part], w_ps[:], ALU.add)
                    last.then_inc(h_ready, 1)
                dve.wait_ge(h_ready, NCH)
                layernorm_stats(nc.vector, link, s.res, st, mv, var_eps, var_ready)
                link(nc.vector.tensor_tensor(k.xs[:], k.xs[:], s.res[:], ALU.add))
                dve.wait_ge(rstd_ready, 1)
                for g in range(NCH):
                    if g:
                        dve.wait_ge(nT_done, g)
                    for t in range(4):
                        last = nc.vector.tensor_scalar(n2[:, t], s.res[:, 4 * g + t], mv[:, 4 * g + t, 0:1],
                                                       rstd[:, 4 * g + t:4 * g + t + 1], ALU.subtract, ALU.mult)
                    last.then_inc(n2_ready, 1)
                    for c, (at, size) in enumerate(HIDC):
                        dve.wait_ge(silu_done, 3 * g + c + 1)
                        if g:
                            dve.wait_ge(y_done, g)
                        nc.vector.tensor_tensor(hid[0:size, c], gate[0:size, c], u3_ps[(3 * g + c) % 2][0:size],
                                                ALU.mult).then_inc(hid_ready, 1)
                    dve.wait_ge(y_done, g + 1)
                    part = slice(4 * g, 4 * g + 4)
                    nc.vector.tensor_tensor(k.xs[:, part], k.xs[:, part], w_ps[:], ALU.add).then_inc(x_ready, 1)


def attention(nc, k, a):
    with ExitStack() as ctx:
        sb = lambda name, shape, dt=F32: ctx.enter_context(nc.sbuf_tensor(f"s_{name}", shape, dt))
        s = Names()
        s.res = sb("res", [P, NT, C])
        s.wo = sb("wo", [P, C])
        s.w1 = sb("w1", [P, HID])
        s.w3 = sb("w3", [P, HID])
        s.w2 = sb("w2", [P, 3, C])
        k.ln_vec = sb("ln_vec", [P, 4])
        s.tail_loaded, s.mask_set = k.sem("tail_loaded"), k.sem("mask_set")
        s.ident16_ready, s.prob_free = k.sem("ident16_ready"), k.sem("prob_free")
        with ExitStack() as stacks:
            sb2 = lambda name, shape, dt=F32: stacks.enter_context(nc.sbuf_tensor(f"s_{name}", shape, dt))
            s.att = None
            s.q_stack = sb2("q_stack", [P, PAIRS, T + P], BF16)
            s.k_stack = sb2("k_stack", [P, NH, T], BF16)
            s.v_parts = sb2("v_parts", [P, NT + 1, NH, VW], BF16)
            s.mask = sb2("mask", [P, 2, 2 * P], BF16)
            s.ident16 = sb2("ident16", [P, P], BF16)
            project(nc, k, a, s)
            maxima(nc, k, a, s)
            s.att = sb2("att", [P, NT, C])
            attend(nc, k, a, s)
            finish_attention(nc, k, a, s)

def phase_semaphores(nc, k, ctx):
    k.phase_sems = []

    def phase_sem(name):
        k.phase_sems.append(ctx.enter_context(nc.semaphore(name)))
        return k.phase_sems[-1]

    k.phase_sem = phase_sem


def clear_phase_semaphores(nc, k):
    with nc.Block() as block:
        @block.gpsimd
        def _(pool):
            for s in k.phase_sems:
                pool.sem_clear(s)


def macaron(nc, a, out):
    with ExitStack() as ctx:
        k = Names()
        k.sb = lambda name, shape, dt=F32: ctx.enter_context(nc.sbuf_tensor(name, shape, dt))
        k.sem = lambda name: ctx.enter_context(nc.semaphore(name))
        k.x_sorted = nc.dram_tensor("x_sorted", [XB * P, C], F32, kind="Internal").ap()
        k.y_sorted = nc.dram_tensor("y_sorted", [YB * P, C], F32, kind="Internal").ap()
        k.xs = k.sb("xs", [P, NT, C])
        constants(nc, k)
        moe_tensors(nc, k)
        with ExitStack() as first:
            phase_semaphores(nc, k, first)
            moe(nc, k, a, 0)
            attention(nc, k, a)
            clear_phase_semaphores(nc, k)
        with ExitStack() as second:
            phase_semaphores(nc, k, second)
            moe(nc, k, a, 1, out)



_INS = ["L0_attn_x", "L0_attn_wq", "L0_attn_wk", "L0_attn_wv", "L0_attn_wo", "L0_attn_w1", "L0_attn_w2",
        "L0_attn_w3", "L0_attn_ln1_g", "L0_attn_ln1_b", "L0_attn_ln2_g", "L0_attn_ln2_b", "L0_ffn_gate_W",
        "L0_ffn_mlp_W1", "L0_ffn_mlp_b1", "L0_ffn_mlp_W2", "L0_ffn_mlp_b2", "L0_ffn_kan_ln_g0",
        "L0_ffn_kan_ln_b0", "L0_ffn_kan_sl_W0", "L0_ffn_kan_sl_b0", "L0_ffn_kan_ln_g1", "L0_ffn_kan_ln_b1",
        "L0_ffn_kan_sl_W1", "L0_ffn_kan_sl_b1"]


def kernel(**inputs):
    import concourse.bacc as bacc
    from concourse.bass_utils import run_bass_kernel_spmd

    nc = bacc.Bacc("TRN2", target_bir_lowering=False, num_devices=1)
    arrays, a = {}, Names()
    for name in _INS:
        data = np.ascontiguousarray(inputs[name])
        arrays[f"in_{name}_dram"] = data
        handle = nc.dram_tensor(f"in_{name}_dram", data.shape, mybir.dt.from_np(data.dtype), kind="ExternalInput")
        a.__dict__[name.removeprefix("L0_attn_").removeprefix("L0_ffn_")] = handle.ap()
    by_channel = [np.asarray(inputs[f"L0_ffn_kan_ln_{v}"]).reshape(E2, -1, P).transpose(2, 1, 0)
                  for v in ("g0", "b0", "g1", "b1")]
    arrays["in_kan_ln_dram"] = np.ascontiguousarray(np.concatenate(by_channel, axis=1))
    a.kan_ln = nc.dram_tensor("in_kan_ln_dram", arrays["in_kan_ln_dram"].shape, F32, kind="ExternalInput").ap()
    arrays["in_attn_ln_dram"] = np.ascontiguousarray(np.stack(
        [np.asarray(inputs[f"L0_attn_{v}"]) for v in ("ln1_g", "ln1_b", "ln2_g", "ln2_b")], axis=1))
    a.attn_ln = nc.dram_tensor("in_attn_ln_dram", (C, 4), F32, kind="ExternalInput").ap()
    freqs = 1.0 / np.float32(10000.0) ** (np.arange(0, HD, 2, dtype=np.float32) / np.float32(HD))
    angle = np.outer(np.arange(T, dtype=np.float32), freqs.astype(np.float32)).astype(np.float64).T
    cos, sin = np.cos(angle), np.sin(angle)
    for name, table in (("cos", np.stack([cos, cos], 1)), ("sin", np.stack([-sin, sin], 1))):
        arrays[f"in_{name}_dram"] = np.ascontiguousarray(table.reshape(HD, T).astype(np.float32))
        a.__dict__[name] = nc.dram_tensor(f"in_{name}_dram", (HD, T), F32, kind="ExternalInput").ap()
    out = nc.dram_tensor("out_0_dram", (1, T, C), F32, kind="ExternalOutput").ap()
    macaron(nc, a, out)
    r = run_bass_kernel_spmd(nc, [arrays], core_ids=[0])
    return r.results[0]["out_0_dram"]
```

```python
from contextlib import ExitStack

import numpy as np

import concourse.bass as bass
from concourse import mybir

ALU = mybir.AluOpType
ACT = mybir.ActivationFunctionType
AX = mybir.AxisListType
F32 = mybir.dt.float32
BF16 = mybir.dt.bfloat16
F16 = mybir.dt.float16
I32 = mybir.dt.int32
U32 = mybir.dt.uint32

P = 128
T = 2048
NT = T // P
C = 128
NE = 8
E2 = NE // 2
TOPK = 2
F = 512
FC = F // P
F2 = F // 2
F2C = F2 // P
G = 8
GRID = np.linspace(-1.2, 0.2, G).astype(np.float32)
EPS = 1e-5
MAXB = TOPK * T // P + NE - 1
NS = MAXB + 7
assert NS % 2 == 0
LEAD = 3
NQ = NS + LEAD
ROWS_OUT = TOPK * T + NS * P
BOUND = "both loops together have at most MAXB blocks"


class Names:
    pass


def bc(ap, axis, n):
    a = ap.unsqueeze(axis)
    shape = list(a.shape)
    shape[axis] = n
    return a.to_broadcast(shape)


def constants(nc, k):
    sb, sem = k.sb, k.sem
    k.ident = sb("ident", [P, P])
    k.ones = sb("ones", [P, P])
    k.later = sb("later", [P, P])
    k.earlier = sb("earlier", [P, NE, NE])
    k.minus_half = sb("minus_half", [P, NT])
    k.slot_no = sb("slot_no", [P, NS])
    k.lane_no = sb("lane_no", [P, P])
    k.one_up = sb("one_up", [P, 1])
    k.pair_no = sb("pair_no", [P, TOPK * NT])
    k.spare_row = sb("spare_row", [P, NS])
    k.scan_ones = sb("scan_ones", [P, NT])
    k.const_made = sem("const_made")
    k.const_set = sem("const_set")
    k.N_CONST = 11




def make_constants(pool, k):
    pool.memset(k.ident[:], 0.0).then_inc(k.const_set, 1)
    pool.memset(k.ones[:], 1.0).then_inc(k.const_made, 1)
    pool.memset(k.later[:], 1.0).then_inc(k.const_set, 1)
    pool.memset(k.earlier[:], 1.0).then_inc(k.const_set, 1)
    pool.memset(k.minus_half[:], -0.5).then_inc(k.const_made, 1)
    pool.memset(k.scan_ones[:], 1.0).then_inc(k.const_made, 1)
    for out, pattern, base, by_partition in (
            (k.lane_no, [[1, P]], 0, 0), (k.one_up, [[0, 1]], 1, 1), (k.pair_no, [[1, TOPK * NT]], 0, 0),
            (k.spare_row, [[P, NS]], TOPK * T + 1, 1)):
        pool.iota(out[:], pattern=pattern, base=base, channel_multiplier=by_partition,
                  allow_small_or_imprecise_dtypes=True).then_inc(k.const_made, 1)
    pool.iota(k.slot_no[:], pattern=[[1, NS]], base=-1, channel_multiplier=0,
              allow_small_or_imprecise_dtypes=True).then_inc(k.const_made, 1)
    pool.wait_ge(k.const_set, 3)
    pool.affine_select(out=k.ident[:], in_=k.ident[:], compare_op=ALU.not_equal, fill=1.0, base=0,
                       pattern=[[-1, P]], channel_multiplier=1).then_inc(k.const_made, 1)
    pool.affine_select(out=k.later[:], in_=k.later[:], compare_op=ALU.is_gt, fill=0.0, base=0,
                       pattern=[[1, P]], channel_multiplier=-1).then_inc(k.const_made, 1)
    pool.affine_select(out=k.earlier[:], in_=k.earlier[:], compare_op=ALU.is_gt, fill=0.0, base=0,
                       pattern=[[1, NE], [-1, NE]], channel_multiplier=0).then_inc(k.const_made, 1)


def moe_tensors(nc, k):
    sb = k.sb
    k.gate_w = sb("gate_w", [P, NE])
    k.kan_b0 = sb("kan_b0", [P, E2, F2])
    k.kan_b1 = sb("kan_b1", [P, E2, C])
    k.kan_ln = sb("kan_ln", [P, 2 * (1 + F2C), E2])
    k.kan_g0, k.kan_c0 = k.kan_ln[:, 0], k.kan_ln[:, 1]
    k.kan_g1, k.kan_c1 = k.kan_ln[:, 2:2 + F2C], k.kan_ln[:, 2 + F2C:]
    k.weight = sb("weight", [P, TOPK, NT])
    k.rows_of = sb("rows_of", [P, NQ, 2], I32)
    k.n_mlp = sb("n_mlp", [P, 1], I32)
    k.n_pairs = sb("n_pairs", [P, 2], I32)
    k.experts = sb("experts", [P, 2, NS // 2 - 1, 4], I32)
    k.rows_in_dram = [k.sem(f"rows_in_dram_{n}") for n in range(2)]
    k.x_loaded = k.sem("x_loaded")
    k.small_loaded = k.sem("small_loaded")
    k.mlp_loaded = [k.sem(f"mlp_loaded_{n}") for n in range(2)]
    k.kan_loaded = [[k.sem(f"kan_loaded{e}_{n}") for e in range(E2)] for n in range(2)]
    k.stored_out = k.sem("stored_out")


def moe_weights(nc, k, ctx, n):
    sb = lambda name, shape: ctx.enter_context(nc.sbuf_tensor(f"{name}_{n}", shape, F32))
    k.kan_w0 = sb("kan_w0", [P, E2, G, F2])
    k.kan_w1 = sb("kan_w1", [P, E2, F2C, G, C])
    k.mlp_w1 = sb("mlp_w1", [P, E2, F])
    k.mlp_w2 = sb("mlp_w2", [P, E2, FC, C])
    k.mlp_b1 = sb("mlp_b1", [P, E2, F])
    k.mlp_b2 = sb("mlp_b2", [P, E2, C])


def load_shared(q, k, a):
    q.dma_start(k.gate_w[:], a.gate_W).then_inc(k.small_loaded, 16)
    q.dma_start(k.kan_ln[:], a.kan_ln).then_inc(k.small_loaded, 16)
    q.dma_start(k.kan_b0[:], a.kan_sl_b0.partition_broadcast(P)).then_inc(k.small_loaded, 16)
    q.dma_start(k.kan_b1[:], a.kan_sl_b1.partition_broadcast(P)).then_inc(k.small_loaded, 16)


N_SHARED = 4


def load_mlps(q, k, a, n):
    q.dma_start(k.mlp_w1[:], a.mlp_W1.rearrange("e p f -> p e f")).then_inc(k.mlp_loaded[n], 16)
    for e in range(E2):
        q.dma_start(k.mlp_w2[:, e], a.mlp_W2[e].rearrange("(c p) h -> p c h", p=P)).then_inc(k.mlp_loaded[n], 16)
    q.dma_start(k.mlp_b1[:], a.mlp_b1.partition_broadcast(P)).then_inc(k.mlp_loaded[n], 16)
    q.dma_start(k.mlp_b2[:], a.mlp_b2.partition_broadcast(P)).then_inc(k.mlp_loaded[n], 16)


def load_kan(q, k, a, n, e):
    q.dma_start(k.kan_w0[:, e], a.kan_sl_W0[e].rearrange("(p g) o -> p g o", g=G)
                ).then_inc(k.kan_loaded[n][e], 16)
    q.dma_start(k.kan_w1[:, e], a.kan_sl_W1[e].rearrange("(c p g) o -> p c g o", p=P, g=G)
                ).then_inc(k.kan_loaded[n][e], 16)


N_MLP = E2 + 3


def route(nc, k, a, n):
    with ExitStack() as ctx:
        sb = lambda name, shape, dt=F32: ctx.enter_context(nc.sbuf_tensor(f"{name}_{n}", shape, dt))
        ps = lambda name, shape: ctx.enter_context(nc.psum_tensor(f"{name}_{n}", shape, F32))
        sem = lambda name: k.phase_sem(f"{name}_{n}")
        xn = sb("xn", [P, NT, C])
        xnT = sb("xnT", [P, NT * P])
        xh = sb("xh", [P, NT, C])
        st = sb("st", [P, NT, 6])
        mv = sb("mv", [P, NT, 2])
        var_eps = sb("var_eps", [P, NT])
        var_eps2 = sb("var_eps2", [P, NT])
        rstd = sb("rstd", [P, NT])
        rstd2 = sb("rstd2", [P, NT])
        rstd_sq = sb("rstd_sq", [P, NT])
        logit = sb("logit", [P, NT, NE])
        top = sb("top", [P, NT])
        below = sb("below", [P, NT, NE])
        prob = sb("prob", [P, NT, NE])
        above = sb("above", [P, NT, NE, NE])
        equal = sb("equal", [P, NT, NE, NE])
        place = sb("place", [P, NT, NE])
        chosen = sb("chosen", [P, NT, NE])
        pick = sb("pick", [P, TOPK, NT, NE])
        weighed = sb("weighed", [P, NT, NE])
        den = sb("den", [P, NT])
        tile_sum = sb("tile_sum", [P, NT, NE])
        up_to = sb("up_to", [P, NT, NE])
        blocks_i = sb("blocks_i", [P, NE], I32)
        blocks = sb("blocks", [P, NE])
        blocks_up_to = sb("blocks_up_to", [P, NE])
        base = sb("base", [P, NE])
        pos = sb("pos", [P, NT, NE])
        tmp = sb("tmp", [P, TOPK, NT, NE])
        at = sb("at", [P, TOPK, NT])
        is_kan = sb("is_kan", [P, TOPK, NT])
        at_i = sb("at_i", [P, TOPK, NT], I32)
        row_i = sb("row_i", [P, TOPK, NT], I32)
        slot_i = sb("slot_i", [P, TOPK, NT], I32)
        row_f = sb("row_f", [P, TOPK, NT])
        slot_f = sb("slot_f", [P, TOPK, NT])
        in_row = sb("in_row", [P, TOPK * NT, P], F16)
        in_slot = sb("in_slot", [P, TOPK * NT, NS], F16)
        numbers = sb("numbers", [P, TOPK * NT, 2, NS], F16)
        found = sb("found", [P, 2, NS])
        code = sb("code", [P, NS])
        code_i = sb("code_i", [P, NS], I32)
        token_i = sb("token_i", [P, NS], I32)
        token = sb("token", [P, NS])
        kan_rows = sb("kan_rows", [P, NS])
        spare = sb("spare", [P, NS])
        pairs_i = sb("pairs_i", [P, 2], I32)
        tab = sb("tab", [P, 2, NS])
        xT_ps = [ps(f"xT_ps{i}", [P, 4 * P]) for i in range(2)]
        logit_ps = ps("logit_ps", [P, NT, NE])
        cum_ps = ps("cum_ps", [P, NT, NE])
        sum_ps = ps("sum_ps", [P, NT, NE])
        found_ps = ps("found_ps", [P, 2, NS])

        var_ready, rstd_ready, xn_ready = sem("var_ready"), sem("rstd_ready"), sem("xn_ready")
        xT_ready, xT_copied = sem("xT_ready"), sem("xT_copied")
        logits_ready, below_ready, prob_ready = sem("logits_ready"), sem("below_ready"), sem("prob_ready")
        chosen_ready, counts_ready = sem("chosen_ready"), sem("counts_ready")
        xh_ready = sem("xh_ready")
        numbers_ready, found_ready = sem("numbers_ready"), sem("found_ready")
        summed, sum_added = sem("summed"), sem("sum_added")
        step = sem("step")

        with nc.Block() as block:
            @block.vector
            def _(dve):
                done = [0]

                def link(ins):
                    done[0] += 1
                    ins.then_inc(step, 1)
                    dve.wait_ge(step, done[0])

                if n == 0:
                    dve.wait_ge(k.x_loaded, 16)
                for t in range(NT):
                    last = nc.vector.bn_stats(st[:, t], k.xs[:, t])
                link(last)
                for t in range(NT):
                    last = nc.vector.bn_aggr(mv[:, t], st[:, t])
                link(last)
                nc.vector.tensor_scalar(var_eps[:], mv[:, :, 1], EPS, None, ALU.add).then_inc(var_ready, 1)
                dve.wait_ge(rstd_ready, 1)
                link(nc.vector.tensor_tensor(rstd_sq[:], rstd[:], rstd[:], ALU.mult))
                link(nc.vector.tensor_tensor(var_eps2[:], mv[:, :, 1], rstd_sq[:], ALU.mult))
                nc.vector.tensor_scalar(var_eps2[:], var_eps2[:], EPS, None, ALU.add).then_inc(var_ready, 1)
                for t in range(NT):
                    last = nc.vector.tensor_scalar(xn[:, t], k.xs[:, t], mv[:, t, 0:1], rstd[:, t:t + 1],
                                                   ALU.subtract, ALU.mult)
                    last.then_inc(xn_ready, 1)
                dve.wait_ge(logits_ready, 1)
                link(nc.vector.tensor_copy(logit[:], logit_ps[:]))
                nc.vector.tensor_reduce(top[:], logit[:], AX.X, ALU.max)
                nc.vector.tensor_tensor(above[:], bc(logit[:], 2, NE), bc(logit[:], 3, NE), ALU.is_gt)
                link(nc.vector.tensor_tensor(equal[:], bc(logit[:], 2, NE), bc(logit[:], 3, NE),
                                             ALU.is_equal))
                nc.vector.tensor_tensor(below[:], logit[:], bc(top[:], 2, NE),
                                        ALU.subtract).then_inc(below_ready, 1)
                dve.wait_ge(k.const_made, k.N_CONST)
                link(nc.vector.tensor_tensor(equal[:], equal[:], bc(k.earlier[:], 1, NT), ALU.mult))
                link(nc.vector.tensor_tensor(above[:], above[:], equal[:], ALU.add))
                link(nc.vector.tensor_reduce(place[:], above[:], AX.X, ALU.add))
                nc.vector.tensor_scalar(chosen[:], place[:], float(TOPK), None,
                                        ALU.is_lt).then_inc(chosen_ready, 1)
                nc.vector.tensor_scalar(pick[:, 0], place[:], 0.0, None, ALU.is_equal)
                link(nc.vector.tensor_scalar(pick[:, 1], place[:], 1.0, None, ALU.is_equal))
                nc.vector.tensor_reduce(is_kan[:], pick[:, :, :, E2:NE], AX.X, ALU.add)
                dve.wait_ge(counts_ready, 1)
                link(nc.vector.tensor_copy(tile_sum[:], sum_ps[:]))
                for e in range(NE):
                    last = nc.vector.tensor_tensor_scan(up_to[:, :, e], k.scan_ones[:], tile_sum[:, :, e],
                                                        0.0, ALU.mult, ALU.add)
                link(last)
                link(nc.vector.tensor_scalar(blocks_i[:], up_to[:, NT - 1], float(P - 1), None, ALU.add))
                link(nc.vector.tensor_scalar(blocks_i[:], blocks_i[:], P.bit_length() - 1, None,
                                             ALU.logical_shift_right))
                link(nc.vector.tensor_copy(blocks[:], blocks_i[:]))
                for h in range(2):
                    last = nc.vector.tensor_tensor_scan(blocks_up_to[:, h * E2:(h + 1) * E2],
                                                        k.scan_ones[:, 0:E2], blocks[:, h * E2:(h + 1) * E2],
                                                        0.0, ALU.mult, ALU.add)
                link(last)
                link(nc.vector.tensor_tensor(base[:], blocks_up_to[:], blocks[:], ALU.subtract))
                link(nc.vector.tensor_scalar(base[:, E2:NE], base[:, E2:NE], blocks_up_to[:, E2 - 1:E2],
                                             1.0, ALU.add, ALU.add))
                link(nc.vector.tensor_scalar(base[:], base[:], 1.0, float(P), ALU.add, ALU.mult))
                link(nc.vector.tensor_tensor(up_to[:], up_to[:], tile_sum[:], ALU.subtract))
                link(nc.vector.tensor_tensor(pos[:], cum_ps[:], up_to[:], ALU.add))
                link(nc.vector.tensor_tensor(pos[:], pos[:], bc(base[:], 1, NT), ALU.add))
                link(nc.vector.tensor_tensor(tmp[:], pick[:], bc(pos[:], 1, TOPK), ALU.mult))
                link(nc.vector.tensor_reduce(at[:], tmp[:], AX.X, ALU.add))
                link(nc.vector.tensor_copy(at_i[:], at[:]))
                nc.vector.tensor_scalar(row_i[:], at_i[:], P - 1, None, ALU.bitwise_and)
                link(nc.vector.tensor_scalar(slot_i[:], at_i[:], P.bit_length() - 1, None,
                                             ALU.logical_shift_right))
                nc.vector.tensor_copy(row_f[:], row_i[:])
                link(nc.vector.tensor_copy(slot_f[:], slot_i[:]))
                link(nc.vector.tensor_tensor(in_slot[:], bc(slot_f[:].rearrange("p j t -> p (j t)"), 2, NS),
                                             bc(k.lane_no[:, 0:NS], 1, TOPK * NT), ALU.is_equal))
                nc.vector.tensor_tensor(numbers[:, :, 0], in_slot[:], bc(k.pair_no[:], 2, NS), ALU.mult)
                nc.vector.tensor_scalar(numbers[:, :, 1], in_slot[:], k.one_up[:], None, ALU.mult)
                for j in range(TOPK):
                    nc.vector.tensor_tensor(in_row[:, j * NT:(j + 1) * NT], bc(row_f[:, j], 2, P),
                                            bc(k.lane_no[:], 1, NT), ALU.is_equal).then_inc(numbers_ready, 1)
                nc.vector.tensor_copy(k.n_mlp[:], blocks_up_to[:, E2 - 1:E2])
                last_of = blocks_up_to[:].rearrange("p (h e) -> p h e", h=2)[:, :, E2 - 1]
                link(nc.vector.tensor_scalar(pairs_i[:], last_of, 2.0, None, ALU.add))
                nc.vector.tensor_scalar(k.n_pairs[:], pairs_i[:], 1, None, ALU.logical_shift_right)
                for h in range(2):
                    last = nc.vector.tensor_scalar(tab[:, h], k.slot_no[:], blocks_up_to[:, h * E2:h * E2 + 1],
                                                   None, ALU.is_ge)
                link(last)
                for e in range(1, E2 - 1):
                    for h in range(2):
                        last = nc.vector.scalar_tensor_tensor(
                            tab[:, h], k.slot_no[:], blocks_up_to[:, h * E2 + e:h * E2 + e + 1],
                            tab[:, h], ALU.is_ge, ALU.add)
                    link(last)
                for half in range(2):
                    nc.vector.tensor_copy(k.experts[:, :, :, 2 * half:2 * half + 2],
                                          tab[:, :, 2 * half:2 * half + NS - 2].rearrange(
                                              "p h (r two) -> p h r two", two=2))
                nc.vector.tensor_scalar(kan_rows[:], k.slot_no[:], blocks_up_to[:, E2 - 1:E2], float(T),
                                        ALU.is_ge, ALU.mult)
                dve.wait_ge(found_ready, 1)
                link(nc.vector.tensor_copy(found[:], found_ps[:]))
                nc.vector.scalar_tensor_tensor(spare[:], found[:, 1], 0.0, k.spare_row[:], ALU.is_equal, ALU.mult)
                link(nc.vector.scalar_tensor_tensor(code[:], found[:, 0], float(P), found[:, 1], ALU.mult, ALU.add))
                link(nc.vector.tensor_scalar(code[:], code[:], -1.0, None, ALU.add))
                nc.vector.tensor_tensor(k.rows_of[:, LEAD:NQ, 1], code[:], spare[:], ALU.add)
                link(nc.vector.tensor_copy(code_i[:], code[:]))
                link(nc.vector.tensor_scalar(token_i[:], code_i[:], T - 1, None, ALU.bitwise_and))
                link(nc.vector.tensor_copy(token[:], token_i[:]))
                nc.vector.tensor_tensor(k.rows_of[:, 0:NS, 0], token[:], kan_rows[:], ALU.add)
                dve.wait_ge(prob_ready, 1)
                link(nc.vector.tensor_tensor(weighed[:], prob[:], chosen[:], ALU.mult))
                nc.vector.tensor_tensor(tmp[:], pick[:], bc(prob[:], 1, TOPK), ALU.mult)
                link(nc.vector.tensor_reduce(den[:], weighed[:], AX.X, ALU.add))
                link(nc.vector.reciprocal(den[:], den[:]))
                nc.vector.tensor_reduce(k.weight[:], tmp[:], AX.X, ALU.add)
                link(nc.vector.tensor_scalar(den[:], den[:], 0.5, None, ALU.mult))
                link(nc.vector.tensor_tensor(k.weight[:], k.weight[:], bc(den[:], 1, TOPK), ALU.mult))
                if n == 0:
                    for e in range(E2):
                        dve.wait_ge(summed, e + 1)
                        sums = xT_ps[e % 2]
                        nc.vector.tensor_tensor(k.kan_b0[:, e], k.kan_b0[:, e], sums[:, 0:F2],
                                                ALU.add).then_inc(sum_added, 1)
                        nc.vector.tensor_tensor(k.kan_b1[:, e], k.kan_b1[:, e], sums[:, F2:F2 + C],
                                                ALU.add).then_inc(sum_added, 1)

            @block.sync
            def _(sp):
                if n == 0:
                    sp.dma_start(k.xs[:], a.x[0].rearrange("(t p) c -> p t c", p=P)).then_inc(k.x_loaded, 16)
                    load_shared(sp, k, a)
                load_mlps(sp, k, a, n)
                load_kan(sp, k, a, n, 0)
                rows = k.x_rows.rearrange("(h t p) c -> h p t c", h=2, p=P)
                sp.wait_ge(xn_ready, NT)
                sp.dma_start(rows[0], xn[:]).then_inc(k.rows_in_dram[n], 16)
                load_kan(sp, k, a, n, 1)
                sp.wait_ge(xh_ready, NT)
                sp.dma_start(rows[1], xh[:]).then_inc(k.rows_in_dram[n], 16)
                load_kan(sp, k, a, n, 2)
                load_kan(sp, k, a, n, 3)
                sp.wait_ge(k.rows_in_dram[n], 32)

            @block.gpsimd
            def _(pool):
                if n == 0:
                    make_constants(pool, k)
                    pool.wait_ge(k.const_made, k.N_CONST)
                pool.wait_ge(var_ready, 1)
                nc.gpsimd.tensor_tensor(rstd[:], var_eps[:], k.minus_half[:], ALU.pow).then_inc(rstd_ready, 1)
                pool.wait_ge(var_ready, 2)
                nc.gpsimd.tensor_tensor(rstd2[:], var_eps2[:], k.minus_half[:], ALU.pow).then_inc(rstd_ready, 1)

            @block.tensor
            def _(pe):
                pe.wait_ge(k.const_made, k.N_CONST)
                for g in range(NT // 4):
                    if g >= 2:
                        pe.wait_ge(xT_copied, g - 1)
                    for t in range(4 * g, 4 * g + 4):
                        pe.wait_ge(xn_ready, t + 1)
                        last = nc.tensor.transpose(xT_ps[g % 2][:, (t % 4) * P:(t % 4 + 1) * P], xn[:, t],
                                                   k.ident[:])
                    last.then_inc(xT_ready, 1)
                if n == 0:
                    pe.wait_ge(k.small_loaded, 16 * N_SHARED)
                for t in range(NT):
                    pe.wait_ge(xT_copied, t // 4 + 1)
                    last = nc.tensor.matmul(logit_ps[:, t], xnT[:, t * P:(t + 1) * P], k.gate_w[:],
                                            start=True, stop=True)
                last.then_inc(logits_ready, 1)
                pe.wait_ge(chosen_ready, 1)
                nc.tensor.matmul(sum_ps[:], k.ones[:], chosen[:], start=True, stop=True)
                nc.tensor.matmul(cum_ps[:], k.later[:], chosen[:], start=True,
                                 stop=True).then_inc(counts_ready, 1)
                for j in range(TOPK):
                    pe.wait_ge(numbers_ready, j + 1)
                    for v in range(j * NT, (j + 1) * NT):
                        last = nc.tensor.matmul(found_ps[:], in_row[:, v], numbers[:, v], start=(v == 0),
                                                stop=(v == TOPK * NT - 1))
                last.then_inc(found_ready, 1)
                if n == 0:
                    for e in range(E2):
                        pe.wait_ge(k.kan_loaded[0][e], 16 * 2)
                        if e >= 2:
                            pe.wait_ge(sum_added, 2 * (e - 1))
                        sums = xT_ps[e % 2]
                        for g in range(G):
                            nc.tensor.matmul(sums[:, 0:F2], k.ones[:], k.kan_w0[:, e, g], start=(g == 0),
                                             stop=(g == G - 1))
                        for c in range(F2C):
                            for g in range(G):
                                last = nc.tensor.matmul(sums[:, F2:F2 + C], k.ones[:], k.kan_w1[:, e, c, g],
                                                        start=(c == 0 and g == 0), stop=(c == F2C - 1 and g == G - 1))
                        last.then_inc(summed, 1)

            @block.scalar
            def _(act):
                for g in range(NT // 4):
                    act.wait_ge(xT_ready, g + 1)
                    nc.scalar.copy(xnT[:, g * 4 * P:(g + 1) * 4 * P], xT_ps[g % 2][:]).then_inc(xT_copied, 1)
                act.wait_ge(rstd_ready, 2)
                for t in range(NT):
                    nc.scalar.activation(xh[:, t], xn[:, t], ACT.Copy, scale=rstd2[:, t:t + 1]).then_inc(xh_ready, 1)
                act.wait_ge(below_ready, 1)
                nc.scalar.activation(prob[:], below[:], ACT.Exp).then_inc(prob_ready, 1)


def load_experts(nc, eng, row):
    return nc.values_load_multi_w_load_instructions(
        row, engines=[eng.engine], min_val=0, max_val=E2 - 1,
        skip_runtime_bounds_check_because="the table counts the experts that end before a block, E2 - 1 at most")[1]


def mlp_blocks(nc, k, a, n):
    with ExitStack() as ctx:
        sb = lambda name, shape, dt=F32: ctx.enter_context(nc.sbuf_tensor(f"{name}_{n}", shape, dt))
        ps = lambda name, shape: ctx.enter_context(nc.psum_tensor(f"{name}_{n}", shape, F32))
        sem = lambda name: k.phase_sem(f"{name}_{n}")
        x_in = [sb(f"m_x_in{u}", [P, C]) for u in range(2)]
        xT = sb("m_xT", [P, P])
        z = sb("m_z", [P, F])
        hT = sb("m_hT", [P, FC, P])
        y = [sb(f"m_y{u}", [P, C]) for u in range(2)]
        rows_now = [sb(f"m_rows_now{u}", [P, 2], I32) for u in range(2)]
        xT_ps = ps("m_xT_ps", [P, P])
        z_ps = ps("m_z_ps", [P, F])
        zT_ps = ps("m_zT_ps", [P, FC, P])
        y_ps = ps("m_y_ps", [P, C])
        loaded, stored = ([sem(f"m_{x}{u}") for u in range(2)] for x in ("loaded", "stored"))
        turned, xT_ready = sem("m_turned"), sem("m_xT_ready")
        z_done, z_ready, zT_done = sem("m_z_done"), sem("m_z_ready"), sem("m_zT_done")
        hT_ready, y_done, y_ready, y_free = sem("m_hT_ready"), sem("m_y_done"), sem("m_y_ready"), sem("m_y_free")
        cleared, noted, rows_ready = sem("m_cleared"), sem("m_noted"), sem("m_rows_ready")

        def pairs(eng):
            return eng.value_load(k.n_pairs[0:1, 0:1], min_val=1, max_val=(MAXB + 2) // 2)

        def experts(eng, ii):
            return load_experts(nc, eng, k.experts[0:1, 0, bass.ds(ii, 1)])

        with nc.Block() as block:
            @block.gpsimd
            def _(pool):
                end = pairs(pool)

                def gather(u, rows):
                    pool.indirect_dma_start(
                        x_in[u][:], None, k.x_rows,
                        bass.IndirectOffsetOnAxis(ap=rows.bitcast(U32), axis=0)).then_inc(loaded[u], 16)

                def one_round(i, ii, u, first):
                    pool.wait_ge(turned, i + 1)
                    if not first:
                        pool.wait_ge(stored[u], ii * 16)
                    pool.sem_inc(y_free, 1)
                    nc.gpsimd.tensor_copy(rows_now[u][:], k.rows_of[:, bass.ds(i + LEAD, 1)]
                                          ).then_inc(rows_ready, 1)
                    pool.wait_ge(rows_ready, i + 1)
                    pool.sem_inc(noted, 1)
                    gather(u, rows_now[u][:, 0:1])
                    pool.wait_ge(y_ready, i + 2)
                    pool.sem_inc(noted, 1)
                    pool.indirect_dma_start(
                        k.y_rows, bass.IndirectOffsetOnAxis(ap=rows_now[u][:, 1:2].bitcast(U32), axis=0),
                        y[u][:], None).then_inc(stored[u], 16)

                for u in range(2):
                    gather(u, k.rows_of[:, 1 + u, 0:1])
                for u in range(2):
                    one_round(u, 0, u, True)
                with pool.Fori(1, end) as ii:
                    for u in range(2):
                        one_round(2 * ii + u, ii, u, False)
                for u in range(2):
                    pool.wait_ge(loaded[u], end * 16 + 16)
                    pool.wait_ge(stored[u], end * 16)
                    pool.sem_inc(noted, 1)

            @block.tensor
            def _(pe):
                end = pairs(pe)

                def turn(u, nth):
                    pe.wait_ge(loaded[u], nth * 16)
                    nc.tensor.transpose(xT_ps[:], x_in[u][:], k.ident[:]).then_inc(turned, 1)

                def by_w1(block, e):
                    pe.wait_ge(xT_ready, block + 1)
                    nc.tensor.matmul(z_ps[:], xT[:], k.mlp_w1[:, bass.ds(e, 1)], start=True,
                                     stop=True).then_inc(z_done, 1)

                turn(0, 1)
                pe.wait_ge(k.mlp_loaded[n], 16 * N_MLP)
                pe.sem_inc(y_ready, 1)
                by_w1(0, experts(pe, 0)[1])
                with pe.Fori(0, end) as ii:
                    for u in range(2):
                        i = 2 * ii + u
                        turn(1 - u, ii + 1 + u)
                        if u == 0:
                            e_pair = experts(pe, ii)
                        e_last, e_next = e_pair[u], e_pair[u + 2]
                        pe.wait_ge(hT_ready, i + 1)
                        pe.wait_ge(y_ready, i + 1)
                        for c in range(FC):
                            last = nc.tensor.matmul(y_ps[:], hT[:, c], k.mlp_w2[:, bass.ds(e_last, 1), c],
                                                    start=(c == 0), stop=(c == FC - 1))
                        last.then_inc(y_done, 1)
                        pe.wait_ge(z_ready, i + 1)
                        for c in range(FC):
                            last = nc.tensor.transpose(zT_ps[:, c], z[:, c * P:(c + 1) * P], k.ident[:])
                        last.then_inc(zT_done, 1)
                        by_w1(i + 1, e_next)

            @block.vector
            def _(dve):
                end = pairs(dve)
                nc.vector.memset(hT[:], 0.0).then_inc(cleared, 1)
                dve.wait_ge(turned, 1)
                nc.vector.tensor_copy(xT[:], xT_ps[:]).then_inc(xT_ready, 1)
                with dve.Fori(0, end) as ii:
                    e_pair = experts(dve, ii)
                    for u in range(2):
                        i = 2 * ii + u
                        e_last, e = e_pair[u], e_pair[u + 1]
                        dve.wait_ge(z_done, i + 1)
                        nc.vector.tensor_tensor(z[:], z_ps[:], k.mlp_b1[:, bass.ds(e, 1)],
                                                ALU.add).then_inc(z_ready, 1)
                        dve.wait_ge(turned, i + 2)
                        nc.vector.tensor_copy(xT[:], xT_ps[:]).then_inc(xT_ready, 1)
                        dve.wait_ge(y_done, i + 1)
                        dve.wait_ge(y_free, i + 1)
                        nc.vector.tensor_tensor(y[u][:], y_ps[:], k.mlp_b2[:, bass.ds(e_last, 1)],
                                                ALU.add).then_inc(y_ready, 1)

            @block.scalar
            def _(act):
                end = pairs(act)
                act.wait_ge(cleared, 1)
                act.preload_act_table(ACT.Gelu)
                act.sem_inc(hT_ready, 1)
                with act.Fori(0, end) as ii:
                    for u in range(2):
                        act.wait_ge(zT_done, 2 * ii + u + 1)
                        nc.scalar.activation(hT[:], zT_ps[:], ACT.Gelu).then_inc(hT_ready, 1)


def kan_blocks(nc, k, a, n):
    with ExitStack() as ctx:
        sb = lambda name, shape, dt=F32: ctx.enter_context(nc.sbuf_tensor(f"{name}_{n}", shape, dt))
        ps = lambda name, shape: ctx.enter_context(nc.psum_tensor(f"{name}_{n}", shape, F32))
        sem = lambda name: k.phase_sem(f"{name}_{n}")
        x_in = [sb(f"k_x_in{u}", [P, C]) for u in range(2)]
        h0T = sb("k_h0T", [P, P])
        tanh0 = sb("k_tanh0", [P, G, P])
        basis0 = sb("k_basis0", [P, G, P])
        z = sb("k_z", [P, F2])
        st = sb("k_st", [P, 6])
        mv = sb("k_mv", [P, 2])
        var_eps = sb("k_var_eps", [P, 1])
        rstd = sb("k_rstd", [P, 1])
        zn = sb("k_zn", [P, F2])
        h1T = sb("k_h1T", [P, F2C, P])
        tanh1 = sb("k_tanh1", [P, G, F2C, P])
        basis1 = sb("k_basis1", [P, G, F2C, P])
        y = [sb(f"k_y{u}", [P, C]) for u in range(2)]
        rows_now = [sb(f"k_rows_now{u}", [P, 2], I32) for u in range(2)]
        xT_ps = ps("k_xT_ps", [P, P])
        z_ps = ps("k_z_ps", [P, F2])
        znT_ps = ps("k_znT_ps", [P, F2C, P])
        y_ps = ps("k_y_ps", [P, C])
        loaded, stored = ([sem(f"k_{x}{u}") for u in range(2)] for x in ("loaded", "stored"))
        turned, h0_ready = sem("k_turned"), sem("k_h0_ready")
        tanh0_done, basis0_ready = sem("k_tanh0_done"), sem("k_basis0_ready")
        tanh1_done, basis1_ready = sem("k_tanh1_done"), sem("k_basis1_ready")
        z_done, z_ready, stats_done, var_ready = sem("k_z_done"), sem("k_z_ready"), sem("k_stats_done"), sem("k_var_ready")
        mean_ready, rstd_ready, zn_ready = sem("k_mean_ready"), sem("k_rstd_ready"), sem("k_zn_ready")
        znT_done, h1_ready = sem("k_znT_done"), sem("k_h1_ready")
        y_done, y_ready, y_free = sem("k_y_done"), sem("k_y_ready"), sem("k_y_free")
        noted, rows_ready = sem("k_noted"), sem("k_rows_ready")
        H0, H1 = 2, 4
        G0, G1 = G // H0, G // H1

        def pairs(eng):
            return eng.value_load(k.n_pairs[0:1, 1:2], min_val=1, max_val=(MAXB + 2) // 2)

        def experts(eng, ii):
            return load_experts(nc, eng, k.experts[0:1, 1, bass.ds(ii, 1)])

        with nc.Block() as block:
            @block.gpsimd
            def _(pool):
                end = pairs(pool)
                start = pool.value_load(k.n_mlp[0:1, 0:1], min_val=0, max_val=MAXB)

                def rows_at(q):
                    at = nc.s_assert_within(q, 0, NQ - 1, skip_runtime_bounds_check_because=BOUND)
                    return k.rows_of[:, bass.ds(at, 1)]

                def gather(u):
                    pool.indirect_dma_start(
                        x_in[u][:], None, k.x_rows,
                        bass.IndirectOffsetOnAxis(ap=rows_now[u][:, 0:1].bitcast(U32), axis=0)
                    ).then_inc(loaded[u], 16)

                def one_round(i, ii, u, first):
                    pool.wait_ge(turned, i + 1)
                    if not first:
                        pool.wait_ge(stored[u], ii * 16)
                    pool.sem_inc(y_free, 1)
                    nc.gpsimd.tensor_copy(rows_now[u][:], rows_at(start + i + (1 + LEAD))
                                          ).then_inc(rows_ready, 1)
                    pool.wait_ge(rows_ready, i + 3)
                    pool.sem_inc(noted, 1)
                    gather(u)
                    pool.wait_ge(var_ready, i + 1)
                    nc.gpsimd.tensor_tensor(rstd[:], var_eps[:], k.minus_half[:, 0:1],
                                            ALU.pow).then_inc(rstd_ready, 1)
                    pool.wait_ge(y_ready, i + 2)
                    pool.sem_inc(noted, 1)
                    pool.indirect_dma_start(
                        k.y_rows, bass.IndirectOffsetOnAxis(ap=rows_now[u][:, 1:2].bitcast(U32), axis=0),
                        y[u][:], None).then_inc(stored[u], 16)

                for u in range(2):
                    nc.gpsimd.tensor_copy(rows_now[u][:], rows_at(start + (2 + u))).then_inc(rows_ready, 1)
                pool.wait_ge(rows_ready, 2)
                for u in range(2):
                    gather(u)
                for u in range(2):
                    one_round(u, 0, u, True)
                with pool.Fori(1, end) as ii:
                    for u in range(2):
                        one_round(2 * ii + u, ii, u, False)
                for u in range(2):
                    pool.wait_ge(loaded[u], end * 16 + 16)
                    pool.wait_ge(stored[u], end * 16)
                    pool.sem_inc(noted, 1)

            @block.tensor
            def _(pe):
                end = pairs(pe)

                def turn(u, nth):
                    pe.wait_ge(loaded[u], nth * 16)
                    nc.tensor.transpose(xT_ps[:], x_in[u][:], k.ident[:]).then_inc(turned, 1)

                def by_w0(block, e):
                    for g in range(G):
                        if g % G0 == 0:
                            pe.wait_ge(basis0_ready, H0 * block + (g // G0 + 1))
                        last = nc.tensor.matmul(z_ps[:], basis0[:, g], k.kan_w0[:, bass.ds(e, 1), g],
                                                start=(g == 0), stop=(g == G - 1))
                    last.then_inc(z_done, 1)

                turn(0, 1)
                pe.wait_ge(h0_ready, 1)
                turn(1, 1)
                for e in range(E2):
                    pe.wait_ge(k.kan_loaded[n][e], 16 * 2)
                pe.sem_inc(y_ready, 1)
                by_w0(0, experts(pe, 0)[1])
                with pe.Fori(0, end) as ii:
                    e_pair = experts(pe, ii)
                    for u in range(2):
                        i = 2 * ii + u
                        e_last, e_next = e_pair[u], e_pair[u + 2]
                        pe.wait_ge(y_ready, i + 1)
                        for g in range(G):
                            if g % G1 == 0:
                                pe.wait_ge(basis1_ready, H1 * i + g // G1 + 1)
                            for c in range(F2C):
                                last = nc.tensor.matmul(y_ps[:], basis1[:, g, c],
                                                        k.kan_w1[:, bass.ds(e_last, 1), c, g],
                                                        start=(g == 0 and c == 0), stop=(g == G - 1 and c == F2C - 1))
                        last.then_inc(y_done, 1)
                        pe.wait_ge(zn_ready, i + 1)
                        for c in range(F2C):
                            last = nc.tensor.transpose(znT_ps[:, c], zn[:, c * P:(c + 1) * P], k.ident[:])
                        last.then_inc(znT_done, 1)
                        pe.wait_ge(h0_ready, i + 2)
                        turn(u, ii + 2)
                        by_w0(i + 1, e_next)

            @block.vector
            def _(dve):
                end = pairs(dve)

                def affine0(e, blocks_turned):
                    dve.wait_ge(turned, blocks_turned)
                    nc.vector.tensor_scalar(h0T[:], xT_ps[:], k.kan_g0[:, bass.ds(e, 1)],
                                            k.kan_c0[:, bass.ds(e, 1)], ALU.mult, ALU.add).then_inc(h0_ready, 1)

                def square0(before):
                    for h in range(H0):
                        dve.wait_ge(tanh0_done, before + h + 1)
                        part = slice(h * G0, (h + 1) * G0)
                        nc.vector.tensor_tensor(basis0[:, part], tanh0[:, part], tanh0[:, part],
                                                ALU.mult).then_inc(basis0_ready, 1)

                nc.vector.memset(h1T[:], 0.0).then_inc(h1_ready, 1)
                affine0(experts(dve, 0)[1], 1)
                square0(0)
                with dve.Fori(0, end) as ii:
                    e_pair = experts(dve, ii)
                    for u in range(2):
                        i = 2 * ii + u
                        e_last, e, e_next = e_pair[u:u + 3]
                        dve.wait_ge(tanh0_done, H0 * i + H0)
                        affine0(e_next, i + 2)
                        for h in range(H1):
                            dve.wait_ge(tanh1_done, H1 * i + h + 1)
                            part = slice(h * G1, (h + 1) * G1)
                            nc.vector.tensor_tensor(basis1[:, part], tanh1[:, part], tanh1[:, part],
                                                    ALU.mult).then_inc(basis1_ready, 1)
                        dve.wait_ge(z_done, i + 1)
                        nc.vector.tensor_tensor(z[:], k.kan_b0[:, bass.ds(e, 1)], z_ps[:],
                                                ALU.subtract).then_inc(z_ready, 1)
                        dve.wait_ge(z_ready, i + 1)
                        nc.vector.bn_stats(st[:], z[:]).then_inc(stats_done, 1)
                        dve.wait_ge(h0_ready, 1)
                        dve.wait_ge(stats_done, i + 1)
                        nc.vector.bn_aggr(mv[:], st[:]).then_inc(mean_ready, 1)
                        dve.wait_ge(mean_ready, i + 1)
                        nc.vector.tensor_scalar(var_eps[:], mv[:, 1:2], EPS, None, ALU.add).then_inc(var_ready, 1)
                        square0(H0 * i + H0)
                        dve.wait_ge(rstd_ready, i + 1)
                        nc.vector.tensor_scalar(zn[:], z[:], mv[:, 0:1], rstd[:], ALU.subtract,
                                                ALU.mult).then_inc(zn_ready, 1)
                        dve.wait_ge(znT_done, i + 1)
                        dve.wait_ge(tanh1_done, H1 * i + H1)
                        for c in range(F2C):
                            last = nc.vector.tensor_scalar(h1T[:, c], znT_ps[:, c], k.kan_g1[:, c, bass.ds(e, 1)],
                                                           k.kan_c1[:, c, bass.ds(e, 1)], ALU.mult, ALU.add)
                        last.then_inc(h1_ready, 1)
                        dve.wait_ge(y_done, i + 1)
                        dve.wait_ge(y_free, i + 1)
                        nc.vector.tensor_tensor(y[u][:], k.kan_b1[:, bass.ds(e_last, 1)], y_ps[:],
                                                ALU.subtract).then_inc(y_ready, 1)

            @block.scalar
            def _(act):
                end = pairs(act)

                def tanh0_parts():
                    for g in range(G):
                        ins = nc.scalar.activation(tanh0[:, g], h0T[:], ACT.Tanh, bias=float(-0.5 * GRID[g]),
                                                   scale=0.5)
                        if g % G0 == G0 - 1:
                            ins.then_inc(tanh0_done, 1)

                act.wait_ge(h0_ready, 1)
                tanh0_parts()
                with act.Fori(0, end) as ii:
                    for u in range(2):
                        i = 2 * ii + u
                        act.wait_ge(h1_ready, i + 1)
                        for g in range(G):
                            ins = nc.scalar.activation(tanh1[:, g], h1T[:], ACT.Tanh, bias=float(-0.5 * GRID[g]),
                                                       scale=0.5)
                            if g % G1 == G1 - 1:
                                ins.then_inc(tanh1_done, 1)
                        act.wait_ge(h0_ready, i + 2)
                        act.wait_ge(basis0_ready, H0 * i + H0)
                        tanh0_parts()


def combine(nc, k, a, n, out):
    PART = 4
    with ExitStack() as ctx:
        got = ctx.enter_context(nc.sbuf_tensor(f"got_{n}", [P, TOPK, NT, C], F32))
        loaded = [k.phase_sem(f"got_loaded{g}_{n}") for g in range(NT // PART)]
        first_added, x_ready = (k.phase_sem(f"{x}_{n}") for x in ("first_added", "x_ready"))
        rows = k.y_rows[0:TOPK * T].rearrange("(j t p) c -> p j t c", j=TOPK, p=P)
        parts = [slice(g * PART, (g + 1) * PART) for g in range(NT // PART)]
        with nc.Block() as block:
            @block.scalar
            def _(act):
                for g, part in enumerate(parts):
                    act.dma_start(got[:, 1, part], rows[:, 1, part]).then_inc(loaded[g], 16)

            @block.vector
            def _(dve):
                for g in range(NT // PART):
                    dve.wait_ge(loaded[g], 16 * TOPK)
                    for j in range(TOPK):
                        for t in range(g * PART, (g + 1) * PART):
                            last = nc.vector.scalar_tensor_tensor(k.xs[:, t], got[:, j, t], k.weight[:, j, t:t + 1],
                                                                  k.xs[:, t], ALU.mult, ALU.add)
                        if j == 0:
                            last.then_inc(first_added, 1)
                            dve.wait_ge(first_added, g + 1)
                    last.then_inc(x_ready, 1)

            @block.sync
            def _(sp):
                for g, part in enumerate(parts):
                    sp.dma_start(got[:, 0, part], rows[:, 0, part]).then_inc(loaded[g], 16)
                if out is not None:
                    tiles = out[0].rearrange("(t p) c -> p t c", p=P)
                    for g, part in enumerate(parts):
                        sp.wait_ge(x_ready, g + 1)
                        sp.dma_start(tiles[:, part], k.xs[:, part]).then_inc(k.stored_out, 16)
                    sp.wait_ge(k.stored_out, 16 * (NT // PART))


def moe(nc, k, a, n, out=None):
    with ExitStack() as ctx:
        moe_weights(nc, k, ctx, n)
        route(nc, k, a, n)
        mlp_blocks(nc, k, a, n)
        kan_blocks(nc, k, a, n)
        combine(nc, k, a, n, out)

NH = 16
HD = C // NH
PAIRS = NH // 2
WINDOW = 128
assert WINDOW == P
PARTS = 3
RUNS = [(0, 3), (3, 2), (5, 1)]
N_PROD = 6
M_ROW = N_PROD * HD
NEG = -1e30
VW = PARTS * HD + 2
HID = 352
HIDC = [(0, 128), (128, 128), (256, 96)]
QK_G = 4


def layernorm_stats(dve, link, x, st, mv, var_eps, ready):
    for t in range(NT):
        last = dve.bn_stats(st[:, t], x[:, t])
    link(last)
    for t in range(NT):
        last = dve.bn_aggr(mv[:, t], st[:, t])
    link(last)
    dve.tensor_scalar(var_eps[:], mv[:, :, 1], EPS, None, ALU.add).then_inc(ready, 1)


def project(nc, k, a, s):
    with ExitStack() as ctx:
        sb = lambda name, shape, dt=F32: ctx.enter_context(nc.sbuf_tensor(f"a_{name}", shape, dt))
        ps = lambda name, shape: ctx.enter_context(nc.psum_tensor(f"a_{name}", shape, F32))
        sem = lambda name: k.phase_sem(f"a_{name}")
        W4 = 4 * P
        NCH = NT // 4
        n1 = sb("n1", [P, NT, C])
        n1T = sb("n1T", [P, T])
        w = sb("w", [P, 3, C])
        wp = sb("wp", [P, 4, C])
        cos = sb("cos", [P, T])
        sin = sb("sin", [P, T])
        st = sb("st", [P, NT, 6])
        mv = sb("mv", [P, NT, 2])
        rstd_sq = sb("rstd_sq", [P, NT])
        scale = sb("scale", [P, NT])
        var_eps = sb("var_eps", [P, NT])
        rstd = sb("rstd", [P, 2, NT])
        part = sb("part", [P, 2, PARTS, 2 * W4], BF16)
        by_cos = sb("by_cos", [P, W4])
        by_sin = sb("by_sin", [P, W4])
        turned_ = sb("turned", [P, W4])
        rest = sb("rest", [P, W4])
        vrest = sb("vrest", [P, W4])
        vrest2 = sb("vrest2", [P, W4])
        nT_ps = ps("nT_ps", [P, W4])
        q_ps = [[ps(f"q_ps{x}{y}", [P, W4]) for y in range(2)] for x in range(2)]
        v_ps = ps("v_ps", [P, 4, C])
        loaded, w_swapped, var_ready, rstd_ready = sem("loaded"), sem("w_swapped"), sem("var_ready"), sem("rstd_ready")
        n1_ready, nT_done, nT_ready = sem("n1_ready"), sem("nT_done"), sem("nT_ready")
        qk_done, qk_used, v_done, v_used = sem("qk_done"), sem("qk_used"), sem("v_done"), sem("v_used")
        rot_ready, hi_ready, rest_ready, mid_ready = sem("rot_ready"), sem("hi_ready"), sem("rest_ready"), sem("mid_ready")
        parts_ready, k_cleared, q_cleared = sem("parts_ready"), sem("k_cleared"), sem("q_cleared")
        parts_out = [sem(f"parts_out{x}") for x in range(2)]
        v_set, k_ones = sem("v_set"), sem("k_ones")
        stacked = [sem("stacked"), k.sem("stacked_by_pool")]
        v_hi, v_rest, v_mid, v_rest2, v_split = sem("v_hi"), sem("v_rest"), sem("v_mid"), sem("v_rest2"), sem("v_split")
        step = sem("step")
        parts_dram = nc.dram_tensor("qk_parts", [2, 2, PARTS, HD * PAIRS, T], BF16, kind="Internal").ap()
        NU = 2 * NCH

        def key_rows(r0, r1, odd):
            return s.k_stack[r0:r1].bitcast(F32).rearrange("r (p two) t -> r two p t", two=2)[:, odd]

        def load_stack(q, odd, h, x, loaded_by_q):
            cols = slice(2 * h * W4, 2 * (h + 1) * W4)
            for run, (c0, cn) in enumerate(RUNS):
                if x == 0:
                    rows = slice(64 * odd + c0 * HD, 64 * odd + (c0 + cn) * HD)
                    q.dma_start(s.q_stack[rows, :, cols],
                                parts_dram[x, odd, 0:cn, :, cols].rearrange("c (d p) t -> (c d) p t", d=HD)
                                ).then_inc(loaded_by_q, 16)
                    continue
                for c in range(c0, c0 + cn):
                    rows = slice(64 * odd + c * HD, 64 * odd + (c + 1) * HD)
                    q.dma_start(s.k_stack[rows, odd::2, cols],
                                parts_dram[x, odd, run, :, cols].rearrange("(d p) t -> d p t", d=HD)
                                ).then_inc(loaded_by_q, 16)

        with nc.Block() as block:
            @block.sync
            def _(sp):
                sp.dma_start(w[:, 0], a.wq).then_inc(loaded, 16)
                sp.dma_start(w[:, 1], a.wk).then_inc(loaded, 16)
                sp.dma_start(w[:, 2], a.wv).then_inc(loaded, 16)
                sp.dma_start(k.ln_vec[:], a.attn_ln).then_inc(loaded, 16)
                sp.dma_start(cos[:], a.cos).then_inc(loaded, 16)
                sp.dma_start(sin[:], a.sin).then_inc(loaded, 16)
                sp.dma_start(s.wo[:], a.wo).then_inc(s.tail_loaded, 16)
                sp.dma_start(s.w1[:], a.w1).then_inc(s.tail_loaded, 16)
                sp.dma_start(s.w3[:], a.w3).then_inc(s.tail_loaded, 16)
                for c, (at, size) in enumerate(HIDC):
                    sp.dma_start(s.w2[0:size, c], a.w2[at:at + size]).then_inc(s.tail_loaded, 16)
                def store_parts(h, x):
                    cols = slice(2 * h * W4, 2 * (h + 1) * W4)
                    sp.wait_ge(parts_ready, 2 * (2 * h + 1) + 2 - x)
                    for odd in range(2):
                        sp.dma_start(parts_dram[x, odd, :, :, cols].rearrange("r k t -> k r t"),
                                     part[64 * odd:64 * (odd + 1), x]).then_inc(parts_out[x], 16)

                store_parts(0, 1)
                store_parts(0, 0)
                sp.wait_ge(k_cleared, 2)
                sp.wait_ge(k_ones, 2)
                sp.wait_ge(q_cleared, 1)
                for x in (1, 0):
                    sp.wait_ge(parts_out[x], 16 * 2)
                    load_stack(sp, 0, 0, x, stacked[0])
                for x in (1, 0):
                    store_parts(1, x)
                    sp.wait_ge(parts_out[x], 16 * 2 * 2)
                    load_stack(sp, 0, 1, x, stacked[0])
                for q in range(2):
                    sp.wait_ge(stacked[q], 16 * (NCH // 2) * (len(RUNS) + N_PROD))

            @block.gpsimd
            def _(pool):
                pool.memset(s.mask[:], 0.0).then_inc(s.mask_set, 1)
                pool.wait_ge(s.mask_set, 1)
                pool.affine_select(out=s.mask[:], in_=s.mask[:], compare_op=ALU.is_ge, fill=NEG, base=0,
                                   pattern=[[0, 2], [1, 2 * P]], channel_multiplier=-1).then_inc(s.mask_set, 1)
                pool.wait_ge(s.mask_set, 2)
                pool.affine_select(out=s.mask[:], in_=s.mask[:], compare_op=ALU.is_ge, fill=NEG, base=WINDOW,
                                   pattern=[[0, 2], [-1, 2 * P]], channel_multiplier=1).then_inc(s.mask_set, 1)
                pool.memset(s.q_stack[:].bitcast(F32), 0.0).then_inc(q_cleared, 1)
                pool.wait_ge(var_ready, 1)
                nc.gpsimd.tensor_tensor(rstd[:, 0], var_eps[:], k.minus_half[:], ALU.pow).then_inc(rstd_ready, 1)
                pool.wait_ge(var_ready, 2)
                nc.gpsimd.tensor_tensor(rstd[:, 1], var_eps[:], k.minus_half[:], ALU.pow).then_inc(rstd_ready, 1)
                ones2 = float(np.array([0x3F803F80], np.uint32).view(np.float32)[0])
                pool.wait_ge(rstd_ready, 2)
                pool.memset(key_rows(32, 64, 0), ones2).then_inc(k_ones, 1)
                pool.wait_ge(k_ones, 1)
                pool.memset(key_rows(96, 128, 1), ones2).then_inc(k_ones, 1)
                pool.wait_ge(k_cleared, 2)
                pool.wait_ge(k_ones, 2)
                for h in range(NCH // 2):
                    for x in (1, 0):
                        pool.wait_ge(parts_out[x], 16 * 2 * (h + 1))
                        load_stack(pool, 1, h, x, stacked[1])

            @block.vector
            def _(dve):
                done = [0]

                def link(ins):
                    done[0] += 1
                    ins.then_inc(step, 1)
                    dve.wait_ge(step, done[0])

                nc.vector.tensor_copy(s.ident16[:], k.ident[:]).then_inc(s.ident16_ready, 1)
                layernorm_stats(nc.vector, link, k.xs, st, mv, var_eps, var_ready)
                dve.wait_ge(rstd_ready, 1)
                link(nc.vector.tensor_tensor(rstd_sq[:], rstd[:, 0], rstd[:, 0], ALU.mult))
                link(nc.vector.tensor_tensor(var_eps[:], mv[:, :, 1], rstd_sq[:], ALU.mult))
                nc.vector.tensor_scalar(var_eps[:], var_eps[:], EPS, None, ALU.add).then_inc(var_ready, 1)
                for t in range(NT):
                    nc.vector.tensor_scalar(s.res[:, t], k.xs[:, t], mv[:, t, 0:1], rstd[:, 0, t:t + 1],
                                            ALU.subtract, ALU.mult)
                dve.wait_ge(rstd_ready, 2)
                link(nc.vector.tensor_tensor(scale[:], rstd[:, 0], rstd[:, 1], ALU.mult))
                for t in range(NT):
                    nc.vector.tensor_scalar(n1[:, t], k.xs[:, t], mv[:, t, 0:1], scale[:, t:t + 1],
                                            ALU.subtract, ALU.mult).then_inc(n1_ready, 1)
                dve.wait_ge(loaded, 16 * 6)
                link(nc.vector.tensor_scalar(w[:, 0], w[:, 0], float(HD) ** -0.5, None, ALU.mult))
                for x in range(2):
                    src = w[:, x].rearrange("r (p o e f) -> r o e f p", p=PAIRS, o=2, f=2)
                    same = wp[:, x].rearrange("r (o e f p) -> r o e f p", p=PAIRS, o=2, f=2)
                    swapped = wp[:, 2 + x].rearrange("r (o e f p) -> r o e f p", p=PAIRS, o=2, f=2)
                    for f in range(2):
                        nc.vector.tensor_copy(same[:, :, :, f], src[:, :, :, f]).then_inc(w_swapped, 1)
                        nc.vector.tensor_copy(swapped[:, :, :, f], src[:, :, :, 1 - f]).then_inc(w_swapped, 1)
                dve.wait_ge(v_set, 1)

                def values(g):
                    dst = s.v_parts[:, g * 4 + 1:(g + 1) * 4 + 1]
                    by_head = lambda x: x.rearrange("p (t h d) -> p t h d", t=4, h=NH)
                    dve.wait_ge(v_done, g + 1)
                    v = v_ps[:].rearrange("p t (h d) -> p t h d", h=NH)
                    link(nc.vector.tensor_copy(dst[:, :, :, 0:HD], v))
                    nc.vector.tensor_tensor(by_head(vrest[:]), v, dst[:, :, :, 0:HD], ALU.subtract).then_inc(v_used, 1)
                    dve.wait_ge(v_used, g + 1)
                    link(nc.vector.tensor_copy(dst[:, :, :, HD:2 * HD], by_head(vrest[:])))
                    link(nc.vector.tensor_tensor(dst[:, :, :, 2 * HD:3 * HD], by_head(vrest[:]),
                                                 dst[:, :, :, HD:2 * HD], ALU.subtract))

                for u in range(NU):
                    x, g = 1 - u % 2, u // 2
                    cols = slice(g * W4, (g + 1) * W4)
                    dve.wait_ge(qk_done, u + 1)
                    if u >= 1:
                        dve.wait_ge(hi_ready, u)
                    nc.vector.tensor_tensor(by_cos[:], q_ps[x][0][:], cos[:, cols], ALU.mult)
                    nc.vector.tensor_tensor(by_sin[:], q_ps[x][1][:], sin[:, cols], ALU.mult).then_inc(qk_used, 1)
                    dve.wait_ge(qk_used, u + 1)
                    nc.vector.tensor_tensor(turned_[:], by_cos[:], by_sin[:], ALU.add).then_inc(rot_ready, 1)
                    if u % 2 == 0:
                        values(g)
                    half = slice((g % 2) * W4, (g % 2 + 1) * W4)
                    dve.wait_ge(hi_ready, u + 1)
                    nc.vector.tensor_tensor(rest[:], turned_[:], part[:, x, 0, half],
                                            ALU.subtract).then_inc(rest_ready, 1)
                    dve.wait_ge(mid_ready, u + 1)
                    nc.vector.tensor_tensor(part[:, x, 2, half], rest[:], part[:, x, 1, half],
                                            ALU.subtract).then_inc(parts_ready, 1)

            @block.scalar
            def _(act):
                def chunk_T(g):
                    act.wait_ge(nT_done, g + 1)
                    nc.scalar.activation(n1T[:, g * W4:(g + 1) * W4], nT_ps[:], ACT.Identity,
                                         bias=k.ln_vec[:, 1:2], scale=k.ln_vec[:, 0:1]).then_inc(nT_ready, 1)

                nc.scalar.copy(s.v_parts[:].rearrange("p t h d -> p (t h d)"),
                               k.scan_ones[:, 0:1].to_broadcast([P, (NT + 1) * NH * VW])).then_inc(v_set, 1)
                for r0, r1, odd in ((64, 128, 0), (0, 64, 1)):
                    nc.scalar.activation(key_rows(r0, r1, odd),
                                         bc(bc(k.scan_ones[r0:r1, 0], 1, T // 2), 1, PAIRS),
                                         ACT.Copy, scale=0.0).then_inc(k_cleared, 1)
                act.wait_ge(loaded, 16 * 6)
                chunk_T(0)
                for u in range(NU):
                    x, g = 1 - u % 2, u // 2
                    if u % 2 == 0 and g + 1 < NCH:
                        chunk_T(g + 1)
                    act.wait_ge(rot_ready, u + 1)
                    half = slice((g % 2) * W4, (g % 2 + 1) * W4)
                    if g % 2 == 0 and g:
                        act.wait_ge(parts_out[x], 16 * 2 * (g // 2))
                    nc.scalar.copy(part[:, x, 0, half], turned_[:]).then_inc(hi_ready, 1)
                    act.wait_ge(rest_ready, u + 1)
                    nc.scalar.copy(part[:, x, 1, half], rest[:]).then_inc(mid_ready, 1)

            @block.tensor
            def _(pe):
                def chunk_T(g):
                    if g:
                        pe.wait_ge(nT_ready, g)
                    for t in range(4):
                        pe.wait_ge(n1_ready, 4 * g + t + 1)
                        last = nc.tensor.transpose(nT_ps[:, t * P:(t + 1) * P], n1[:, 4 * g + t], k.ident[:])
                    last.then_inc(nT_done, 1)

                chunk_T(0)
                pe.wait_ge(w_swapped, 8)
                for u in range(NU):
                    x, g = 1 - u % 2, u // 2
                    if u % 2 == 0:
                        if g + 1 < NCH:
                            chunk_T(g + 1)
                        pe.wait_ge(nT_ready, g + 1)
                        if g:
                            pe.wait_ge(v_used, g)
                        for t in range(4):
                            last = nc.tensor.matmul(v_ps[:, t], n1T[:, (4 * g + t) * P:(4 * g + t + 1) * P], w[:, 2],
                                                    start=True, stop=True)
                        last.then_inc(v_done, 1)
                    if u >= 2:
                        pe.wait_ge(qk_used, u - 1)
                    nc.tensor.matmul(q_ps[x][0][:], wp[:, x], n1T[:, g * W4:(g + 1) * W4], start=True, stop=True)
                    nc.tensor.matmul(q_ps[x][1][:], wp[:, 2 + x], n1T[:, g * W4:(g + 1) * W4], start=True,
                                     stop=True).then_inc(qk_done, 1)


def maxima(nc, k, a, s):
    with ExitStack() as ctx:
        sb = lambda name, shape, dt=F32: ctx.enter_context(nc.sbuf_tensor(f"x_{name}", shape, dt))
        sem = lambda name: k.phase_sem(f"x_{name}")
        minus_max = sb("minus_max", [P, NT, NH])
        mT = sb("mT", [NH, T])
        mrest = sb("mrest", [NH, T])
        mpart = sb("mpart", [NH, PARTS, T], BF16)
        NG = NH // QK_G
        scored, reduced = sem("scored"), sem("reduced")
        mT_done, mT_ready = sem("mT_done"), sem("mT_ready")
        hi, rest1, mid, low, out_done, in_done = (sem("hi"), sem("rest1"), sem("mid"), sem("low"), sem("out_done"),
                                                 sem("in_done"))
        m_dram = nc.dram_tensor("m_parts", [PARTS, NH, T], BF16, kind="Internal").ap()

        with ExitStack() as psctx:
            sc_ps = [psctx.enter_context(nc.psum_tensor(f"x_sc_ps{g}", [P, QK_G, 2 * P], F32)) for g in range(NG)]
            with nc.Block() as block:
                @block.tensor
                def _(pe):
                    pe.wait_ge(s.mask_set, 3)
                    pe.wait_ge(s.ident16_ready, 1)

                    def scores(i, first):
                        keys = P if first else 2 * P
                        for g in range(NG):
                            if not first:
                                pe.wait_ge(reduced, i * NG + g - NG + 1)
                            for b in range(QK_G // 2):
                                h = g * QK_G + 2 * b
                                bank = sc_ps[g][:, 2 * b:2 * b + 2, 2 * P - keys:]
                                nc.tensor.matmul(bank, s.ident16[:], s.mask[:, :, 2 * P - keys:],
                                                 start=True, stop=False)
                                for j in range(2):
                                    q = s.q_stack[:, h // 2, bass.ds(i * P, P)]
                                    kk = s.k_stack[:, h + j, bass.ds(i * P - (keys - P), keys)]
                                    last = nc.tensor.matmul(bank[:, j], q, kk, start=False, stop=(j == 1))
                            last.then_inc(scored, 1)

                    scores(0, True)
                    with pe.Fori(1, NT) as i:
                        scores(i, False)

                @block.vector
                def _(dve):
                    def reduce(i, first):
                        for g in range(NG):
                            dve.wait_ge(scored, i * NG + g + 1)
                            src = sc_ps[g][:, :, P:] if first else sc_ps[g][:]
                            dst = minus_max[:, bass.ds(i, 1), g * QK_G:(g + 1) * QK_G]
                            nc.vector.tensor_reduce(dst, src, AX.X, ALU.max, negate=True).then_inc(reduced, 1)

                    reduce(0, True)
                    with dve.Fori(1, NT) as i:
                        reduce(i, False)
        mT_ps = [ctx.enter_context(nc.psum_tensor(f"x_mT_ps{g}", [NH, 4 * P], F32)) for g in range(NT // 4)]
        with nc.Block() as block:
            @block.tensor
            def _(pe):
                for t in range(NT):
                    last = nc.tensor.transpose(mT_ps[t // 4][:, (t % 4) * P:(t % 4 + 1) * P], minus_max[:, t],
                                               k.ident[:])
                    if t % 4 == 3:
                        last.then_inc(mT_done, 1)

            @block.vector
            def _(dve):
                for g in range(NT // 4):
                    dve.wait_ge(mT_done, g + 1)
                    last = nc.vector.tensor_copy(mT[:, g * 4 * P:(g + 1) * 4 * P], mT_ps[g][:])
                last.then_inc(mT_ready, 1)
                dve.wait_ge(mT_ready, 1)
                nc.vector.tensor_copy(mpart[:, 0], mT[:]).then_inc(hi, 1)
                dve.wait_ge(hi, 1)
                nc.vector.tensor_tensor(mrest[:], mT[:], mpart[:, 0], ALU.subtract).then_inc(rest1, 1)
                dve.wait_ge(rest1, 1)
                nc.vector.tensor_copy(mpart[:, 1], mrest[:]).then_inc(mid, 1)
                dve.wait_ge(mid, 1)
                nc.vector.tensor_tensor(mpart[:, 2], mrest[:], mpart[:, 1], ALU.subtract).then_inc(low, 1)

            @block.sync
            def _(sp):
                sp.wait_ge(low, 1)
                sp.dma_start(m_dram.rearrange("r h t -> h r t"), mpart[:]).then_inc(out_done, 16)
                sp.wait_ge(out_done, 16)
                for odd in range(2):
                    row = 64 * odd + M_ROW
                    sp.dma_start(s.q_stack[row:row + PARTS, :, 0:T],
                                 m_dram.rearrange("r (p two) t -> two r p t", two=2)[odd]).then_inc(in_done, 16)
                sp.wait_ge(in_done, 32)


def attend(nc, k, a, s):
    with ExitStack() as ctx:
        sb = lambda name, shape, dt=F32: ctx.enter_context(nc.sbuf_tensor(f"p_{name}", shape, dt))
        ps = lambda name, shape: ctx.enter_context(nc.psum_tensor(f"p_{name}", shape, F32))
        sem = lambda name: k.phase_sem(f"p_{name}")
        NG = NH // QK_G
        assert NG == 4
        prob_bufs = [sb(f"prob{g}", [P, QK_G, 2 * P]) for g in range(3)]
        prob = [prob_bufs[0], prob_bufs[1], prob_bufs[2], prob_bufs[1]]
        hi = [sb(f"hi{u}", [P, NH, 2 * P], F16) for u in range(2)]
        low = [sb(f"low{u}", [P, NH, 2 * P], F16) for u in range(2)]
        total = sb("total", [P, NH, HD])
        inv = sb("inv", [P, NH])
        sc_ps = [ps(f"sc_ps{g}", [P, QK_G, 2 * P]) for g in range(2)]
        o_ps = [ps(f"o_ps{u}", [P, NH, VW]) for u in range(2)]
        scored, exp_done, out_done = sem("scored"), sem("exp_done"), sem("out_done")
        hi_act, hi_dve = sem("hi_act"), sem("hi_dve")
        low_pool, low_dve = sem("low_pool"), sem("low_dve")
        total_ready, inv_ready, att_ready = sem("total_ready"), sem("inv_ready"), sem("att_ready")
        cleared = sem("cleared")

        def head_slice(g):
            return slice(g * QK_G, (g + 1) * QK_G)

        def all_rounds(eng, one_round):
            for j in range(2):
                one_round(j, j, first=(j == 0), second=(j == 1))
            with eng.Fori(1, NT // 2) as jj:
                for u in range(2):
                    one_round(2 * jj + u, u, first=False, second=False)

        with nc.Block() as block:
            @block.tensor
            def _(pe):
                def values(j, u, g):
                    if g == 0:
                        pe.wait_ge(low_pool, j + 1)
                    else:
                        pe.wait_ge(low_dve, j * 3 + g)
                    for h in range(g * QK_G, (g + 1) * QK_G):
                        terms = [(x[w_][:, h, c * P:(c + 1) * P], tile)
                                 for w_, c, tile in ((1 - u, 1, j), (u, 0, j + 1)) for x in (hi, low)]
                        for m, (p_, tile) in enumerate(terms):
                            last = nc.tensor.matmul(o_ps[u][:, h], p_, s.v_parts[:, bass.ds(tile, 1), h],
                                                    start=(m == 0), stop=(m == 3))
                    last.then_inc(out_done, 1)

                def one_round(j, u, first, second):
                    for g in range(NG):
                        if g >= 2 or not first:
                            pe.wait_ge(exp_done, j * NG + g - 1)
                        for b in range(QK_G // 2):
                            h = g * QK_G + 2 * b
                            bank = sc_ps[g % 2][:, 2 * b:2 * b + 2]
                            nc.tensor.matmul(bank, s.ident16[:], s.mask[:], start=True, stop=False)
                            for x in range(2):
                                last = nc.tensor.matmul(
                                    bank[:, x], s.k_stack[:, h + x, bass.ds(j * P, P)],
                                    s.q_stack[:, h // 2, bass.ds(j * P, 2 * P)], start=False, stop=(x == 1))
                        last.then_inc(scored, 1)
                        if not first:
                            if g == 0 and not second:
                                pe.wait_ge(att_ready, j - 1)
                            values(j - 1, 1 - u, g)

                pe.wait_ge(cleared, 2)
                pe.sem_inc(att_ready, 1)
                all_rounds(pe, one_round)
                pe.wait_ge(att_ready, NT - 1)
                for g in range(NG):
                    values(NT - 1, 1, g)

            @block.scalar
            def _(act):
                def exp(j, g, first):
                    act.wait_ge(scored, j * NG + g + 1)
                    if g == 0 and not first:
                        act.wait_ge(low_pool, j)
                    if g == 1 and not first:
                        act.wait_ge(low_dve, j * 3)
                    if g == 3:
                        act.wait_ge(low_dve, j * 3 + 1)
                    nc.scalar.activation(prob[g][:], sc_ps[g % 2][:], ACT.Exp).then_inc(exp_done, 1)

                def round_off(j, u, g, first):
                    act.wait_ge(exp_done, j * NG + g + 1)
                    if not first:
                        act.wait_ge(out_done, j * NG + g - 3)
                    nc.scalar.copy(hi[u][:, head_slice(g)], prob[g][:]).then_inc(hi_act, 1)

                def one_round(j, u, first, second):
                    exp(j, 0, first)
                    exp(j, 1, first)
                    round_off(j, u, 0, first)
                    exp(j, 2, first)
                    round_off(j, u, 2, first)
                    exp(j, 3, first)

                act.preload_act_table(ACT.Exp)
                all_rounds(act, one_round)

            @block.gpsimd
            def _(pool):
                def one_round(j, u, first, second):
                    pool.wait_ge(hi_act, j * 2 + 1)
                    nc.gpsimd.tensor_tensor(low[u][:, head_slice(0)], prob[0][:], hi[u][:, head_slice(0)],
                                            ALU.subtract).then_inc(low_pool, 1)

                all_rounds(pool, one_round)

            @block.vector
            def _(dve):
                def round_off(j, u, g, first):
                    dve.wait_ge(exp_done, j * NG + g + 1)
                    if not first:
                        dve.wait_ge(out_done, j * NG + g - 3)
                    nc.vector.tensor_copy(hi[u][:, head_slice(g)], prob[g][:]).then_inc(hi_dve, 1)

                def remainder(j, u, g):
                    if g == 2:
                        dve.wait_ge(hi_act, j * 2 + 2)
                    else:
                        dve.wait_ge(hi_dve, j * 2 + (g + 1) // 2)
                    nc.vector.tensor_tensor(low[u][:, head_slice(g)], prob[g][:], hi[u][:, head_slice(g)],
                                            ALU.subtract).then_inc(low_dve, 1)

                def normalize(j, u):
                    dve.wait_ge(out_done, j * NG + NG)
                    sums = o_ps[u][:, :, 0:PARTS * HD].rearrange("p h (r d) -> p h d r", r=PARTS)
                    nc.vector.tensor_reduce(total[:], sums, AX.X, ALU.add).then_inc(total_ready, 1)
                    nc.vector.reciprocal(inv[:], o_ps[u][:, :, PARTS * HD]).then_inc(inv_ready, 1)
                    dve.wait_ge(total_ready, j + 1)
                    dve.wait_ge(inv_ready, j + 1)
                    nc.vector.tensor_tensor(
                        s.att[:, bass.ds(j, 1)].rearrange("p t (h d) -> p (t h) d", h=NH), total[:],
                        bc(inv[:], 2, HD), ALU.mult).then_inc(att_ready, 1)

                def one_round(j, u, first, second):
                    round_off(j, u, 1, first)
                    remainder(j, u, 1)
                    if not first and not second:
                        normalize(j - 2, u)
                    remainder(j, u, 2)
                    round_off(j, u, 3, first)
                    remainder(j, u, 3)

                nc.vector.memset(hi[1][:].bitcast(F32), 0.0).then_inc(cleared, 1)
                nc.vector.memset(low[1][:].bitcast(F32), 0.0).then_inc(cleared, 1)
                all_rounds(dve, one_round)
                normalize(NT - 2, 0)
                dve.wait_ge(att_ready, NT)
                normalize(NT - 1, 1)


def finish_attention(nc, k, a, s):
    with ExitStack() as ctx:
        sb = lambda name, shape, dt=F32: ctx.enter_context(nc.sbuf_tensor(f"f_{name}", shape, dt))
        ps = lambda name, shape: ctx.enter_context(nc.psum_tensor(f"f_{name}", shape, F32))
        sem = lambda name: k.phase_sem(f"f_{name}")
        W4 = 4 * P
        NCH = NT // 4
        attT = sb("attT", [P, W4])
        st = sb("st", [P, NT, 6])
        mv = sb("mv", [P, NT, 2])
        var_eps = sb("var_eps", [P, NT])
        rstd = sb("rstd", [P, NT])
        n2 = sb("n2", [P, 4, C])
        n2T = sb("n2T", [P, W4])
        gate = sb("gate", [P, 3, W4])
        hid = sb("hid", [P, 3, W4])
        T_ps = ps("T_ps", [P, W4])
        w_ps = ps("w_ps", [P, 4, C])
        u1_ps = [ps(f"u1_ps{x}", [P, W4]) for x in range(2)]
        u3_ps = [ps(f"u3_ps{x}", [P, W4]) for x in range(2)]
        aT_done, aT_ready, wo_done, h_ready = sem("aT_done"), sem("aT_ready"), sem("wo_done"), sem("h_ready")
        var_ready, rstd_ready, n2_ready = sem("var_ready"), sem("rstd_ready"), sem("n2_ready")
        nT_done, nT_ready, u_done, silu_done, hid_ready = (sem("nT_done"), sem("nT_ready"), sem("u_done"),
                                                         sem("silu_done"), sem("hid_ready"))
        y_done, x_ready = sem("y_done"), sem("x_ready")
        step = sem("step")

        with nc.Block() as block:
            @block.tensor
            def _(pe):
                pe.wait_ge(s.tail_loaded, 16 * 6)
                for g in range(NCH):
                    if g:
                        pe.wait_ge(aT_ready, g)
                    for t in range(4):
                        last = nc.tensor.transpose(T_ps[:, t * P:(t + 1) * P], s.att[:, 4 * g + t], k.ident[:])
                    last.then_inc(aT_done, 1)
                    pe.wait_ge(aT_ready, g + 1)
                    if g:
                        pe.wait_ge(h_ready, g)
                    for t in range(4):
                        last = nc.tensor.matmul(w_ps[:, t], attT[:, t * P:(t + 1) * P], s.wo[:], start=True, stop=True)
                    last.then_inc(wo_done, 1)
                pe.wait_ge(h_ready, NCH)
                for g in range(NCH):
                    pe.wait_ge(n2_ready, g + 1)
                    for t in range(4):
                        last = nc.tensor.transpose(T_ps[:, t * P:(t + 1) * P], n2[:, t], k.ident[:])
                    last.then_inc(nT_done, 1)
                    pe.wait_ge(nT_ready, g + 1)
                    for c, (at, size) in enumerate(HIDC):
                        v = 3 * g + c
                        if v >= 2:
                            pe.wait_ge(hid_ready, v - 1)
                        nc.tensor.matmul(u1_ps[v % 2][0:size], s.w1[:, at:at + size], n2T[:], start=True, stop=True)
                        nc.tensor.matmul(u3_ps[v % 2][0:size], s.w3[:, at:at + size], n2T[:], start=True,
                                         stop=True).then_inc(u_done, 1)
                    pe.wait_ge(hid_ready, 3 * g + 3)
                    if g:
                        pe.wait_ge(x_ready, g)
                    for t in range(4):
                        for c, (at, size) in enumerate(HIDC):
                            last = nc.tensor.matmul(w_ps[:, t], hid[0:size, c, t * P:(t + 1) * P], s.w2[0:size, c],
                                                    start=(c == 0), stop=(c == 2))
                    last.then_inc(y_done, 1)

            @block.scalar
            def _(act):
                for g in range(NCH):
                    act.wait_ge(aT_done, g + 1)
                    if g:
                        act.wait_ge(wo_done, g)
                    nc.scalar.copy(attT[:], T_ps[:]).then_inc(aT_ready, 1)
                for g in range(NCH):
                    act.wait_ge(nT_done, g + 1)
                    nc.scalar.activation(n2T[:], T_ps[:], ACT.Identity, bias=k.ln_vec[:, 3:4],
                                         scale=k.ln_vec[:, 2:3]).then_inc(nT_ready, 1)
                    for c, (at, size) in enumerate(HIDC):
                        act.wait_ge(u_done, 3 * g + c + 1)
                        if g:
                            act.wait_ge(hid_ready, 3 * g + c - 2)
                        nc.scalar.activation(gate[0:size, c], u1_ps[(3 * g + c) % 2][0:size],
                                             ACT.Silu).then_inc(silu_done, 1)

            @block.gpsimd
            def _(pool):
                pool.wait_ge(var_ready, 1)
                nc.gpsimd.tensor_tensor(rstd[:], var_eps[:], k.minus_half[:], ALU.pow).then_inc(rstd_ready, 1)

            @block.vector
            def _(dve):
                done = [0]

                def link(ins):
                    done[0] += 1
                    ins.then_inc(step, 1)
                    dve.wait_ge(step, done[0])

                for g in range(NCH):
                    dve.wait_ge(wo_done, g + 1)
                    part = slice(4 * g, 4 * g + 4)
                    last = nc.vector.tensor_tensor(s.res[:, part], s.res[:, part], w_ps[:], ALU.add)
                    last.then_inc(h_ready, 1)
                dve.wait_ge(h_ready, NCH)
                layernorm_stats(nc.vector, link, s.res, st, mv, var_eps, var_ready)
                link(nc.vector.tensor_tensor(k.xs[:], k.xs[:], s.res[:], ALU.add))
                dve.wait_ge(rstd_ready, 1)
                for g in range(NCH):
                    if g:
                        dve.wait_ge(nT_done, g)
                    for t in range(4):
                        last = nc.vector.tensor_scalar(n2[:, t], s.res[:, 4 * g + t], mv[:, 4 * g + t, 0:1],
                                                       rstd[:, 4 * g + t:4 * g + t + 1], ALU.subtract, ALU.mult)
                    last.then_inc(n2_ready, 1)
                    for c, (at, size) in enumerate(HIDC):
                        dve.wait_ge(silu_done, 3 * g + c + 1)
                        if g:
                            dve.wait_ge(y_done, g)
                        nc.vector.tensor_tensor(hid[0:size, c], gate[0:size, c], u3_ps[(3 * g + c) % 2][0:size],
                                                ALU.mult).then_inc(hid_ready, 1)
                    dve.wait_ge(y_done, g + 1)
                    part = slice(4 * g, 4 * g + 4)
                    nc.vector.tensor_tensor(k.xs[:, part], k.xs[:, part], w_ps[:], ALU.add).then_inc(x_ready, 1)


def attention(nc, k, a):
    with ExitStack() as ctx:
        sb = lambda name, shape, dt=F32: ctx.enter_context(nc.sbuf_tensor(f"s_{name}", shape, dt))
        s = Names()
        s.res = sb("res", [P, NT, C])
        s.wo = sb("wo", [P, C])
        s.w1 = sb("w1", [P, HID])
        s.w3 = sb("w3", [P, HID])
        s.w2 = sb("w2", [P, 3, C])
        k.ln_vec = sb("ln_vec", [P, 4])
        s.tail_loaded, s.mask_set = k.sem("tail_loaded"), k.sem("mask_set")
        s.ident16_ready, s.prob_free = k.sem("ident16_ready"), k.sem("prob_free")
        with ExitStack() as stacks:
            sb2 = lambda name, shape, dt=F32: stacks.enter_context(nc.sbuf_tensor(f"s_{name}", shape, dt))
            s.att = None
            s.q_stack = sb2("q_stack", [P, PAIRS, T + P], BF16)
            s.k_stack = sb2("k_stack", [P, NH, T], BF16)
            s.v_parts = sb2("v_parts", [P, NT + 1, NH, VW], BF16)
            s.mask = sb2("mask", [P, 2, 2 * P], BF16)
            s.ident16 = sb2("ident16", [P, P], BF16)
            project(nc, k, a, s)
            maxima(nc, k, a, s)
            s.att = sb2("att", [P, NT, C])
            attend(nc, k, a, s)
            finish_attention(nc, k, a, s)

def phase_semaphores(nc, k, ctx):
    k.phase_sems = []

    def phase_sem(name):
        k.phase_sems.append(ctx.enter_context(nc.semaphore(name)))
        return k.phase_sems[-1]

    k.phase_sem = phase_sem


def clear_phase_semaphores(nc, k):
    with nc.Block() as block:
        @block.gpsimd
        def _(pool):
            for s in k.phase_sems:
                pool.sem_clear(s)


def macaron(nc, a, out):
    with ExitStack() as ctx:
        k = Names()
        k.sb = lambda name, shape, dt=F32: ctx.enter_context(nc.sbuf_tensor(name, shape, dt))
        k.sem = lambda name: ctx.enter_context(nc.semaphore(name))
        k.x_rows = nc.dram_tensor("x_rows", [2 * T, C], F32, kind="Internal").ap()
        k.y_rows = nc.dram_tensor("y_rows", [ROWS_OUT, C], F32, kind="Internal").ap()
        k.xs = k.sb("xs", [P, NT, C])
        constants(nc, k)
        moe_tensors(nc, k)
        with ExitStack() as first:
            phase_semaphores(nc, k, first)
            moe(nc, k, a, 0)
            attention(nc, k, a)
            clear_phase_semaphores(nc, k)
        with ExitStack() as second:
            phase_semaphores(nc, k, second)
            moe(nc, k, a, 1, out)



_INS = ["L0_attn_x", "L0_attn_wq", "L0_attn_wk", "L0_attn_wv", "L0_attn_wo", "L0_attn_w1", "L0_attn_w2",
        "L0_attn_w3", "L0_attn_ln1_g", "L0_attn_ln1_b", "L0_attn_ln2_g", "L0_attn_ln2_b", "L0_ffn_gate_W",
        "L0_ffn_mlp_W1", "L0_ffn_mlp_b1", "L0_ffn_mlp_W2", "L0_ffn_mlp_b2", "L0_ffn_kan_ln_g0",
        "L0_ffn_kan_ln_b0", "L0_ffn_kan_sl_W0", "L0_ffn_kan_sl_b0", "L0_ffn_kan_ln_g1", "L0_ffn_kan_ln_b1",
        "L0_ffn_kan_sl_W1", "L0_ffn_kan_sl_b1"]


def kernel(**inputs):
    import concourse.bacc as bacc
    from concourse.bass_utils import run_bass_kernel_spmd

    nc = bacc.Bacc("TRN2", target_bir_lowering=False, num_devices=1)
    arrays, a = {}, Names()
    for name in _INS:
        data = np.ascontiguousarray(inputs[name])
        arrays[f"in_{name}_dram"] = data
        handle = nc.dram_tensor(f"in_{name}_dram", data.shape, mybir.dt.from_np(data.dtype), kind="ExternalInput")
        a.__dict__[name.removeprefix("L0_attn_").removeprefix("L0_ffn_")] = handle.ap()
    by_channel = [np.asarray(inputs[f"L0_ffn_kan_ln_{v}"]).reshape(E2, -1, P).transpose(2, 1, 0)
                  for v in ("g0", "b0", "g1", "b1")]
    arrays["in_kan_ln_dram"] = np.ascontiguousarray(np.concatenate(by_channel, axis=1))
    a.kan_ln = nc.dram_tensor("in_kan_ln_dram", arrays["in_kan_ln_dram"].shape, F32, kind="ExternalInput").ap()
    arrays["in_attn_ln_dram"] = np.ascontiguousarray(np.stack(
        [np.asarray(inputs[f"L0_attn_{v}"]) for v in ("ln1_g", "ln1_b", "ln2_g", "ln2_b")], axis=1))
    a.attn_ln = nc.dram_tensor("in_attn_ln_dram", (C, 4), F32, kind="ExternalInput").ap()
    freqs = 1.0 / np.float32(10000.0) ** (np.arange(0, HD, 2, dtype=np.float32) / np.float32(HD))
    angle = np.outer(np.arange(T, dtype=np.float32), freqs.astype(np.float32)).astype(np.float64).T
    cos, sin = np.cos(angle), np.sin(angle)
    for name, table in (("cos", np.stack([cos, cos], 1)), ("sin", np.stack([-sin, sin], 1))):
        by_channel = table.reshape(HD, T).astype(np.float32)
        arrays[f"in_{name}_dram"] = np.ascontiguousarray(np.tile(np.repeat(by_channel, PAIRS, axis=0), (2, 1)))
        a.__dict__[name] = nc.dram_tensor(f"in_{name}_dram", (C, T), F32, kind="ExternalInput").ap()
    out = nc.dram_tensor("out_0_dram", (1, T, C), F32, kind="ExternalOutput").ap()
    macaron(nc, a, out)
    r = run_bass_kernel_spmd(nc, [arrays], core_ids=[0])
    return r.results[0]["out_0_dram"]
```

```python
from contextlib import ExitStack

import numpy as np

import concourse.bass as bass
from concourse import mybir

ALU = mybir.AluOpType
ACT = mybir.ActivationFunctionType
AX = mybir.AxisListType
F32 = mybir.dt.float32
BF16 = mybir.dt.bfloat16
F16 = mybir.dt.float16
I32 = mybir.dt.int32
U32 = mybir.dt.uint32

P = 128
T = 2048
NT = T // P
C = 128
NE = 8
E2 = NE // 2
TOPK = 2
F = 512
FC = F // P
F2 = F // 2
F2C = F2 // P
G = 8
GRID = np.linspace(-1.2, 0.2, G).astype(np.float32)
EPS = 1e-5
MAXB = TOPK * T // P + NE - 1
NS = MAXB + 7
assert NS % 2 == 0
LEAD = 4
NQ = NS + LEAD
ROWS_OUT = TOPK * T + NS * P
BOUND = "both loops together have at most MAXB blocks"


class Names:
    pass


def bc(ap, axis, n):
    a = ap.unsqueeze(axis)
    shape = list(a.shape)
    shape[axis] = n
    return a.to_broadcast(shape)


def constants(nc, k):
    sb, sem = k.sb, k.sem
    k.ident = sb("ident", [P, P])
    k.ones = sb("ones", [P, P])
    k.later = sb("later", [P, P])
    k.earlier = sb("earlier", [P, NE, NE])
    k.minus_half = sb("minus_half", [P, NT])
    k.slot_no = sb("slot_no", [P, NS])
    k.lane_no = sb("lane_no", [P, P])
    k.one_up = sb("one_up", [P, 1])
    k.pair_no = sb("pair_no", [P, TOPK * NT])
    k.spare_row = sb("spare_row", [P, NS])
    k.scan_ones = sb("scan_ones", [P, NT])
    k.const_made = sem("const_made")
    k.const_set = sem("const_set")
    k.N_CONST = 11




def make_constants(pool, k):
    pool.memset(k.ident[:], 0.0).then_inc(k.const_set, 1)
    pool.memset(k.ones[:], 1.0).then_inc(k.const_made, 1)
    pool.memset(k.later[:], 1.0).then_inc(k.const_set, 1)
    pool.memset(k.earlier[:], 1.0).then_inc(k.const_set, 1)
    pool.memset(k.minus_half[:], -0.5).then_inc(k.const_made, 1)
    pool.memset(k.scan_ones[:], 1.0).then_inc(k.const_made, 1)
    for out, pattern, base, by_partition in (
            (k.lane_no, [[1, P]], 0, 0), (k.one_up, [[0, 1]], 1, 1), (k.pair_no, [[1, TOPK * NT]], 0, 0),
            (k.spare_row, [[P, NS]], TOPK * T + 1, 1)):
        pool.iota(out[:], pattern=pattern, base=base, channel_multiplier=by_partition,
                  allow_small_or_imprecise_dtypes=True).then_inc(k.const_made, 1)
    pool.iota(k.slot_no[:], pattern=[[1, NS]], base=-1, channel_multiplier=0,
              allow_small_or_imprecise_dtypes=True).then_inc(k.const_made, 1)
    pool.wait_ge(k.const_set, 3)
    pool.affine_select(out=k.ident[:], in_=k.ident[:], compare_op=ALU.not_equal, fill=1.0, base=0,
                       pattern=[[-1, P]], channel_multiplier=1).then_inc(k.const_made, 1)
    pool.affine_select(out=k.later[:], in_=k.later[:], compare_op=ALU.is_gt, fill=0.0, base=0,
                       pattern=[[1, P]], channel_multiplier=-1).then_inc(k.const_made, 1)
    pool.affine_select(out=k.earlier[:], in_=k.earlier[:], compare_op=ALU.is_gt, fill=0.0, base=0,
                       pattern=[[1, NE], [-1, NE]], channel_multiplier=0).then_inc(k.const_made, 1)


def moe_tensors(nc, k):
    sb = k.sb
    k.gate_w = sb("gate_w", [P, NE])
    k.kan_b0 = sb("kan_b0", [P, E2, F2])
    k.kan_b1 = sb("kan_b1", [P, E2, C])
    k.kan_ln = sb("kan_ln", [P, 2 * (1 + F2C), E2])
    k.kan_g0, k.kan_c0 = k.kan_ln[:, 0], k.kan_ln[:, 1]
    k.kan_g1, k.kan_c1 = k.kan_ln[:, 2:2 + F2C], k.kan_ln[:, 2 + F2C:]
    k.weight = sb("weight", [P, TOPK, NT])
    k.rows_of = sb("rows_of", [P, NQ, 2], I32)
    k.n_mlp = sb("n_mlp", [P, 1], I32)
    k.n_pairs = sb("n_pairs", [P, 2], I32)
    k.experts = sb("experts", [P, 2, NS // 2 - 1, 4], I32)
    k.rows_in_dram = [k.sem(f"rows_in_dram_{n}") for n in range(2)]
    k.x_loaded = k.sem("x_loaded")
    k.small_loaded = k.sem("small_loaded")
    k.mlp_loaded = [k.sem(f"mlp_loaded_{n}") for n in range(2)]
    k.kan_loaded = [k.sem(f"kan_loaded{e}_0") for e in range(E2)]
    k.kans_loaded_again = k.sem("kans_loaded_again")
    k.stored_out = k.sem("stored_out")


def moe_weights(nc, k, ctx, n):
    sb = lambda name, shape: ctx.enter_context(nc.sbuf_tensor(f"{name}_{n}", shape, F32))
    k.kan_w0 = sb("kan_w0", [P, E2, G, F2])
    k.kan_w1 = sb("kan_w1", [P, E2, F2C, G, C])
    k.mlp_w1 = sb("mlp_w1", [P, E2, F])
    k.mlp_w2 = sb("mlp_w2", [P, E2, FC, C])
    k.mlp_b1 = sb("mlp_b1", [P, E2, F])
    k.mlp_b2 = sb("mlp_b2", [P, E2, C])


def load_shared(q, k, a):
    q.dma_start(k.gate_w[:], a.gate_W).then_inc(k.small_loaded, 16)
    q.dma_start(k.kan_ln[:], a.kan_ln).then_inc(k.small_loaded, 16)
    q.dma_start(k.kan_b0[:], a.kan_sl_b0.partition_broadcast(P)).then_inc(k.small_loaded, 16)
    q.dma_start(k.kan_b1[:], a.kan_sl_b1.partition_broadcast(P)).then_inc(k.small_loaded, 16)


N_SHARED = 4


def load_mlps(q, k, a, n):
    q.dma_start(k.mlp_w1[:], a.mlp_W1.rearrange("e p f -> p e f")).then_inc(k.mlp_loaded[n], 16)
    for e in range(E2):
        q.dma_start(k.mlp_w2[:, e], a.mlp_W2[e].rearrange("(c p) h -> p c h", p=P)).then_inc(k.mlp_loaded[n], 16)
    q.dma_start(k.mlp_b1[:], a.mlp_b1.partition_broadcast(P)).then_inc(k.mlp_loaded[n], 16)
    q.dma_start(k.mlp_b2[:], a.mlp_b2.partition_broadcast(P)).then_inc(k.mlp_loaded[n], 16)


def load_kan(q, k, a, n, e):
    q.dma_start(k.kan_w0[:, e], a.kan_sl_W0[e].rearrange("(p g) o -> p g o", g=G)
                ).then_inc(k.kans_loaded_again if n else k.kan_loaded[e], 16)
    q.dma_start(k.kan_w1[:, e], a.kan_sl_W1[e].rearrange("(c p g) o -> p c g o", p=P, g=G)
                ).then_inc(k.kans_loaded_again if n else k.kan_loaded[e], 16)


N_MLP = E2 + 3
EARLY = 1
FOLDS = (G.bit_length() - 1) + ((F2C * G).bit_length() - 1)


class ChunkStats:

    def __init__(self, nc, k, sem, name):
        self.nc, self.k = nc, k
        self.var_steps = sem(f"{name}_var_steps")
        self.rstd_ready = sem(f"{name}_rstd_ready")

    def on_vector(self, dve, g):
        k, nc, part = self.k, self.nc, slice(4 * g, 4 * g + 4)
        for t in range(4 * g, 4 * g + 4):
            last = nc.vector.bn_stats(k.st[:, t], k.xs[:, t])
        last.then_inc(self.var_steps, 1)
        dve.wait_ge(self.var_steps, 3 * g + 1)
        for t in range(4 * g, 4 * g + 4):
            last = nc.vector.bn_aggr(k.mv[:, t], k.st[:, t])
        last.then_inc(self.var_steps, 1)
        dve.wait_ge(self.var_steps, 3 * g + 2)
        nc.vector.tensor_scalar(k.var_eps[:, part], k.mv[:, part, 1], EPS, None, ALU.add).then_inc(self.var_steps, 1)

    def on_gpsimd(self, pool, g):
        k, part = self.k, slice(4 * g, 4 * g + 4)
        pool.wait_ge(self.var_steps, 3 * g + 3)
        self.nc.gpsimd.tensor_tensor(k.rstd[:, part], k.var_eps[:, part], k.minus_half[:, part],
                                     ALU.pow).then_inc(self.rstd_ready, 1)


def route(nc, k, a, n):
    with ExitStack() as ctx:
        sb = lambda name, shape, dt=F32: ctx.enter_context(nc.sbuf_tensor(f"{name}_{n}", shape, dt))
        ps = lambda name, shape: ctx.enter_context(nc.psum_tensor(f"{name}_{n}", shape, F32))
        sem = lambda name: k.moe_sem(name)
        xn = sb("xn", [P, NT, C])
        xnT = sb("xnT", [P, NT * P])
        xh = sb("xh", [P, NT, C])
        var_eps2 = sb("var_eps2", [P, NT])
        rstd2 = sb("rstd2", [P, NT])
        rstd_sq = sb("rstd_sq", [P, NT])
        logit = sb("logit", [P, NT, NE])
        top = sb("top", [P, NT])
        below = sb("below", [P, NT, NE])
        prob = sb("prob", [P, NT, NE])
        above = sb("above", [P, NT, NE, NE])
        equal = sb("equal", [P, NT, NE, NE])
        place = sb("place", [P, NT, NE])
        chosen = sb("chosen", [P, NT, NE])
        pick = sb("pick", [P, TOPK, NT, NE])
        weighed = sb("weighed", [P, NT, NE])
        den = sb("den", [P, NT])
        tile_sum = sb("tile_sum", [P, NT, NE])
        up_to = sb("up_to", [P, NT, NE])
        blocks_i = sb("blocks_i", [P, NE], I32)
        blocks = sb("blocks", [P, NE])
        blocks_up_to = sb("blocks_up_to", [P, NE])
        base = sb("base", [P, NE])
        pos = sb("pos", [P, NT, NE])
        tmp = sb("tmp", [P, TOPK, NT, NE])
        at = sb("at", [P, TOPK, NT])
        is_kan = sb("is_kan", [P, TOPK, NT])
        at_i = sb("at_i", [P, TOPK, NT], I32)
        row_i = sb("row_i", [P, TOPK, NT], I32)
        slot_i = sb("slot_i", [P, TOPK, NT], I32)
        row_f = sb("row_f", [P, TOPK, NT])
        slot_f = sb("slot_f", [P, TOPK, NT])
        in_row = sb("in_row", [P, TOPK * NT, P], F16)
        in_slot = sb("in_slot", [P, TOPK * NT, NS], F16)
        numbers = sb("numbers", [P, TOPK * NT, 2, NS], F16)
        found = sb("found", [P, 2, NS])
        code = sb("code", [P, NS])
        code_i = sb("code_i", [P, NS], I32)
        token_i = sb("token_i", [P, NS], I32)
        token = sb("token", [P, NS])
        kan_rows = sb("kan_rows", [P, NS])
        spare = sb("spare", [P, NS])
        pairs_i = sb("pairs_i", [P, 2], I32)
        tab = sb("tab", [P, 2, NS])
        xT_ps = [ps(f"xT_ps{i}", [P, 4 * P]) for i in range(2)]
        logit_ps = ps("logit_ps", [P, NT, NE])
        cum_ps = ps("cum_ps", [P, NT, NE])
        sum_ps = ps("sum_ps", [P, NT, NE])
        found_ps = ps("found_ps", [P, 2, NS])
        fold0 = sb("fold0", [P, G // 2, F2])
        fold1 = sb("fold1", [P, F2C * G // 2, C])

        var_ready, rstd_ready, xn_ready = sem("var_ready"), sem("rstd_ready"), sem("xn_ready")
        xT_ready, xT_copied = sem("xT_ready"), sem("xT_copied")
        logits_ready, below_ready, prob_ready = sem("logits_ready"), sem("below_ready"), sem("prob_ready")
        chosen_ready, counts_ready = sem("chosen_ready"), sem("counts_ready")
        xh_ready = sem("xh_ready")
        numbers_ready, found_ready = sem("numbers_ready"), sem("found_ready")
        in_slot_ready, in_row_ready = sem("in_slot_ready"), sem("in_row_ready")
        summed, sum_added, folded = sem("summed"), sem("sum_added"), sem("folded")
        step = sem("step")

        with nc.Block() as block:
            @block.vector
            def _(dve):
                done = [0]

                def link(ins):
                    done[0] += 1
                    ins.then_inc(step, 1)
                    dve.wait_ge(step, done[0])

                if n == 0:
                    dve.wait_ge(k.x_loaded, 16)
                    for t in range(NT):
                        last = nc.vector.bn_stats(k.st[:, t], k.xs[:, t])
                    link(last)
                    for t in range(NT):
                        last = nc.vector.bn_aggr(k.mv[:, t], k.st[:, t])
                    link(last)
                    nc.vector.tensor_scalar(k.var_eps[:], k.mv[:, :, 1], EPS, None, ALU.add).then_inc(var_ready, 1)
                    dve.wait_ge(rstd_ready, 1)
                link(nc.vector.tensor_tensor(rstd_sq[:], k.rstd[:], k.rstd[:], ALU.mult))
                link(nc.vector.tensor_tensor(var_eps2[:], k.mv[:, :, 1], rstd_sq[:], ALU.mult))
                nc.vector.tensor_scalar(var_eps2[:], var_eps2[:], EPS, None, ALU.add).then_inc(var_ready, 1)
                for t in range(NT):
                    last = nc.vector.tensor_scalar(xn[:, t], k.xs[:, t], k.mv[:, t, 0:1], k.rstd[:, t:t + 1],
                                                   ALU.subtract, ALU.mult)
                    last.then_inc(xn_ready, 1)
                dve.wait_ge(logits_ready, 1)
                link(nc.vector.tensor_copy(logit[:], logit_ps[:]))
                nc.vector.tensor_reduce(top[:], logit[:], AX.X, ALU.max)
                nc.vector.tensor_tensor(above[:], bc(logit[:], 2, NE), bc(logit[:], 3, NE), ALU.is_gt)
                link(nc.vector.tensor_tensor(equal[:], bc(logit[:], 2, NE), bc(logit[:], 3, NE),
                                             ALU.is_equal))
                nc.vector.tensor_tensor(below[:], logit[:], bc(top[:], 2, NE),
                                        ALU.subtract).then_inc(below_ready, 1)
                dve.wait_ge(k.const_made, k.N_CONST)
                link(nc.vector.tensor_tensor(equal[:], equal[:], bc(k.earlier[:], 1, NT), ALU.mult))
                link(nc.vector.tensor_tensor(above[:], above[:], equal[:], ALU.add))
                link(nc.vector.tensor_reduce(place[:], above[:], AX.X, ALU.add))
                nc.vector.tensor_scalar(chosen[:], place[:], float(TOPK), None,
                                        ALU.is_lt).then_inc(chosen_ready, 1)
                nc.vector.tensor_scalar(pick[:, 0], place[:], 0.0, None, ALU.is_equal)
                link(nc.vector.tensor_scalar(pick[:, 1], place[:], 1.0, None, ALU.is_equal))
                nc.vector.tensor_reduce(is_kan[:], pick[:, :, :, E2:NE], AX.X, ALU.add)
                dve.wait_ge(counts_ready, 1)
                link(nc.vector.tensor_copy(tile_sum[:], sum_ps[:]))
                for e in range(NE):
                    last = nc.vector.tensor_tensor_scan(up_to[:, :, e], k.scan_ones[:], tile_sum[:, :, e],
                                                        0.0, ALU.mult, ALU.add)
                link(last)
                link(nc.vector.tensor_scalar(blocks_i[:], up_to[:, NT - 1], float(P - 1), None, ALU.add))
                link(nc.vector.tensor_scalar(blocks_i[:], blocks_i[:], P.bit_length() - 1, None,
                                             ALU.logical_shift_right))
                link(nc.vector.tensor_copy(blocks[:], blocks_i[:]))
                for h in range(2):
                    last = nc.vector.tensor_tensor_scan(blocks_up_to[:, h * E2:(h + 1) * E2],
                                                        k.scan_ones[:, 0:E2], blocks[:, h * E2:(h + 1) * E2],
                                                        0.0, ALU.mult, ALU.add)
                link(last)
                link(nc.vector.tensor_tensor(base[:], blocks_up_to[:], blocks[:], ALU.subtract))
                link(nc.vector.tensor_scalar(base[:, E2:NE], base[:, E2:NE], blocks_up_to[:, E2 - 1:E2],
                                             1.0, ALU.add, ALU.add))
                link(nc.vector.tensor_scalar(base[:], base[:], 1.0, float(P), ALU.add, ALU.mult))
                link(nc.vector.tensor_tensor(up_to[:], up_to[:], tile_sum[:], ALU.subtract))
                link(nc.vector.tensor_tensor(pos[:], cum_ps[:], up_to[:], ALU.add))
                link(nc.vector.tensor_tensor(pos[:], pos[:], bc(base[:], 1, NT), ALU.add))
                link(nc.vector.tensor_tensor(tmp[:], pick[:], bc(pos[:], 1, TOPK), ALU.mult))
                link(nc.vector.tensor_reduce(at[:], tmp[:], AX.X, ALU.add))
                link(nc.vector.tensor_copy(at_i[:], at[:]))
                nc.vector.tensor_scalar(row_i[:], at_i[:], P - 1, None, ALU.bitwise_and)
                link(nc.vector.tensor_scalar(slot_i[:], at_i[:], P.bit_length() - 1, None,
                                             ALU.logical_shift_right))
                nc.vector.tensor_copy(row_f[:], row_i[:])
                link(nc.vector.tensor_copy(slot_f[:], slot_i[:]))
                nc.vector.tensor_tensor(in_slot[:], bc(slot_f[:].rearrange("p j t -> p (j t)"), 2, NS),
                                        bc(k.lane_no[:, 0:NS], 1, TOPK * NT), ALU.is_equal).then_inc(in_slot_ready, 1)
                for j in range(TOPK):
                    nc.vector.tensor_tensor(in_row[:, j * NT:(j + 1) * NT], bc(row_f[:, j], 2, P),
                                            bc(k.lane_no[:], 1, NT), ALU.is_equal).then_inc(in_row_ready, 1)
                nc.vector.tensor_copy(k.n_mlp[:], blocks_up_to[:, E2 - 1:E2])
                last_of = blocks_up_to[:].rearrange("p (h e) -> p h e", h=2)[:, :, E2 - 1]
                link(nc.vector.tensor_scalar(pairs_i[:], last_of, 2.0, None, ALU.add))
                nc.vector.tensor_scalar(k.n_pairs[:], pairs_i[:], 1, None, ALU.logical_shift_right)
                for h in range(2):
                    last = nc.vector.tensor_scalar(tab[:, h], k.slot_no[:], blocks_up_to[:, h * E2:h * E2 + 1],
                                                   None, ALU.is_ge)
                link(last)
                for e in range(1, E2 - 1):
                    for h in range(2):
                        last = nc.vector.scalar_tensor_tensor(
                            tab[:, h], k.slot_no[:], blocks_up_to[:, h * E2 + e:h * E2 + e + 1],
                            tab[:, h], ALU.is_ge, ALU.add)
                    link(last)
                for half in range(2):
                    nc.vector.tensor_copy(k.experts[:, :, :, 2 * half:2 * half + 2],
                                          tab[:, :, 2 * half:2 * half + NS - 2].rearrange(
                                              "p h (r two) -> p h r two", two=2))
                nc.vector.tensor_scalar(kan_rows[:], k.slot_no[:], blocks_up_to[:, E2 - 1:E2], float(T),
                                        ALU.is_ge, ALU.mult)
                dve.wait_ge(found_ready, 1)
                link(nc.vector.tensor_copy(found[:], found_ps[:]))
                nc.vector.scalar_tensor_tensor(spare[:], found[:, 1], 0.0, k.spare_row[:], ALU.is_equal, ALU.mult)
                link(nc.vector.scalar_tensor_tensor(code[:], found[:, 0], float(P), found[:, 1], ALU.mult, ALU.add))
                link(nc.vector.tensor_scalar(code[:], code[:], -1.0, None, ALU.add))
                nc.vector.tensor_tensor(k.rows_of[:, LEAD:NQ, 1], code[:], spare[:], ALU.add)
                link(nc.vector.tensor_copy(code_i[:], code[:]))
                link(nc.vector.tensor_scalar(token_i[:], code_i[:], T - 1, None, ALU.bitwise_and))
                link(nc.vector.tensor_copy(token[:], token_i[:]))
                nc.vector.tensor_tensor(k.rows_of[:, 0:NS, 0], token[:], kan_rows[:], ALU.add)
                dve.wait_ge(prob_ready, 1)
                link(nc.vector.tensor_tensor(weighed[:], prob[:], chosen[:], ALU.mult))
                nc.vector.tensor_tensor(tmp[:], pick[:], bc(prob[:], 1, TOPK), ALU.mult)
                link(nc.vector.tensor_reduce(den[:], weighed[:], AX.X, ALU.add))
                link(nc.vector.reciprocal(den[:], den[:]))
                nc.vector.tensor_reduce(k.weight[:], tmp[:], AX.X, ALU.add)
                link(nc.vector.tensor_scalar(den[:], den[:], 0.5, None, ALU.mult))
                link(nc.vector.tensor_tensor(k.weight[:], k.weight[:], bc(den[:], 1, TOPK), ALU.mult))
                if n == 0:
                    for e in range(E2):
                        dve.wait_ge(summed, e + 1)
                        sums = xT_ps[e % 2]
                        nc.vector.tensor_tensor(k.kan_b0[:, e], k.kan_b0[:, e], sums[:, 0:F2],
                                                ALU.add).then_inc(sum_added, 1)
                        nc.vector.tensor_tensor(k.kan_b1[:, e], k.kan_b1[:, e], sums[:, F2:F2 + C],
                                                ALU.add).then_inc(sum_added, 1)

            @block.sync
            def _(sp):
                if n == 0:
                    sp.dma_start(k.xs[:], a.x[0].rearrange("(t p) c -> p t c", p=P)).then_inc(k.x_loaded, 16)
                    load_shared(sp, k, a)
                load_mlps(sp, k, a, n)
                load_kan(sp, k, a, n, 0)
                rows = k.x_rows.rearrange("(h t p) c -> h p t c", h=2, p=P)
                sp.wait_ge(xn_ready, NT)
                sp.dma_start(rows[0], xn[:]).then_inc(k.rows_in_dram[n], 16)
                load_kan(sp, k, a, n, 1)
                sp.wait_ge(xh_ready, NT)
                sp.dma_start(rows[1], xh[:]).then_inc(k.rows_in_dram[n], 16)
                load_kan(sp, k, a, n, 2)
                load_kan(sp, k, a, n, 3)
                sp.wait_ge(k.rows_in_dram[n], 32)

            @block.gpsimd
            def _(pool):
                if n == 0:
                    make_constants(pool, k)
                    pool.wait_ge(k.const_made, k.N_CONST)
                if n == 0:
                    pool.wait_ge(var_ready, 1)
                    nc.gpsimd.tensor_tensor(k.rstd[:], k.var_eps[:], k.minus_half[:], ALU.pow).then_inc(rstd_ready, 1)
                pool.wait_ge(var_ready, 2 - n)
                nc.gpsimd.tensor_tensor(rstd2[:], var_eps2[:], k.minus_half[:], ALU.pow).then_inc(rstd_ready, 1)
                pool.wait_ge(in_slot_ready, 1)
                nc.gpsimd.tensor_tensor(numbers[:, :, 0], in_slot[:], bc(k.pair_no[:], 2, NS),
                                        ALU.mult).then_inc(numbers_ready, 1)
                if n == 0:
                    pool.wait_ge(k.kan_loaded[E2 - 1], 16 * 2)
                    by_rows = k.kan_w1[:, E2 - 1].rearrange("p c g o -> p (c g) o")
                    done = 0
                    for src, dst, rows in ((k.kan_w0[:, E2 - 1], fold0, G), (by_rows, fold1, F2C * G)):
                        while rows > 1:
                            rows //= 2
                            nc.gpsimd.tensor_tensor(dst[:, 0:rows], src[:, 0:rows], src[:, rows:2 * rows],
                                                    ALU.add).then_inc(folded, 1)
                            done += 1
                            pool.wait_ge(folded, done)
                            src = dst
                    assert done == FOLDS

            @block.tensor
            def _(pe):
                def column_sums(e):
                    sums = xT_ps[e % 2]
                    if e >= 2:
                        pe.wait_ge(sum_added, 2 * (e - 1))
                    if e == E2 - 1:
                        pe.wait_ge(folded, FOLDS)
                        terms0, terms1 = [fold0[:, 0]], [fold1[:, 0]]
                    else:
                        pe.wait_ge(k.kan_loaded[e], 16 * 2)
                        terms0 = [k.kan_w0[:, e, g] for g in range(G)]
                        terms1 = [k.kan_w1[:, e, c, g] for c in range(F2C) for g in range(G)]
                    for out, terms in ((sums[:, 0:F2], terms0), (sums[:, F2:F2 + C], terms1)):
                        for m, term in enumerate(terms):
                            last = nc.tensor.matmul(out, k.ones[:], term, start=(m == 0), stop=(m == len(terms) - 1))
                    last.then_inc(summed, 1)

                pe.wait_ge(k.const_made, k.N_CONST)
                for g in range(NT // 4):
                    if g >= 2:
                        pe.wait_ge(xT_copied, g - 1)
                    for t in range(4 * g, 4 * g + 4):
                        pe.wait_ge(xn_ready, t + 1)
                        last = nc.tensor.transpose(xT_ps[g % 2][:, (t % 4) * P:(t % 4 + 1) * P], xn[:, t],
                                                   k.ident[:])
                    last.then_inc(xT_ready, 1)
                if n == 0:
                    pe.wait_ge(k.small_loaded, 16 * N_SHARED)
                for t in range(NT):
                    pe.wait_ge(xT_copied, t // 4 + 1)
                    last = nc.tensor.matmul(logit_ps[:, t], xnT[:, t * P:(t + 1) * P], k.gate_w[:],
                                            start=True, stop=True)
                last.then_inc(logits_ready, 1)
                if n == 0:
                    for e in range(EARLY):
                        column_sums(e)
                pe.wait_ge(chosen_ready, 1)
                nc.tensor.matmul(sum_ps[:], k.ones[:], chosen[:], start=True, stop=True)
                nc.tensor.matmul(cum_ps[:], k.later[:], chosen[:], start=True,
                                 stop=True).then_inc(counts_ready, 1)
                if n == 0:
                    column_sums(EARLY)
                pe.wait_ge(numbers_ready, 2)
                for j in range(TOPK):
                    pe.wait_ge(in_row_ready, j + 1)
                    for v in range(j * NT, (j + 1) * NT):
                        last = nc.tensor.matmul(found_ps[:], in_row[:, v], numbers[:, v], start=(v == 0),
                                                stop=(v == TOPK * NT - 1))
                last.then_inc(found_ready, 1)
                if n == 0:
                    for e in range(EARLY + 1, E2):
                        column_sums(e)

            @block.scalar
            def _(act):
                for g in range(NT // 4):
                    act.wait_ge(xT_ready, g + 1)
                    nc.scalar.copy(xnT[:, g * 4 * P:(g + 1) * 4 * P], xT_ps[g % 2][:]).then_inc(xT_copied, 1)
                act.wait_ge(rstd_ready, 2 - n)
                for t in range(NT):
                    nc.scalar.activation(xh[:, t], xn[:, t], ACT.Copy, scale=rstd2[:, t:t + 1]).then_inc(xh_ready, 1)
                act.wait_ge(below_ready, 1)
                nc.scalar.activation(prob[:], below[:], ACT.Exp).then_inc(prob_ready, 1)
                act.wait_ge(in_slot_ready, 1)
                nc.scalar.activation(numbers[:, :, 1], in_slot[:], ACT.Copy, scale=k.one_up[:]).then_inc(numbers_ready, 1)


def load_experts(nc, eng, row):
    return nc.values_load_multi_w_load_instructions(
        row, engines=[eng.engine], min_val=0, max_val=E2 - 1,
        skip_runtime_bounds_check_because="the table counts the experts that end before a block, E2 - 1 at most")[1]


def mlp_blocks(nc, k, a, n):
    with ExitStack() as ctx:
        sb = lambda name, shape, dt=F32: ctx.enter_context(nc.sbuf_tensor(f"{name}_{n}", shape, dt))
        ps = lambda name, shape: ctx.enter_context(nc.psum_tensor(f"{name}_{n}", shape, F32))
        sem = lambda name: k.moe_sem(name)
        x_in = [sb(f"m_x_in{u}", [P, C]) for u in range(2)]
        xT = sb("m_xT", [P, P])
        z = sb("m_z", [P, F])
        hT = sb("m_hT", [P, FC, P])
        y = [sb(f"m_y{u}", [P, C]) for u in range(2)]
        rows_now = [sb(f"m_rows_now{u}", [P, 2], I32) for u in range(2)]
        xT_ps = ps("m_xT_ps", [P, P])
        z_ps = ps("m_z_ps", [P, F])
        zT_ps = ps("m_zT_ps", [P, FC, P])
        y_ps = ps("m_y_ps", [P, C])
        loaded, stored = ([k.sem(f"m_{x}{u}_{n}") for u in range(2)] for x in ("loaded", "stored"))
        turned, xT_ready = sem("m_turned"), sem("m_xT_ready")
        z_done, z_ready, zT_done = sem("m_z_done"), sem("m_z_ready"), sem("m_zT_done")
        hT_ready, y_done, y_ready, y_free = sem("m_hT_ready"), sem("m_y_done"), sem("m_y_ready"), sem("m_y_free")
        cleared, noted, rows_ready = sem("m_cleared"), sem("m_noted"), sem("m_rows_ready")

        def pairs(eng):
            return eng.value_load(k.n_pairs[0:1, 0:1], min_val=1, max_val=(MAXB + 2) // 2)

        def experts(eng, ii):
            return load_experts(nc, eng, k.experts[0:1, 0, bass.ds(ii, 1)])

        with nc.Block() as block:
            @block.gpsimd
            def _(pool):
                end = pairs(pool)

                def gather(u, rows):
                    pool.indirect_dma_start(
                        x_in[u][:], None, k.x_rows,
                        bass.IndirectOffsetOnAxis(ap=rows.bitcast(U32), axis=0)).then_inc(loaded[u], 16)

                def one_round(i, ii, u, first):
                    pool.wait_ge(turned, i + 2)
                    if not first:
                        pool.wait_ge(stored[u], ii * 16)
                    pool.sem_inc(y_free, 1)
                    nc.gpsimd.tensor_copy(rows_now[u][:], k.rows_of[:, bass.ds(i + LEAD, 1)]
                                          ).then_inc(rows_ready, 1)
                    pool.wait_ge(rows_ready, i + 1)
                    pool.sem_inc(noted, 1)
                    gather(1 - u, rows_now[u][:, 0:1])
                    pool.wait_ge(y_ready, i + 2)
                    pool.sem_inc(noted, 1)
                    pool.indirect_dma_start(
                        k.y_rows, bass.IndirectOffsetOnAxis(ap=rows_now[u][:, 1:2].bitcast(U32), axis=0),
                        y[u][:], None).then_inc(stored[u], 16)

                for b in range(LEAD - 1):
                    if b == 2:
                        pool.wait_ge(turned, 1)
                    gather(b % 2, k.rows_of[:, 1 + b, 0:1])
                for u in range(2):
                    one_round(u, 0, u, True)
                with pool.Fori(1, end) as ii:
                    for u in range(2):
                        one_round(2 * ii + u, ii, u, False)
                for u in range(2):
                    pool.wait_ge(loaded[u], end * 16 + (32 - 16 * u))
                    pool.wait_ge(stored[u], end * 16)
                    pool.sem_inc(noted, 1)

            @block.tensor
            def _(pe):
                end = pairs(pe)

                def turn(u, nth):
                    pe.wait_ge(loaded[u], nth * 16)
                    nc.tensor.transpose(xT_ps[:], x_in[u][:], k.ident[:]).then_inc(turned, 1)

                def by_w1(block, e):
                    pe.wait_ge(xT_ready, block + 1)
                    nc.tensor.matmul(z_ps[:], xT[:], k.mlp_w1[:, bass.ds(e, 1)], start=True,
                                     stop=True).then_inc(z_done, 1)

                turn(0, 1)
                pe.wait_ge(k.mlp_loaded[n], 16 * N_MLP)
                pe.sem_inc(y_ready, 1)
                by_w1(0, experts(pe, 0)[1])
                with pe.Fori(0, end) as ii:
                    for u in range(2):
                        i = 2 * ii + u
                        turn(1 - u, ii + 1 + u)
                        if u == 0:
                            e_pair = experts(pe, ii)
                        e_last, e_next = e_pair[u], e_pair[u + 2]
                        pe.wait_ge(hT_ready, i + 1)
                        pe.wait_ge(y_ready, i + 1)
                        for c in range(FC):
                            last = nc.tensor.matmul(y_ps[:], hT[:, c], k.mlp_w2[:, bass.ds(e_last, 1), c],
                                                    start=(c == 0), stop=(c == FC - 1))
                        last.then_inc(y_done, 1)
                        pe.wait_ge(z_ready, i + 1)
                        for c in range(FC):
                            last = nc.tensor.transpose(zT_ps[:, c], z[:, c * P:(c + 1) * P], k.ident[:])
                        last.then_inc(zT_done, 1)
                        by_w1(i + 1, e_next)

            @block.vector
            def _(dve):
                end = pairs(dve)
                nc.vector.memset(hT[:], 0.0).then_inc(cleared, 1)
                dve.wait_ge(turned, 1)
                nc.vector.tensor_copy(xT[:], xT_ps[:]).then_inc(xT_ready, 1)
                with dve.Fori(0, end) as ii:
                    e_pair = experts(dve, ii)
                    for u in range(2):
                        i = 2 * ii + u
                        e_last, e = e_pair[u], e_pair[u + 1]
                        dve.wait_ge(z_done, i + 1)
                        nc.vector.tensor_tensor(z[:], z_ps[:], k.mlp_b1[:, bass.ds(e, 1)],
                                                ALU.add).then_inc(z_ready, 1)
                        dve.wait_ge(turned, i + 2)
                        nc.vector.tensor_copy(xT[:], xT_ps[:]).then_inc(xT_ready, 1)
                        dve.wait_ge(y_done, i + 1)
                        dve.wait_ge(y_free, i + 1)
                        nc.vector.tensor_tensor(y[u][:], y_ps[:], k.mlp_b2[:, bass.ds(e_last, 1)],
                                                ALU.add).then_inc(y_ready, 1)

            @block.scalar
            def _(act):
                end = pairs(act)
                act.wait_ge(cleared, 1)
                act.preload_act_table(ACT.Gelu)
                act.sem_inc(hT_ready, 1)
                with act.Fori(0, end) as ii:
                    for u in range(2):
                        act.wait_ge(zT_done, 2 * ii + u + 1)
                        nc.scalar.activation(hT[:], zT_ps[:], ACT.Gelu).then_inc(hT_ready, 1)


def kan_blocks(nc, k, a, n):
    with ExitStack() as ctx:
        sb = lambda name, shape, dt=F32: ctx.enter_context(nc.sbuf_tensor(f"{name}_{n}", shape, dt))
        ps = lambda name, shape: ctx.enter_context(nc.psum_tensor(f"{name}_{n}", shape, F32))
        sem = lambda name: k.moe_sem(name)
        x_in = [sb(f"k_x_in{u}", [P, C]) for u in range(2)]
        h0T = sb("k_h0T", [P, P])
        tanh0 = sb("k_tanh0", [P, G, P])
        basis0 = sb("k_basis0", [P, G, P])
        z = sb("k_z", [P, F2])
        st = sb("k_st", [P, 6])
        mv = sb("k_mv", [P, 2])
        var_eps = sb("k_var_eps", [P, 1])
        rstd = sb("k_rstd", [P, 1])
        zn = sb("k_zn", [P, F2])
        h1T = sb("k_h1T", [P, F2C, P])
        tanh1 = sb("k_tanh1", [P, G, F2C, P])
        basis1 = sb("k_basis1", [P, G, F2C, P])
        y = [sb(f"k_y{u}", [P, C]) for u in range(2)]
        rows_now = [sb(f"k_rows_now{u}", [P, 2], I32) for u in range(2)]
        rows_first = sb("k_rows_first", [P, LEAD - 1, 2], I32)
        xT_ps = ps("k_xT_ps", [P, P])
        z_ps = ps("k_z_ps", [P, F2])
        znT_ps = ps("k_znT_ps", [P, F2C, P])
        y_ps = ps("k_y_ps", [P, C])
        loaded, stored = ([k.sem(f"k_{x}{u}_{n}") for u in range(2)] for x in ("loaded", "stored"))
        turned, h0_ready = sem("k_turned"), sem("k_h0_ready")
        tanh0_done, basis0_ready = sem("k_tanh0_done"), sem("k_basis0_ready")
        tanh1_done, basis1_ready = sem("k_tanh1_done"), sem("k_basis1_ready")
        z_done, z_ready, stats_done, var_ready = sem("k_z_done"), sem("k_z_ready"), sem("k_stats_done"), sem("k_var_ready")
        mean_ready, rstd_ready, zn_ready = sem("k_mean_ready"), sem("k_rstd_ready"), sem("k_zn_ready")
        znT_done, h1_ready = sem("k_znT_done"), sem("k_h1_ready")
        y_done, y_ready, y_free = sem("k_y_done"), sem("k_y_ready"), sem("k_y_free")
        noted, rows_ready = sem("k_noted"), sem("k_rows_ready")
        H0, H1 = 2, 4
        G0, G1 = G // H0, G // H1

        def pairs(eng):
            return eng.value_load(k.n_pairs[0:1, 1:2], min_val=1, max_val=(MAXB + 2) // 2)

        def experts(eng, ii):
            return load_experts(nc, eng, k.experts[0:1, 1, bass.ds(ii, 1)])

        with nc.Block() as block:
            @block.gpsimd
            def _(pool):
                end = pairs(pool)
                start = pool.value_load(k.n_mlp[0:1, 0:1], min_val=0, max_val=MAXB)

                def rows_at(q, size=1):
                    at = nc.s_assert_within(q, 0, NQ - size, skip_runtime_bounds_check_because=BOUND)
                    return k.rows_of[:, bass.ds(at, size)]

                def gather(u, rows):
                    pool.indirect_dma_start(
                        x_in[u][:], None, k.x_rows,
                        bass.IndirectOffsetOnAxis(ap=rows.bitcast(U32), axis=0)).then_inc(loaded[u], 16)

                def one_round(i, ii, u, first):
                    pool.wait_ge(turned, i + 2)
                    if not first:
                        pool.wait_ge(stored[u], ii * 16)
                    pool.sem_inc(y_free, 1)
                    nc.gpsimd.tensor_copy(rows_now[u][:], rows_at(start + i + (1 + LEAD))
                                          ).then_inc(rows_ready, 1)
                    pool.wait_ge(rows_ready, i + 2)
                    pool.sem_inc(noted, 1)
                    gather(1 - u, rows_now[u][:, 0:1])
                    pool.wait_ge(var_ready, i + 1)
                    nc.gpsimd.tensor_tensor(rstd[:], var_eps[:], k.minus_half[:, 0:1],
                                            ALU.pow).then_inc(rstd_ready, 1)
                    pool.wait_ge(y_ready, i + 2)
                    pool.sem_inc(noted, 1)
                    pool.indirect_dma_start(
                        k.y_rows, bass.IndirectOffsetOnAxis(ap=rows_now[u][:, 1:2].bitcast(U32), axis=0),
                        y[u][:], None).then_inc(stored[u], 16)

                nc.gpsimd.tensor_copy(rows_first[:], rows_at(start + 2, LEAD - 1)).then_inc(rows_ready, 1)
                pool.wait_ge(rows_ready, 1)
                for b in range(LEAD - 1):
                    if b == 2:
                        pool.wait_ge(turned, 1)
                    gather(b % 2, rows_first[:, b, 0:1])
                for u in range(2):
                    one_round(u, 0, u, True)
                with pool.Fori(1, end) as ii:
                    for u in range(2):
                        one_round(2 * ii + u, ii, u, False)
                for u in range(2):
                    pool.wait_ge(loaded[u], end * 16 + (32 - 16 * u))
                    pool.wait_ge(stored[u], end * 16)
                    pool.sem_inc(noted, 1)

            @block.tensor
            def _(pe):
                end = pairs(pe)

                def turn(u, nth):
                    pe.wait_ge(loaded[u], nth * 16)
                    nc.tensor.transpose(xT_ps[:], x_in[u][:], k.ident[:]).then_inc(turned, 1)

                def by_w0(block, e):
                    for g in range(G):
                        if g % G0 == 0:
                            pe.wait_ge(basis0_ready, H0 * block + (g // G0 + 1))
                        last = nc.tensor.matmul(z_ps[:], basis0[:, g], k.kan_w0[:, bass.ds(e, 1), g],
                                                start=(g == 0), stop=(g == G - 1))
                    last.then_inc(z_done, 1)

                turn(0, 1)
                pe.wait_ge(h0_ready, 1)
                turn(1, 1)
                if n == 0:
                    for e in range(E2):
                        pe.wait_ge(k.kan_loaded[e], 16 * 2)
                else:
                    pe.wait_ge(k.kans_loaded_again, 16 * 2 * E2)
                pe.sem_inc(y_ready, 1)
                by_w0(0, experts(pe, 0)[1])
                with pe.Fori(0, end) as ii:
                    e_pair = experts(pe, ii)
                    for u in range(2):
                        i = 2 * ii + u
                        e_last, e_next = e_pair[u], e_pair[u + 2]
                        pe.wait_ge(y_ready, i + 1)
                        for g in range(G):
                            if g % G1 == 0:
                                pe.wait_ge(basis1_ready, H1 * i + g // G1 + 1)
                            for c in range(F2C):
                                last = nc.tensor.matmul(y_ps[:], basis1[:, g, c],
                                                        k.kan_w1[:, bass.ds(e_last, 1), c, g],
                                                        start=(g == 0 and c == 0), stop=(g == G - 1 and c == F2C - 1))
                        last.then_inc(y_done, 1)
                        pe.wait_ge(zn_ready, i + 1)
                        for c in range(F2C):
                            last = nc.tensor.transpose(znT_ps[:, c], zn[:, c * P:(c + 1) * P], k.ident[:])
                        last.then_inc(znT_done, 1)
                        pe.wait_ge(h0_ready, i + 2)
                        turn(u, ii + 2)
                        by_w0(i + 1, e_next)

            @block.vector
            def _(dve):
                end = pairs(dve)

                def affine0(e, blocks_turned):
                    dve.wait_ge(turned, blocks_turned)
                    nc.vector.tensor_scalar(h0T[:], xT_ps[:], k.kan_g0[:, bass.ds(e, 1)],
                                            k.kan_c0[:, bass.ds(e, 1)], ALU.mult, ALU.add).then_inc(h0_ready, 1)

                def square0(before, parts=range(H0)):
                    for h in parts:
                        dve.wait_ge(tanh0_done, before + h + 1)
                        part = slice(h * G0, (h + 1) * G0)
                        nc.vector.tensor_tensor(basis0[:, part], tanh0[:, part], tanh0[:, part],
                                                ALU.mult).then_inc(basis0_ready, 1)

                nc.vector.memset(h1T[:], 0.0).then_inc(h1_ready, 1)
                affine0(experts(dve, 0)[1], 1)
                square0(0)
                with dve.Fori(0, end) as ii:
                    e_pair = experts(dve, ii)
                    for u in range(2):
                        i = 2 * ii + u
                        e_last, e, e_next = e_pair[u:u + 3]
                        dve.wait_ge(tanh0_done, H0 * i + H0)
                        affine0(e_next, i + 2)
                        for h in range(H1):
                            if h == H1 - 1:
                                dve.wait_ge(z_done, i + 1)
                                nc.vector.tensor_tensor(z[:], k.kan_b0[:, bass.ds(e, 1)], z_ps[:],
                                                        ALU.subtract).then_inc(z_ready, 1)
                            dve.wait_ge(tanh1_done, H1 * i + h + 1)
                            part = slice(h * G1, (h + 1) * G1)
                            nc.vector.tensor_tensor(basis1[:, part], tanh1[:, part], tanh1[:, part],
                                                    ALU.mult).then_inc(basis1_ready, 1)
                        dve.wait_ge(z_ready, i + 1)
                        nc.vector.bn_stats(st[:], z[:]).then_inc(stats_done, 1)
                        dve.wait_ge(h0_ready, 1)
                        dve.wait_ge(stats_done, i + 1)
                        nc.vector.bn_aggr(mv[:], st[:]).then_inc(mean_ready, 1)
                        dve.wait_ge(mean_ready, i + 1)
                        nc.vector.tensor_scalar(var_eps[:], mv[:, 1:2], EPS, None, ALU.add).then_inc(var_ready, 1)
                        square0(H0 * i + H0, [0])
                        dve.wait_ge(rstd_ready, i + 1)
                        nc.vector.tensor_scalar(zn[:], z[:], mv[:, 0:1], rstd[:], ALU.subtract,
                                                ALU.mult).then_inc(zn_ready, 1)
                        square0(H0 * i + H0, [1])
                        dve.wait_ge(znT_done, i + 1)
                        dve.wait_ge(tanh1_done, H1 * i + H1)
                        for c in range(F2C):
                            last = nc.vector.tensor_scalar(h1T[:, c], znT_ps[:, c], k.kan_g1[:, c, bass.ds(e, 1)],
                                                           k.kan_c1[:, c, bass.ds(e, 1)], ALU.mult, ALU.add)
                        last.then_inc(h1_ready, 1)
                        dve.wait_ge(y_done, i + 1)
                        dve.wait_ge(y_free, i + 1)
                        nc.vector.tensor_tensor(y[u][:], k.kan_b1[:, bass.ds(e_last, 1)], y_ps[:],
                                                ALU.subtract).then_inc(y_ready, 1)

            @block.scalar
            def _(act):
                end = pairs(act)

                def tanh0_parts():
                    for g in range(G):
                        ins = nc.scalar.activation(tanh0[:, g], h0T[:], ACT.Tanh, bias=float(-0.5 * GRID[g]),
                                                   scale=0.5)
                        if g % G0 == G0 - 1:
                            ins.then_inc(tanh0_done, 1)

                act.wait_ge(h0_ready, 1)
                tanh0_parts()
                with act.Fori(0, end) as ii:
                    for u in range(2):
                        i = 2 * ii + u
                        act.wait_ge(h1_ready, i + 1)
                        for g in range(G):
                            ins = nc.scalar.activation(tanh1[:, g], h1T[:], ACT.Tanh, bias=float(-0.5 * GRID[g]),
                                                       scale=0.5)
                            if g % G1 == G1 - 1:
                                ins.then_inc(tanh1_done, 1)
                        act.wait_ge(h0_ready, i + 2)
                        act.wait_ge(basis0_ready, H0 * i + H0)
                        tanh0_parts()


def combine(nc, k, a, n, out):
    PART = 4
    with ExitStack() as ctx:
        got = ctx.enter_context(nc.sbuf_tensor(f"got_{n}", [P, TOPK, NT, C], F32))
        loaded = [k.moe_sem(f"got_loaded{g}") for g in range(NT // PART)]
        first_added, x_ready = (k.moe_sem(x) for x in ("first_added", "x_ready"))
        rows = k.y_rows[0:TOPK * T].rearrange("(j t p) c -> p j t c", j=TOPK, p=P)
        stats = ChunkStats(nc, k, k.sem, "got") if out is None else None
        parts = [slice(g * PART, (g + 1) * PART) for g in range(NT // PART)]
        with nc.Block() as block:
            @block.scalar
            def _(act):
                for g, part in enumerate(parts):
                    act.dma_start(got[:, 1, part], rows[:, 1, part]).then_inc(loaded[g], 16)

            @block.vector
            def _(dve):
                for g in range(NT // PART):
                    dve.wait_ge(loaded[g], 16 * TOPK)
                    for j in range(TOPK):
                        for t in range(g * PART, (g + 1) * PART):
                            last = nc.vector.scalar_tensor_tensor(k.xs[:, t], got[:, j, t], k.weight[:, j, t:t + 1],
                                                                  k.xs[:, t], ALU.mult, ALU.add)
                        if j == 0:
                            last.then_inc(first_added, 1)
                            dve.wait_ge(first_added, g + 1)
                    last.then_inc(x_ready, 1)
                    if stats:
                        dve.wait_ge(x_ready, g + 1)
                        stats.on_vector(dve, g)

            @block.gpsimd
            def _(pool):
                if stats:
                    for g in range(NT // PART):
                        stats.on_gpsimd(pool, g)

            @block.sync
            def _(sp):
                for g, part in enumerate(parts):
                    sp.dma_start(got[:, 0, part], rows[:, 0, part]).then_inc(loaded[g], 16)
                if out is not None:
                    tiles = out[0].rearrange("(t p) c -> p t c", p=P)
                    for g, part in enumerate(parts):
                        sp.wait_ge(x_ready, g + 1)
                        sp.dma_start(tiles[:, part], k.xs[:, part]).then_inc(k.stored_out, 16)
                    sp.wait_ge(k.stored_out, 16 * (NT // PART))


def moe(nc, k, a, n, out=None):
    with ExitStack() as ctx:
        moe_weights(nc, k, ctx, n)
        route(nc, k, a, n)
        mlp_blocks(nc, k, a, n)
        kan_blocks(nc, k, a, n)
        combine(nc, k, a, n, out)

NH = 16
HD = C // NH
PAIRS = NH // 2
WINDOW = 128
assert WINDOW == P
PARTS = 3
RUNS = [(0, 3), (3, 2), (5, 1)]
N_PROD = 6
M_ROW = N_PROD * HD
NEG = -1e30
VW = PARTS * HD + 2
HID = 352
HIDC = [(0, 128), (128, 128), (256, 96)]
QK_G = 4


def project(nc, k, a, s):
    with ExitStack() as ctx:
        sb = lambda name, shape, dt=F32: ctx.enter_context(nc.sbuf_tensor(f"a_{name}", shape, dt))
        ps = lambda name, shape: ctx.enter_context(nc.psum_tensor(f"a_{name}", shape, F32))
        sem = lambda name: k.sem(f"a_{name}")
        W4 = 4 * P
        NCH = NT // 4
        n1 = sb("n1", [P, NT, C])
        n1T = sb("n1T", [P, T])
        w = sb("w", [P, 3, C])
        wp = sb("wp", [P, 4, C])
        cos = sb("cos", [P, T])
        sin = sb("sin", [P, T])
        rstd_sq = sb("rstd_sq", [P, NT])
        scale = sb("scale", [P, NT])
        var_eps = sb("var_eps", [P, NT])
        rstd2 = sb("rstd2", [P, NT])
        part = sb("part", [P, 2, PARTS, 2 * W4], BF16)
        by_cos = sb("by_cos", [P, W4])
        by_sin = sb("by_sin", [P, W4])
        turned_ = sb("turned", [P, W4])
        rest = sb("rest", [P, W4])
        vrest = sb("vrest", [P, W4])
        nT_ps = ps("nT_ps", [P, W4])
        q_ps = [[ps(f"q_ps{x}{y}", [P, W4]) for y in range(2)] for x in range(2)]
        v_ps = ps("v_ps", [P, 4, C])
        loaded, w_swapped, var_ready, rstd_ready = sem("loaded"), sem("w_swapped"), sem("var_ready"), sem("rstd_ready")
        n1_ready, nT_done, nT_ready = sem("n1_ready"), sem("nT_done"), sem("nT_ready")
        qk_done, qk_used, v_done, v_used = sem("qk_done"), sem("qk_used"), sem("v_done"), sem("v_used")
        rot_ready, hi_ready, rest_ready, mid_ready = sem("rot_ready"), sem("hi_ready"), sem("rest_ready"), sem("mid_ready")
        parts_ready, k_cleared, q_cleared = sem("parts_ready"), sem("k_cleared"), sem("q_cleared")
        parts_out = [sem(f"parts_out{x}") for x in range(2)]
        v_set, k_set = sem("v_set"), sem("k_set")
        stacked = [sem("stacked"), k.sem("stacked_by_pool")]
        step = sem("step")
        parts_dram = nc.dram_tensor("qk_parts", [2, 2, PARTS, HD * PAIRS, T], BF16, kind="Internal").ap()
        NU = 2 * NCH

        def key_rows(r0, r1, odd):
            return s.k_stack[r0:r1].bitcast(F32).rearrange("r (p two) t -> r two p t", two=2)[:, odd]

        def half(g):
            return slice((g % 2) * W4, (g % 2 + 1) * W4)

        def load_stack(q, odd, h, x, loaded_by_q):
            cols = slice(2 * h * W4, 2 * (h + 1) * W4)
            for run, (c0, cn) in enumerate(RUNS):
                if x == 0:
                    rows = slice(64 * odd + c0 * HD, 64 * odd + (c0 + cn) * HD)
                    q.dma_start(s.q_stack[rows, :, cols],
                                parts_dram[x, odd, 0:cn, :, cols].rearrange("c (d p) t -> (c d) p t", d=HD)
                                ).then_inc(loaded_by_q, 16)
                    continue
                for c in range(c0, c0 + cn):
                    rows = slice(64 * odd + c * HD, 64 * odd + (c + 1) * HD)
                    q.dma_start(s.k_stack[rows, odd::2, cols],
                                parts_dram[x, odd, run, :, cols].rearrange("(d p) t -> d p t", d=HD)
                                ).then_inc(loaded_by_q, 16)

        with nc.Block() as block:
            @block.sync
            def _(sp):
                sp.dma_start(w[:, 0], a.wq).then_inc(loaded, 16)
                sp.dma_start(w[:, 1], a.wk).then_inc(loaded, 16)
                sp.dma_start(w[:, 2], a.wv).then_inc(loaded, 16)
                sp.dma_start(k.ln_vec[:], a.attn_ln).then_inc(loaded, 16)
                sp.dma_start(cos[:], a.cos).then_inc(loaded, 16)
                sp.dma_start(sin[:], a.sin).then_inc(loaded, 16)
                sp.dma_start(s.wo[:], a.wo).then_inc(s.tail_loaded, 16)
                sp.dma_start(s.w1[:], a.w1).then_inc(s.tail_loaded, 16)
                sp.dma_start(s.w3[:], a.w3).then_inc(s.tail_loaded, 16)
                for c, (at, size) in enumerate(HIDC):
                    sp.dma_start(s.w2[0:size, c], a.w2[at:at + size]).then_inc(s.tail_loaded, 16)
                def store_parts(h, x):
                    cols = slice(2 * h * W4, 2 * (h + 1) * W4)
                    sp.wait_ge(parts_ready, 2 * (2 * h + 1) + 2 - x)
                    for odd in range(2):
                        sp.dma_start(parts_dram[x, odd, :, :, cols].rearrange("r k t -> k r t"),
                                     part[64 * odd:64 * (odd + 1), x]).then_inc(parts_out[x], 16)

                store_parts(0, 1)
                store_parts(0, 0)
                sp.wait_ge(k_cleared, 1)
                sp.wait_ge(k_set, 3)
                sp.wait_ge(q_cleared, 1)
                for x in (1, 0):
                    sp.wait_ge(parts_out[x], 16 * 2)
                    load_stack(sp, 0, 0, x, stacked[0])
                for x in (1, 0):
                    store_parts(1, x)
                    sp.wait_ge(parts_out[x], 16 * 2 * 2)
                    load_stack(sp, 0, 1, x, stacked[0])
                for q in range(2):
                    sp.wait_ge(stacked[q], 16 * (NCH // 2) * (len(RUNS) + N_PROD))

            @block.gpsimd
            def _(pool):
                pool.memset(s.mask[:], 0.0).then_inc(s.mask_set, 1)
                pool.wait_ge(s.mask_set, 1)
                pool.affine_select(out=s.mask[:], in_=s.mask[:], compare_op=ALU.is_ge, fill=NEG, base=0,
                                   pattern=[[0, 2], [1, 2 * P]], channel_multiplier=-1).then_inc(s.mask_set, 1)
                pool.wait_ge(s.mask_set, 2)
                pool.affine_select(out=s.mask[:], in_=s.mask[:], compare_op=ALU.is_ge, fill=NEG, base=WINDOW,
                                   pattern=[[0, 2], [-1, 2 * P]], channel_multiplier=1).then_inc(s.mask_set, 1)
                pool.wait_ge(var_ready, 1)
                nc.gpsimd.tensor_tensor(rstd2[:], var_eps[:], k.minus_half[:], ALU.pow).then_inc(rstd_ready, 1)
                ones2 = float(np.array([0x3F803F80], np.uint32).view(np.float32)[0])
                pool.wait_ge(rstd_ready, 1)
                pool.memset(s.q_stack[:].bitcast(F32), 0.0).then_inc(q_cleared, 1)
                pool.wait_ge(q_cleared, 1)
                pool.memset(key_rows(32, 64, 0), ones2).then_inc(k_set, 1)
                pool.wait_ge(k_set, 1)
                pool.memset(key_rows(96, 128, 1), ones2).then_inc(k_set, 1)
                pool.wait_ge(k_set, 2)
                pool.memset(key_rows(0, 64, 1), 0.0).then_inc(k_set, 1)
                pool.wait_ge(k_cleared, 1)
                pool.wait_ge(k_set, 3)
                for h in range(NCH // 2):
                    for x in (1, 0):
                        pool.wait_ge(parts_out[x], 16 * 2 * (h + 1))
                        load_stack(pool, 1, h, x, stacked[1])

            @block.vector
            def _(dve):
                done = [0]

                def link(ins):
                    done[0] += 1
                    ins.then_inc(step, 1)
                    dve.wait_ge(step, done[0])

                nc.vector.tensor_copy(s.ident16[:], k.ident[:]).then_inc(s.ident16_ready, 1)
                link(nc.vector.tensor_tensor(rstd_sq[:], k.rstd[:], k.rstd[:], ALU.mult))
                link(nc.vector.tensor_tensor(var_eps[:], k.mv[:, :, 1], rstd_sq[:], ALU.mult))
                nc.vector.tensor_scalar(var_eps[:], var_eps[:], EPS, None, ALU.add).then_inc(var_ready, 1)
                for t in range(NT):
                    nc.vector.tensor_scalar(s.res[:, t], k.xs[:, t], k.mv[:, t, 0:1], k.rstd[:, t:t + 1],
                                            ALU.subtract, ALU.mult)
                dve.wait_ge(rstd_ready, 1)
                link(nc.vector.tensor_tensor(scale[:], k.rstd[:], rstd2[:], ALU.mult))
                for t in range(NT):
                    nc.vector.tensor_scalar(n1[:, t], k.xs[:, t], k.mv[:, t, 0:1], scale[:, t:t + 1],
                                            ALU.subtract, ALU.mult).then_inc(n1_ready, 1)
                dve.wait_ge(loaded, 16 * 6)
                link(nc.vector.tensor_scalar(w[:, 0], w[:, 0], float(HD) ** -0.5, None, ALU.mult))
                for x in range(2):
                    src = w[:, x].rearrange("r (p o e f) -> r o e f p", p=PAIRS, o=2, f=2)
                    same = wp[:, x].rearrange("r (o e f p) -> r o e f p", p=PAIRS, o=2, f=2)
                    swapped = wp[:, 2 + x].rearrange("r (o e f p) -> r o e f p", p=PAIRS, o=2, f=2)
                    for f in range(2):
                        nc.vector.tensor_copy(same[:, :, :, f], src[:, :, :, f]).then_inc(w_swapped, 1)
                        nc.vector.tensor_copy(swapped[:, :, :, f], src[:, :, :, 1 - f]).then_inc(w_swapped, 1)
                dve.wait_ge(v_set, 1)

                def values(g):
                    dst = s.v_parts[:, g * 4 + 1:(g + 1) * 4 + 1]
                    by_head = lambda x: x.rearrange("p (t h d) -> p t h d", t=4, h=NH)
                    dve.wait_ge(v_done, g + 1)
                    v = v_ps[:].rearrange("p t (h d) -> p t h d", h=NH)
                    link(nc.vector.tensor_copy(dst[:, :, :, 0:HD], v))
                    nc.vector.tensor_tensor(by_head(vrest[:]), v, dst[:, :, :, 0:HD], ALU.subtract).then_inc(v_used, 1)
                    dve.wait_ge(v_used, g + 1)
                    link(nc.vector.tensor_copy(dst[:, :, :, HD:2 * HD], by_head(vrest[:])))
                    link(nc.vector.tensor_tensor(dst[:, :, :, 2 * HD:3 * HD], by_head(vrest[:]),
                                                 dst[:, :, :, HD:2 * HD], ALU.subtract))

                def last_part(u):
                    x, g = 1 - u % 2, u // 2
                    dve.wait_ge(mid_ready, u + 1)
                    nc.vector.tensor_tensor(part[:, x, 2, half(g)], rest[:], part[:, x, 1, half(g)],
                                            ALU.subtract).then_inc(parts_ready, 1)

                for u in range(NU):
                    x, g = 1 - u % 2, u // 2
                    cols = slice(g * W4, (g + 1) * W4)
                    dve.wait_ge(qk_done, u + 1)
                    if u >= 1:
                        dve.wait_ge(hi_ready, u)
                    nc.vector.tensor_tensor(by_cos[:], q_ps[x][0][:], cos[:, cols], ALU.mult)
                    nc.vector.tensor_tensor(by_sin[:], q_ps[x][1][:], sin[:, cols], ALU.mult).then_inc(qk_used, 1)
                    dve.wait_ge(qk_used, u + 1)
                    nc.vector.tensor_tensor(turned_[:], by_cos[:], by_sin[:], ALU.add).then_inc(rot_ready, 1)
                    if u % 2 == 0:
                        values(g)
                    if u:
                        last_part(u - 1)
                        dve.wait_ge(parts_ready, u)
                    dve.wait_ge(hi_ready, u + 1)
                    nc.vector.tensor_tensor(rest[:], turned_[:], part[:, x, 0, half(g)],
                                            ALU.subtract).then_inc(rest_ready, 1)
                last_part(NU - 1)

            @block.scalar
            def _(act):
                def chunk_T(g):
                    act.wait_ge(nT_done, g + 1)
                    nc.scalar.activation(n1T[:, g * W4:(g + 1) * W4], nT_ps[:], ACT.Identity,
                                         bias=k.ln_vec[:, 1:2], scale=k.ln_vec[:, 0:1]).then_inc(nT_ready, 1)

                nc.scalar.copy(s.v_parts[:].rearrange("p t h d -> p (t h d)"),
                               k.scan_ones[:, 0:1].to_broadcast([P, (NT + 1) * NH * VW])).then_inc(v_set, 1)
                act.wait_ge(loaded, 16 * 6)
                chunk_T(0)
                nc.scalar.activation(key_rows(64, 128, 0), bc(bc(k.scan_ones[64:128, 0], 1, T // 2), 1, PAIRS),
                                     ACT.Copy, scale=0.0).then_inc(k_cleared, 1)
                for u in range(NU):
                    x, g = 1 - u % 2, u // 2
                    if u % 2 == 0 and g + 1 < NCH:
                        chunk_T(g + 1)
                    act.wait_ge(rot_ready, u + 1)
                    if g % 2 == 0 and g:
                        act.wait_ge(parts_out[x], 16 * 2 * (g // 2))
                    nc.scalar.copy(part[:, x, 0, half(g)], turned_[:]).then_inc(hi_ready, 1)
                    act.wait_ge(rest_ready, u + 1)
                    nc.scalar.copy(part[:, x, 1, half(g)], rest[:]).then_inc(mid_ready, 1)

            @block.tensor
            def _(pe):
                def chunk_T(g):
                    if g:
                        pe.wait_ge(nT_ready, g)
                    for t in range(4):
                        pe.wait_ge(n1_ready, 4 * g + t + 1)
                        last = nc.tensor.transpose(nT_ps[:, t * P:(t + 1) * P], n1[:, 4 * g + t], k.ident[:])
                    last.then_inc(nT_done, 1)

                chunk_T(0)
                pe.wait_ge(w_swapped, 8)
                for u in range(NU):
                    x, g = 1 - u % 2, u // 2
                    if u % 2 == 0:
                        if g + 1 < NCH:
                            chunk_T(g + 1)
                        pe.wait_ge(nT_ready, g + 1)
                        if g:
                            pe.wait_ge(v_used, g)
                        for t in range(4):
                            last = nc.tensor.matmul(v_ps[:, t], n1T[:, (4 * g + t) * P:(4 * g + t + 1) * P], w[:, 2],
                                                    start=True, stop=True)
                        last.then_inc(v_done, 1)
                    if u >= 2:
                        pe.wait_ge(qk_used, u - 1)
                    nc.tensor.matmul(q_ps[x][0][:], wp[:, x], n1T[:, g * W4:(g + 1) * W4], start=True, stop=True)
                    nc.tensor.matmul(q_ps[x][1][:], wp[:, 2 + x], n1T[:, g * W4:(g + 1) * W4], start=True,
                                     stop=True).then_inc(qk_done, 1)


def maxima(nc, k, a, s):
    with ExitStack() as ctx:
        sb = lambda name, shape, dt=F32: ctx.enter_context(nc.sbuf_tensor(f"x_{name}", shape, dt))
        sem = lambda name: k.sem(f"x_{name}")
        minus_max = sb("minus_max", [P, NT, NH])
        mT = sb("mT", [NH, T])
        mrest = sb("mrest", [NH, T])
        mpart = sb("mpart", [NH, PARTS, T], BF16)
        NG = NH // QK_G
        HALF = T // 2
        scored, reduced = sem("scored"), sem("reduced")
        mT_done, mT_ready = sem("mT_done"), sem("mT_ready")
        hi, rest1, mid, low = sem("hi"), sem("rest1"), sem("mid"), sem("low")
        split = sem("split")
        out_done, in_done = sem("out_done"), sem("in_done")
        m_dram = nc.dram_tensor("m_parts", [PARTS, NH, T], BF16, kind="Internal").ap()
        BUFS = 3
        sc_ps = [ctx.enter_context(nc.psum_tensor(f"x_sc_ps{g}", [P, QK_G, 2 * P], F32)) for g in range(BUFS)]
        mT_ps = ctx.enter_context(nc.psum_tensor("x_mT_ps", [NH, HALF], F32))
        ROUNDS = (NT - 1) // BUFS
        ROUNDS_1 = (NT // 2 + 1) // BUFS
        assert NT == 1 + ROUNDS * BUFS and 1 + ROUNDS_1 * BUFS >= NT // 2

        def cols(h):
            return slice(h * HALF, (h + 1) * HALF)

        with nc.Block() as block:
            @block.tensor
            def _(pe):
                pe.wait_ge(s.mask_set, 3)
                pe.wait_ge(s.ident16_ready, 1)

                def scores(i, r, first=False):
                    keys = P if first else 2 * P
                    for g in range(NG):
                        if not first or g >= BUFS:
                            pe.wait_ge(reduced, i * NG + (g + 1 - BUFS))
                        buf = sc_ps[(r * NG + g) % BUFS]
                        for b in range(QK_G // 2):
                            h = g * QK_G + 2 * b
                            bank = buf[:, 2 * b:2 * b + 2, 2 * P - keys:]
                            nc.tensor.matmul(bank, s.ident16[:], s.mask[:, :, 2 * P - keys:],
                                             start=True, stop=False)
                            for j in range(2):
                                q = s.q_stack[:, h // 2, bass.ds(i * P, P)]
                                kk = s.k_stack[:, h + j, bass.ds(i * P - (keys - P), keys)]
                                last = nc.tensor.matmul(bank[:, j], q, kk, start=False, stop=(j == 1))
                        last.then_inc(scored, 1)

                def turn_maxima(h):
                    pe.wait_ge(reduced, (h + 1) * NG * NT // 2)
                    if h:
                        pe.wait_ge(mT_ready, 1)
                    for t in range(NT // 2):
                        last = nc.tensor.transpose(mT_ps[:, t * P:(t + 1) * P], minus_max[:, h * NT // 2 + t],
                                                   k.ident[:])
                    last.then_inc(mT_done, 1)

                scores(0, 0, first=True)
                for h, (start, end) in enumerate(((0, ROUNDS_1), (ROUNDS_1, ROUNDS))):
                    with pe.Fori(start, end) as m:
                        for r in range(1, BUFS + 1):
                            scores(BUFS * m + r, r)
                    turn_maxima(h)

            @block.vector
            def _(dve):
                def reduce(i, r, first=False):
                    for g in range(NG):
                        dve.wait_ge(scored, i * NG + g + 1)
                        buf = sc_ps[(r * NG + g) % BUFS]
                        src = buf[:, :, P:] if first else buf[:]
                        dst = minus_max[:, bass.ds(i, 1), g * QK_G:(g + 1) * QK_G]
                        nc.vector.tensor_reduce(dst, src, AX.X, ALU.max, negate=True).then_inc(reduced, 1)

                reduce(0, 0, first=True)
                with dve.Fori(0, ROUNDS) as m:
                    for r in range(1, BUFS + 1):
                        reduce(BUFS * m + r, r)
                dve.wait_ge(mT_done, 2)
                nc.vector.tensor_copy(mT[:, cols(1)], mT_ps[:]).then_inc(split, 1)
                dve.wait_ge(split, 1)
                nc.vector.tensor_copy(mpart[:, 0, cols(1)], mT[:, cols(1)]).then_inc(split, 1)
                dve.wait_ge(split, 2)
                nc.vector.tensor_tensor(mrest[:, cols(1)], mT[:, cols(1)], mpart[:, 0, cols(1)],
                                        ALU.subtract).then_inc(split, 1)
                dve.wait_ge(split, 3)
                nc.vector.tensor_copy(mpart[:, 1, cols(1)], mrest[:, cols(1)]).then_inc(split, 1)
                dve.wait_ge(split, 4)
                nc.vector.tensor_tensor(mpart[:, 2, cols(1)], mrest[:, cols(1)], mpart[:, 1, cols(1)],
                                        ALU.subtract).then_inc(split, 1)

            @block.scalar
            def _(act):
                act.wait_ge(mT_done, 1)
                nc.scalar.copy(mT[:, cols(0)], mT_ps[:]).then_inc(mT_ready, 1)
                act.wait_ge(mT_ready, 1)
                nc.scalar.copy(mpart[:, 0, cols(0)], mT[:, cols(0)]).then_inc(hi, 1)
                act.wait_ge(rest1, 1)
                nc.scalar.copy(mpart[:, 1, cols(0)], mrest[:, cols(0)]).then_inc(mid, 1)

            @block.gpsimd
            def _(pool):
                pool.wait_ge(hi, 1)
                nc.gpsimd.tensor_tensor(mrest[:, cols(0)], mT[:, cols(0)], mpart[:, 0, cols(0)],
                                        ALU.subtract).then_inc(rest1, 1)
                pool.wait_ge(mid, 1)
                nc.gpsimd.tensor_tensor(mpart[:, 2, cols(0)], mrest[:, cols(0)], mpart[:, 1, cols(0)],
                                        ALU.subtract).then_inc(low, 1)
                for used in k.moe_sems.values():
                    pool.sem_clear(used)

            @block.sync
            def _(sp):
                for h in range(2):
                    if h == 0:
                        sp.wait_ge(low, 1)
                    else:
                        sp.wait_ge(split, 5)
                    sp.dma_start(m_dram[:, :, cols(h)].rearrange("r h t -> h r t"),
                                 mpart[:, :, cols(h)]).then_inc(out_done, 16)
                    sp.wait_ge(out_done, 16 * (h + 1))
                    for odd in range(2):
                        row = 64 * odd + M_ROW
                        sp.dma_start(s.q_stack[row:row + PARTS, :, cols(h)],
                                     m_dram[:, :, cols(h)].rearrange("r (p two) t -> two r p t", two=2)[odd]
                                     ).then_inc(in_done, 16)
                sp.wait_ge(in_done, 64)


def attend(nc, k, a, s):
    with ExitStack() as ctx:
        sb = lambda name, shape, dt=F32: ctx.enter_context(nc.sbuf_tensor(f"p_{name}", shape, dt))
        ps = lambda name, shape: ctx.enter_context(nc.psum_tensor(f"p_{name}", shape, F32))
        sem = lambda name: k.sem(f"p_{name}")
        NG = NH // QK_G
        assert NG == 4
        prob = [sb(f"prob{g}", [P, QK_G, 2 * P]) for g in range(NG)]
        hi = [sb(f"hi{u}", [P, NH, 2 * P], F16) for u in range(2)]
        low = [sb(f"low{u}", [P, NH, 2 * P], F16) for u in range(2)]
        v_pair = [sb(f"v_pair{u}", [P, 2, NH, VW], BF16) for u in range(2)]
        total = sb("total", [P, NH, HD])
        inv = sb("inv", [P, NH])
        sc_ps = [ps(f"sc_ps{g}", [P, QK_G, 2 * P]) for g in range(2)]
        o_ps = [ps(f"o_ps{u}", [P, NH, VW]) for u in range(2)]
        scored, exp_done, out_done = sem("scored"), sem("exp_done"), sem("out_done")
        hi_act, hi_dve = sem("hi_act"), sem("hi_dve")
        low_pool, low_dve = sem("low_pool"), sem("low_dve")
        total_ready, inv_ready, att_ready = sem("total_ready"), sem("inv_ready"), sem("att_ready")
        cleared, v_ready = sem("cleared"), sem("v_ready")

        def head_slice(g):
            return slice(g * QK_G, (g + 1) * QK_G)

        def all_rounds(eng, one_round):
            for j in range(2):
                one_round(j, j, first=(j == 0), second=(j == 1))
            with eng.Fori(1, NT // 2) as jj:
                for u in range(2):
                    one_round(2 * jj + u, u, first=False, second=False)

        with nc.Block() as block:
            @block.tensor
            def _(pe):
                def values(j, u, g):
                    pe.wait_ge(low_dve if g % 2 else low_pool, j * 2 + g // 2 + 1)
                    if g == 0:
                        pe.wait_ge(v_ready, j + 1)
                    for h in range(g * QK_G, (g + 1) * QK_G):
                        terms = [(x[w_][:, h, c * P:(c + 1) * P], 1 - c)
                                 for w_, c in ((1 - u, 1), (u, 0)) for x in (hi, low)]
                        for m, (p_, tile) in enumerate(terms):
                            last = nc.tensor.matmul(o_ps[u][:, h], p_, v_pair[u][:, tile, h],
                                                    start=(m == 0), stop=(m == 3))
                    last.then_inc(out_done, 1)

                def one_round(j, u, first, second):
                    for g in range(NG):
                        if g >= 2 or not first:
                            pe.wait_ge(exp_done, j * NG + g - 1)
                        for b in range(QK_G // 2):
                            h = g * QK_G + 2 * b
                            bank = sc_ps[g % 2][:, 2 * b:2 * b + 2]
                            nc.tensor.matmul(bank, s.ident16[:], s.mask[:], start=True, stop=False)
                            for x in range(2):
                                last = nc.tensor.matmul(
                                    bank[:, x], s.k_stack[:, h + x, bass.ds(j * P, P)],
                                    s.q_stack[:, h // 2, bass.ds(j * P, 2 * P)], start=False, stop=(x == 1))
                        last.then_inc(scored, 1)
                        if g and not first:
                            if g == 1 and not second:
                                pe.wait_ge(att_ready, j - 1)
                            values(j - 1, 1 - u, g - 1)
                    if not first:
                        values(j - 1, 1 - u, NG - 1)

                pe.wait_ge(cleared, 2)
                pe.sem_inc(att_ready, 1)
                all_rounds(pe, one_round)
                pe.wait_ge(att_ready, NT - 1)
                for g in range(NG):
                    values(NT - 1, 1, g)

            @block.scalar
            def _(act):
                def exp(j, g, first):
                    act.wait_ge(scored, j * NG + g + 1)
                    if not first:
                        act.wait_ge(low_dve if g % 2 else low_pool, j * 2 + g // 2 - 1)
                    nc.scalar.activation(prob[g][:], sc_ps[g % 2][:], ACT.Exp).then_inc(exp_done, 1)

                def round_off(j, u, g, first):
                    act.wait_ge(exp_done, j * NG + g + 1)
                    if not first:
                        act.wait_ge(out_done, j * NG + g - 3)
                    nc.scalar.copy(hi[u][:, head_slice(g)], prob[g][:]).then_inc(hi_act, 1)

                def one_round(j, u, first, second):
                    exp(j, 0, first)
                    exp(j, 1, first)
                    round_off(j, u, 0, first)
                    exp(j, 2, first)
                    exp(j, 3, first)

                act.preload_act_table(ACT.Exp)
                all_rounds(act, one_round)

            @block.gpsimd
            def _(pool):
                def one_round(j, u, first, second):
                    for g in (0, 2):
                        if g == 0:
                            pool.wait_ge(hi_act, j + 1)
                        else:
                            pool.wait_ge(hi_dve, j * 3 + 2)
                        nc.gpsimd.tensor_tensor(low[u][:, head_slice(g)], prob[g][:], hi[u][:, head_slice(g)],
                                                ALU.subtract).then_inc(low_pool, 1)

                all_rounds(pool, one_round)

            @block.vector
            def _(dve):
                def round_off(j, u, g, first):
                    dve.wait_ge(exp_done, j * NG + g + 1)
                    if not first:
                        dve.wait_ge(out_done, j * NG + g - 3)
                    nc.vector.tensor_copy(hi[u][:, head_slice(g)], prob[g][:]).then_inc(hi_dve, 1)

                def remainder(j, u, g):
                    dve.wait_ge(hi_dve, j * 3 + g)
                    nc.vector.tensor_tensor(low[u][:, head_slice(g)], prob[g][:], hi[u][:, head_slice(g)],
                                            ALU.subtract).then_inc(low_dve, 1)

                def normalize(j, u):
                    dve.wait_ge(out_done, j * NG + NG)
                    sums = o_ps[u][:, :, 0:PARTS * HD].rearrange("p h (r d) -> p h d r", r=PARTS)
                    nc.vector.tensor_reduce(total[:], sums, AX.X, ALU.add).then_inc(total_ready, 1)
                    nc.vector.reciprocal(inv[:], o_ps[u][:, :, PARTS * HD]).then_inc(inv_ready, 1)
                    dve.wait_ge(total_ready, j + 1)
                    dve.wait_ge(inv_ready, j + 1)
                    nc.vector.tensor_tensor(
                        s.att[:, bass.ds(j, 1)].rearrange("p t (h d) -> p (t h) d", h=NH), total[:],
                        bc(inv[:], 2, HD), ALU.mult).then_inc(att_ready, 1)

                def one_round(j, u, first, second):
                    round_off(j, u, 1, first)
                    remainder(j, u, 1)
                    round_off(j, u, 2, first)
                    if not first and not second:
                        normalize(j - 2, u)
                    nc.vector.tensor_copy(v_pair[u][:], s.v_parts[:, bass.ds(j, 2)]).then_inc(v_ready, 1)
                    round_off(j, u, 3, first)
                    remainder(j, u, 3)

                nc.vector.memset(hi[1][:].bitcast(F32), 0.0).then_inc(cleared, 1)
                nc.vector.memset(low[1][:].bitcast(F32), 0.0).then_inc(cleared, 1)
                all_rounds(dve, one_round)
                normalize(NT - 2, 0)
                dve.wait_ge(att_ready, NT)
                normalize(NT - 1, 1)


def finish_attention(nc, k, a, s):
    with ExitStack() as ctx:
        sb = lambda name, shape, dt=F32: ctx.enter_context(nc.sbuf_tensor(f"f_{name}", shape, dt))
        ps = lambda name, shape: ctx.enter_context(nc.psum_tensor(f"f_{name}", shape, F32))
        sem = lambda name: k.sem(f"f_{name}")
        W4 = 4 * P
        NCH = NT // 4
        attT = [sb(f"attT{u}", [P, W4]) for u in range(2)]
        st = sb("st", [P, NT, 6])
        mv = sb("mv", [P, NT, 2])
        var_eps = sb("var_eps", [P, NT])
        rstd = sb("rstd", [P, NT])
        n2 = [sb(f"n2{u}", [P, 4, C]) for u in range(2)]
        n2T = [sb(f"n2T{u}", [P, W4]) for u in range(2)]
        gate = sb("gate", [P, 3, W4])
        hid = [sb(f"hid{u}", [P, 3, W4]) for u in range(2)]
        T_ps = [ps(f"T_ps{u}", [P, W4]) for u in range(2)]
        w_ps = [ps(f"w_ps{u}", [P, 4, C]) for u in range(2)]
        u1_ps = [ps(f"u1_ps{x}", [P, W4]) for x in range(2)]
        u3_ps = [ps(f"u3_ps{x}", [P, W4]) for x in range(2)]
        aT_done, aT_ready, wo_done, h_ready = sem("aT_done"), sem("aT_ready"), sem("wo_done"), sem("h_ready")
        var_steps = sem("var_steps")
        rstd_ready, n2_ready = sem("rstd_ready"), sem("n2_ready")
        nT_done, nT_ready, u_done, silu_done, hid_ready = (sem("nT_done"), sem("nT_ready"), sem("u_done"),
                                                         sem("silu_done"), sem("hid_ready"))
        y_done, h_added, x_ready = sem("y_done"), sem("h_added"), sem("x_ready")
        stats = ChunkStats(nc, k, k.sem, "f_next")

        def chunk(g):
            return slice(4 * g, 4 * g + 4)

        with nc.Block() as block:
            @block.tensor
            def _(pe):
                def turn_attention(g):
                    if g >= 2:
                        pe.wait_ge(aT_ready, g - 1)
                    for t in range(4):
                        last = nc.tensor.transpose(T_ps[g % 2][:, t * P:(t + 1) * P], s.att[:, 4 * g + t],
                                                   k.ident[:])
                    last.then_inc(aT_done, 1)

                def by_wo(g):
                    pe.wait_ge(aT_ready, g + 1)
                    if g >= 2:
                        pe.wait_ge(h_ready, g - 1)
                    for t in range(4):
                        last = nc.tensor.matmul(w_ps[g % 2][:, t], attT[g % 2][:, t * P:(t + 1) * P], s.wo[:],
                                                start=True, stop=True)
                    last.then_inc(wo_done, 1)

                def turn_n2(g):
                    pe.wait_ge(n2_ready, g + 1)
                    if g < 2:
                        pe.wait_ge(aT_ready, NCH - 1 + g)
                    else:
                        pe.wait_ge(nT_ready, g - 1)
                    for t in range(4):
                        last = nc.tensor.transpose(T_ps[g % 2][:, t * P:(t + 1) * P], n2[g % 2][:, t], k.ident[:])
                    last.then_inc(nT_done, 1)

                def by_w1_w3(g):
                    pe.wait_ge(nT_ready, g + 1)
                    for c, (at, size) in enumerate(HIDC):
                        v = 3 * g + c
                        if v >= 2:
                            pe.wait_ge(hid_ready, v - 1)
                        nc.tensor.matmul(u1_ps[v % 2][0:size], s.w1[:, at:at + size], n2T[g % 2][:],
                                         start=True, stop=True)
                        nc.tensor.matmul(u3_ps[v % 2][0:size], s.w3[:, at:at + size], n2T[g % 2][:],
                                         start=True, stop=True).then_inc(u_done, 1)

                def by_w2(g):
                    pe.wait_ge(hid_ready, 3 * g + 3)
                    if g < 2:
                        pe.wait_ge(h_ready, NCH)
                    else:
                        pe.wait_ge(x_ready, g - 1)
                    for t in range(4):
                        for c, (at, size) in enumerate(HIDC):
                            last = nc.tensor.matmul(w_ps[g % 2][:, t], hid[g % 2][0:size, c, t * P:(t + 1) * P],
                                                    s.w2[0:size, c], start=(c == 0), stop=(c == 2))
                    last.then_inc(y_done, 1)

                pe.wait_ge(s.tail_loaded, 16 * 6)
                turn_attention(0)
                for g in range(NCH):
                    if g + 1 < NCH:
                        turn_attention(g + 1)
                    by_wo(g)
                turn_n2(0)
                for g in range(NCH):
                    if g + 1 < NCH:
                        turn_n2(g + 1)
                    by_w1_w3(g)
                    if g:
                        by_w2(g - 1)
                by_w2(NCH - 1)

            @block.scalar
            def _(act):
                def affine(g):
                    act.wait_ge(nT_done, g + 1)
                    if g >= 2:
                        act.wait_ge(u_done, 3 * (g - 1))
                    nc.scalar.activation(n2T[g % 2][:], T_ps[g % 2][:], ACT.Identity, bias=k.ln_vec[:, 3:4],
                                         scale=k.ln_vec[:, 2:3]).then_inc(nT_ready, 1)

                act.preload_act_table(ACT.Silu)
                for g in range(NCH):
                    act.wait_ge(aT_done, g + 1)
                    if g >= 2:
                        act.wait_ge(wo_done, g - 1)
                    nc.scalar.copy(attT[g % 2][:], T_ps[g % 2][:]).then_inc(aT_ready, 1)
                affine(0)
                for g in range(NCH):
                    if g + 1 < NCH:
                        affine(g + 1)
                    for c, (at, size) in enumerate(HIDC):
                        act.wait_ge(u_done, 3 * g + c + 1)
                        if g:
                            act.wait_ge(hid_ready, 3 * g + c - 2)
                        nc.scalar.activation(gate[0:size, c], u1_ps[(3 * g + c) % 2][0:size],
                                             ACT.Silu).then_inc(silu_done, 1)

            @block.gpsimd
            def _(pool):
                for g in range(NCH):
                    pool.wait_ge(var_steps, 3 * g + 3)
                    nc.gpsimd.tensor_tensor(rstd[:, chunk(g)], var_eps[:, chunk(g)], k.minus_half[:, chunk(g)],
                                            ALU.pow).then_inc(rstd_ready, 1)
                for g in range(NCH):
                    stats.on_gpsimd(pool, g)

            @block.vector
            def _(dve):
                def normalize(g):
                    dve.wait_ge(rstd_ready, g + 1)
                    if g >= 2:
                        dve.wait_ge(nT_done, g - 1)
                    for t in range(4):
                        at = 4 * g + t
                        last = nc.vector.tensor_scalar(n2[g % 2][:, t], s.res[:, at], mv[:, at, 0:1],
                                                       rstd[:, at:at + 1], ALU.subtract, ALU.mult)
                    last.then_inc(n2_ready, 1)

                for g in range(NCH):
                    dve.wait_ge(wo_done, g + 1)
                    nc.vector.tensor_tensor(s.res[:, chunk(g)], s.res[:, chunk(g)], w_ps[g % 2][:],
                                            ALU.add).then_inc(h_ready, 1)
                    dve.wait_ge(h_ready, g + 1)
                    for t in range(4 * g, 4 * g + 4):
                        last = nc.vector.bn_stats(st[:, t], s.res[:, t])
                    last.then_inc(var_steps, 1)
                    dve.wait_ge(var_steps, 3 * g + 1)
                    for t in range(4 * g, 4 * g + 4):
                        last = nc.vector.bn_aggr(mv[:, t], st[:, t])
                    last.then_inc(var_steps, 1)
                    dve.wait_ge(var_steps, 3 * g + 2)
                    nc.vector.tensor_scalar(var_eps[:, chunk(g)], mv[:, chunk(g), 1], EPS, None,
                                            ALU.add).then_inc(var_steps, 1)
                    nc.vector.tensor_tensor(k.xs[:, chunk(g)], k.xs[:, chunk(g)], s.res[:, chunk(g)],
                                            ALU.add).then_inc(h_added, 1)
                    if g == 1:
                        normalize(0)
                normalize(1)
                dve.wait_ge(h_added, NCH)

                def add_ffn(g):
                    dve.wait_ge(y_done, g + 1)
                    nc.vector.tensor_tensor(k.xs[:, chunk(g)], k.xs[:, chunk(g)], w_ps[g % 2][:],
                                            ALU.add).then_inc(x_ready, 1)
                    dve.wait_ge(x_ready, g + 1)
                    stats.on_vector(dve, g)

                for g in range(NCH):
                    if g + 2 < NCH:
                        normalize(g + 2)
                    for c, (at, size) in enumerate(HIDC):
                        dve.wait_ge(silu_done, 3 * g + c + 1)
                        if g >= 2:
                            dve.wait_ge(y_done, g - 1)
                        nc.vector.tensor_tensor(hid[g % 2][0:size, c], gate[0:size, c],
                                                u3_ps[(3 * g + c) % 2][0:size], ALU.mult).then_inc(hid_ready, 1)
                    if g:
                        add_ffn(g - 1)
                add_ffn(NCH - 1)


def attention(nc, k, a):
    with ExitStack() as ctx:
        sb = lambda name, shape, dt=F32: ctx.enter_context(nc.sbuf_tensor(f"s_{name}", shape, dt))
        s = Names()
        s.res = sb("res", [P, NT, C])
        s.wo = sb("wo", [P, C])
        s.w1 = sb("w1", [P, HID])
        s.w3 = sb("w3", [P, HID])
        s.w2 = sb("w2", [P, 3, C])
        k.ln_vec = sb("ln_vec", [P, 4])
        s.tail_loaded, s.mask_set = k.sem("tail_loaded"), k.sem("mask_set")
        s.ident16_ready = k.sem("ident16_ready")
        with ExitStack() as stacks:
            sb2 = lambda name, shape, dt=F32: stacks.enter_context(nc.sbuf_tensor(f"s_{name}", shape, dt))
            s.att = None
            s.q_stack = sb2("q_stack", [P, PAIRS, T + P], BF16)
            s.k_stack = sb2("k_stack", [P, NH, T], BF16)
            s.v_parts = sb2("v_parts", [P, NT + 1, NH, VW], BF16)
            s.mask = sb2("mask", [P, 2, 2 * P], BF16)
            s.ident16 = sb2("ident16", [P, P], BF16)
            project(nc, k, a, s)
            maxima(nc, k, a, s)
            s.att = sb2("att", [P, NT, C])
            attend(nc, k, a, s)
            finish_attention(nc, k, a, s)

def macaron(nc, a, out):
    with ExitStack() as ctx:
        k = Names()
        k.sb = lambda name, shape, dt=F32: ctx.enter_context(nc.sbuf_tensor(name, shape, dt))
        k.sem = lambda name: ctx.enter_context(nc.semaphore(name))
        k.moe_sems = {}

        def moe_sem(name):
            if name not in k.moe_sems:
                k.moe_sems[name] = k.sem(name)
            return k.moe_sems[name]

        k.moe_sem = moe_sem
        k.x_rows = nc.dram_tensor("x_rows", [2 * T, C], F32, kind="Internal").ap()
        k.y_rows = nc.dram_tensor("y_rows", [ROWS_OUT, C], F32, kind="Internal").ap()
        k.xs = k.sb("xs", [P, NT, C])
        k.st = k.sb("st", [P, NT, 6])
        k.mv = k.sb("mv", [P, NT, 2])
        k.var_eps = k.sb("var_eps", [P, NT])
        k.rstd = k.sb("rstd", [P, NT])
        constants(nc, k)
        moe_tensors(nc, k)
        moe(nc, k, a, 0)
        attention(nc, k, a)
        moe(nc, k, a, 1, out)


_INS = ["L0_attn_x", "L0_attn_wq", "L0_attn_wk", "L0_attn_wv", "L0_attn_wo", "L0_attn_w1", "L0_attn_w2",
        "L0_attn_w3", "L0_attn_ln1_g", "L0_attn_ln1_b", "L0_attn_ln2_g", "L0_attn_ln2_b", "L0_ffn_gate_W",
        "L0_ffn_mlp_W1", "L0_ffn_mlp_b1", "L0_ffn_mlp_W2", "L0_ffn_mlp_b2", "L0_ffn_kan_ln_g0",
        "L0_ffn_kan_ln_b0", "L0_ffn_kan_sl_W0", "L0_ffn_kan_sl_b0", "L0_ffn_kan_ln_g1", "L0_ffn_kan_ln_b1",
        "L0_ffn_kan_sl_W1", "L0_ffn_kan_sl_b1"]


def kernel(**inputs):
    import concourse.bacc as bacc
    from concourse.bass_utils import run_bass_kernel_spmd

    nc = bacc.Bacc("TRN2", target_bir_lowering=False, num_devices=1)
    arrays, a = {}, Names()
    for name in _INS:
        data = np.ascontiguousarray(inputs[name])
        arrays[f"in_{name}_dram"] = data
        handle = nc.dram_tensor(f"in_{name}_dram", data.shape, mybir.dt.from_np(data.dtype), kind="ExternalInput")
        a.__dict__[name.removeprefix("L0_attn_").removeprefix("L0_ffn_")] = handle.ap()
    by_channel = [np.asarray(inputs[f"L0_ffn_kan_ln_{v}"]).reshape(E2, -1, P).transpose(2, 1, 0)
                  for v in ("g0", "b0", "g1", "b1")]
    arrays["in_kan_ln_dram"] = np.ascontiguousarray(np.concatenate(by_channel, axis=1))
    a.kan_ln = nc.dram_tensor("in_kan_ln_dram", arrays["in_kan_ln_dram"].shape, F32, kind="ExternalInput").ap()
    arrays["in_attn_ln_dram"] = np.ascontiguousarray(np.stack(
        [np.asarray(inputs[f"L0_attn_{v}"]) for v in ("ln1_g", "ln1_b", "ln2_g", "ln2_b")], axis=1))
    a.attn_ln = nc.dram_tensor("in_attn_ln_dram", (C, 4), F32, kind="ExternalInput").ap()
    freqs = 1.0 / np.float32(10000.0) ** (np.arange(0, HD, 2, dtype=np.float32) / np.float32(HD))
    angle = np.outer(np.arange(T, dtype=np.float32), freqs.astype(np.float32)).astype(np.float64).T
    cos, sin = np.cos(angle), np.sin(angle)
    for name, table in (("cos", np.stack([cos, cos], 1)), ("sin", np.stack([-sin, sin], 1))):
        by_channel = table.reshape(HD, T).astype(np.float32)
        arrays[f"in_{name}_dram"] = np.ascontiguousarray(np.tile(np.repeat(by_channel, PAIRS, axis=0), (2, 1)))
        a.__dict__[name] = nc.dram_tensor(f"in_{name}_dram", (C, T), F32, kind="ExternalInput").ap()
    out = nc.dram_tensor("out_0_dram", (1, T, C), F32, kind="ExternalOutput").ap()
    macaron(nc, a, out)
    r = run_bass_kernel_spmd(nc, [arrays], core_ids=[0])
    return r.results[0]["out_0_dram"]
```
